# Optimizing a Trainium2 kernel written in Bass

```python
import numpy as np
import jax
import jax.numpy as jnp

def _softmax(x, axis=-1):
    return jax.nn.softmax(x, axis=axis)

def _gelu(x):
    return jax.nn.gelu(x, approximate=True)

def _silu(x):
    return jax.nn.silu(x)

def _sigmoid(x):
    return jax.nn.sigmoid(x)

def _layernorm(x, axis=-1, eps=1e-05):
    m = jnp.mean(x, axis=axis, keepdims=True)
    v = jnp.var(x, axis=axis, keepdims=True)
    return (x - m) / jnp.sqrt(v + eps)

def _scatter_add(tgt, idx, src, axis=0):
    return tgt.at[idx].add(src)

def _segment_sum(src, seg, n):
    return jax.ops.segment_sum(src, seg, n)
kernel_name = 'mk_gnn_preln_d4_gnn_r16_56caaf'

def setup_inputs(seed: int=0):
    np.random.seed(seed)
    _w = jnp.asarray

    def _rec_inputs():
        import jax
        import jax.numpy as jnp
        _gk = jax.random.key(seed)
        x = -0.000202 + 1 * jax.random.normal(jax.random.fold_in(_gk, 1), (3125, 128), jnp.float32)
        _s = jax.random.randint(jax.random.fold_in(_gk, 2), (50000,), 0, 3125, jnp.int32)
        _d = jax.random.randint(jax.random.fold_in(_gk, 3), (50000,), 0, 3125, jnp.int32)
        _loop = jnp.arange(3125, dtype=jnp.int32)
        src = jnp.concatenate([_s, _d, _loop])
        dst = jnp.concatenate([_d, _s, _loop])
        _o = jnp.argsort(dst, stable=True)
        src = src[_o]
        dst = dst[_o]
        edge_attr_32 = 0.000298249 + 1.00014 * jax.random.normal(jax.random.fold_in(_gk, 12), (103125, 32), jnp.float32)
        return (x, src, dst, edge_attr_32)
    x, src, dst, edge_attr_32 = _rec_inputs()

    def _L0_gnn_setup():
        import jax, jax.numpy as jnp
        import numpy as np
        N_NODES = 3125
        N_EDGES = 50000
        DIM = 128
        BN_EPS = 1e-05
        key = jax.random.key(seed)
        ks = jax.random.split(key, 12)
        d = DIM
        s = 1.0 / np.sqrt(d)
        x = jax.random.normal(ks[0], (N_NODES, d), dtype=jnp.float32)
        edge_index = jax.random.randint(ks[1], (2, N_EDGES), 0, N_NODES, dtype=jnp.int64)
        W_msg = jax.random.uniform(ks[2], (d, d), jnp.float32, -s, s)
        b_msg = jax.random.uniform(ks[3], (d,), jnp.float32, -s, s)
        sa = 1.0 / np.sqrt(2 * d)
        W_att = jax.random.uniform(ks[4], (2 * d, 1), jnp.float32, -sa, sa)
        b_att = jax.random.uniform(ks[5], (1,), jnp.float32, -sa, sa)
        W_ih = jax.random.uniform(ks[6], (3 * d, d), jnp.float32, -s, s)
        b_ih = jax.random.uniform(ks[7], (3 * d,), jnp.float32, -s, s)
        W_hh = jax.random.uniform(ks[8], (3 * d, d), jnp.float32, -s, s)
        b_hh = jax.random.uniform(ks[9], (3 * d,), jnp.float32, -s, s)
        gamma = jnp.ones((d,), jnp.float32)
        beta = jnp.zeros((d,), jnp.float32)
        return {'x': x, 'edge_index': edge_index, 'W_msg': W_msg, 'b_msg': b_msg, 'W_att': W_att, 'b_att': b_att, 'W_ih': W_ih, 'b_ih': b_ih, 'W_hh': W_hh, 'b_hh': b_hh, 'gamma': gamma, 'beta': beta}
    _L0_gnn_all = _L0_gnn_setup()
    _L0_gnn_in = {k: v for k, v in _L0_gnn_all.items() if k in ('W_msg', 'b_msg', 'W_att', 'b_att', 'W_ih', 'b_ih', 'W_hh', 'b_hh', 'gamma', 'beta')}
    del _L0_gnn_all

    def _L1_gnn_setup():
        import jax, jax.numpy as jnp
        import numpy as np
        NUM_LAYERS = 3

        def _scatter_mean_layer(x, src, dst, num_nodes):
            msgs = x[src]
            summed = jax.ops.segment_sum(msgs, dst, num_segments=num_nodes)
            counts = jax.ops.segment_sum(jnp.ones((src.shape[0],), dtype=x.dtype), dst, num_segments=num_nodes)
            return summed / jnp.maximum(counts, 1.0)[:, None]
        key = jax.random.key(seed)
        k1, k2, k3 = jax.random.split(key, 3)
        N, E, D = (6250, 200000, 128)
        x = jax.random.normal(k1, (N, D), dtype=jnp.float32)
        src = jax.random.randint(k2, (E,), 0, N)
        dst = jax.random.randint(k3, (E,), 0, N)
        edge_index = jnp.stack([src, dst], axis=0).astype(jnp.int64)
        return {'x': x, 'edge_index': edge_index}
    _L1_gnn_all = _L1_gnn_setup()
    _L1_gnn_in = {k: v for k, v in _L1_gnn_all.items() if k in ()}
    del _L1_gnn_all

    def _L2_gnn_setup():
        import jax, jax.numpy as jnp
        import numpy as np
        N_NODES = 3125
        N_EDGES = 50000
        D_IN = 128
        D_OUT = 128
        BN_EPS = 1e-05

        def _bn_eval(x, gamma, beta, rm, rv):
            return (x - rm) * jax.lax.rsqrt(rv + BN_EPS) * gamma + beta
        key = jax.random.key(seed)
        ks = jax.random.split(key, 8)
        feat = jax.random.normal(ks[0], (N_NODES, D_IN), dtype=jnp.float32)
        src = jax.random.randint(ks[1], (N_EDGES,), 0, N_NODES, dtype=jnp.int32)
        dst = jax.random.randint(ks[2], (N_EDGES,), 0, N_NODES, dtype=jnp.int32)
        s = float(np.sqrt(6.0 / (D_IN + D_OUT))) * float(np.sqrt(2.0))
        W_self = jax.random.uniform(ks[3], (D_OUT, D_IN), jnp.float32, -s, s)
        b_self = jnp.zeros((D_OUT,), jnp.float32)
        W1 = jax.random.uniform(ks[4], (D_OUT, D_IN), jnp.float32, -s, s)
        W2 = jax.random.uniform(ks[5], (D_OUT, D_OUT), jnp.float32, -s, s)
        ones = jnp.ones((D_OUT,), jnp.float32)
        zeros = jnp.zeros((D_OUT,), jnp.float32)
        return {'feat': feat, 'src': src, 'dst': dst, 'W_self': W_self, 'b_self': b_self, 'W1': W1, 'gamma1': ones, 'beta1': zeros, 'rm1': zeros, 'rv1': ones, 'W2': W2, 'gamma2': ones, 'beta2': zeros, 'rm2': zeros, 'rv2': ones}
    _L2_gnn_all = _L2_gnn_setup()
    _L2_gnn_in = {k: v for k, v in _L2_gnn_all.items() if k in ('W_self', 'b_self', 'W1', 'gamma1', 'beta1', 'rm1', 'rv1', 'W2', 'gamma2', 'beta2', 'rm2', 'rv2')}
    del _L2_gnn_all

    def _L3_gnn_setup():
        import jax, jax.numpy as jnp
        import numpy as np
        N = 3125
        E = 625000
        D = 128
        H = 8
        C = D // H
        DE = 32
        NEG_SLOPE = 0.2
        LN_EPS = 1e-05

        def _ln(x, g, b):
            mu = x.mean(-1, keepdims=True)
            var = ((x - mu) ** 2).mean(-1, keepdims=True)
            return (x - mu) * jax.lax.rsqrt(var + LN_EPS) * g + b

        def _gatv2(x, edge_index, edge_attr, W_l, W_r, W_e, att, bias):
            n = x.shape[0]
            loop = jnp.arange(n, dtype=edge_index.dtype)
            src = jnp.concatenate([edge_index[0], loop])
            dst = jnp.concatenate([edge_index[1], loop])
            ea = jnp.concatenate([edge_attr, jnp.broadcast_to(edge_attr.mean(0), (n, edge_attr.shape[1]))], 0)
            x_l = (x @ W_l).reshape(n, H, C)
            x_r = (x @ W_r).reshape(n, H, C)
            e = (ea @ W_e).reshape(-1, H, C)
            m = jax.nn.leaky_relu(x_l[src] + x_r[dst] + e, NEG_SLOPE)
            alpha = jnp.einsum('ehc,hc->eh', m, att)
            amax = jax.ops.segment_max(alpha, dst, num_segments=n)
            expa = jnp.exp(alpha - amax[dst])
            denom = jax.ops.segment_sum(expa, dst, num_segments=n)
            a = expa / (denom[dst] + 1e-16)
            out = jax.ops.segment_sum(x_l[src] * a[:, :, None], dst, num_segments=n)
            return out.reshape(n, D) + bias
        key = jax.random.key(seed)
        k = jax.random.split(key, 9)

        def gw(i, shape, fan_in):
            return jax.random.normal(k[i], shape, jnp.float32) / np.sqrt(fan_in).astype(np.float32)
        return {'x': jax.random.normal(k[0], (N, D), jnp.float32), 'edge_index': jax.random.randint(k[1], (2, E), 0, N, jnp.int32), 'edge_attr': jax.random.normal(k[2], (E, DE), jnp.float32), 'W_l': gw(3, (D, D), D), 'W_r': gw(4, (D, D), D), 'W_e': gw(5, (DE, D), DE), 'att': gw(6, (H, C), C), 'bias': jnp.zeros((D,), jnp.float32), 'ln1_g': jnp.ones((D,), jnp.float32), 'ln1_b': jnp.zeros((D,), jnp.float32), 'ln2_g': jnp.ones((D,), jnp.float32), 'ln2_b': jnp.zeros((D,), jnp.float32), 'W1': gw(7, (D, 2 * D), D), 'b1': jnp.zeros((2 * D,), jnp.float32), 'W2': gw(8, (2 * D, D), 2 * D), 'b2': jnp.zeros((D,), jnp.float32)}
    _L3_gnn_all = _L3_gnn_setup()
    _L3_gnn_in = {k: v for k, v in _L3_gnn_all.items() if k in ('W_l', 'W_r', 'W_e', 'att', 'bias', 'ln1_g', 'ln1_b', 'ln2_g', 'ln2_b', 'W1', 'b1', 'W2', 'b2')}
    del _L3_gnn_all
    return {'x': x, 'src': src, 'dst': dst, 'edge_attr_32': edge_attr_32, 'L0_gnn_W_msg': _L0_gnn_in['W_msg'], 'L0_gnn_b_msg': _L0_gnn_in['b_msg'], 'L0_gnn_W_att': _L0_gnn_in['W_att'], 'L0_gnn_b_att': _L0_gnn_in['b_att'], 'L0_gnn_W_ih': _L0_gnn_in['W_ih'], 'L0_gnn_b_ih': _L0_gnn_in['b_ih'], 'L0_gnn_W_hh': _L0_gnn_in['W_hh'], 'L0_gnn_b_hh': _L0_gnn_in['b_hh'], 'L0_gnn_gamma': _L0_gnn_in['gamma'], 'L0_gnn_beta': _L0_gnn_in['beta'], 'L2_gnn_W_self': _L2_gnn_in['W_self'], 'L2_gnn_b_self': _L2_gnn_in['b_self'], 'L2_gnn_W1': _L2_gnn_in['W1'], 'L2_gnn_gamma1': _L2_gnn_in['gamma1'], 'L2_gnn_beta1': _L2_gnn_in['beta1'], 'L2_gnn_rm1': _L2_gnn_in['rm1'], 'L2_gnn_rv1': _L2_gnn_in['rv1'], 'L2_gnn_W2': _L2_gnn_in['W2'], 'L2_gnn_gamma2': _L2_gnn_in['gamma2'], 'L2_gnn_beta2': _L2_gnn_in['beta2'], 'L2_gnn_rm2': _L2_gnn_in['rm2'], 'L2_gnn_rv2': _L2_gnn_in['rv2'], 'L3_gnn_W_l': _L3_gnn_in['W_l'], 'L3_gnn_W_r': _L3_gnn_in['W_r'], 'L3_gnn_W_e': _L3_gnn_in['W_e'], 'L3_gnn_att': _L3_gnn_in['att'], 'L3_gnn_bias': _L3_gnn_in['bias'], 'L3_gnn_ln1_g': _L3_gnn_in['ln1_g'], 'L3_gnn_ln1_b': _L3_gnn_in['ln1_b'], 'L3_gnn_ln2_g': _L3_gnn_in['ln2_g'], 'L3_gnn_ln2_b': _L3_gnn_in['ln2_b'], 'L3_gnn_W1': _L3_gnn_in['W1'], 'L3_gnn_b1': _L3_gnn_in['b1'], 'L3_gnn_W2': _L3_gnn_in['W2'], 'L3_gnn_b2': _L3_gnn_in['b2']}

def reference(x, src, dst, edge_attr_32, L0_gnn_W_msg, L0_gnn_b_msg, L0_gnn_W_att, L0_gnn_b_att, L0_gnn_W_ih, L0_gnn_b_ih, L0_gnn_W_hh, L0_gnn_b_hh, L0_gnn_gamma, L0_gnn_beta, L2_gnn_W_self, L2_gnn_b_self, L2_gnn_W1, L2_gnn_gamma1, L2_gnn_beta1, L2_gnn_rm1, L2_gnn_rv1, L2_gnn_W2, L2_gnn_gamma2, L2_gnn_beta2, L2_gnn_rm2, L2_gnn_rv2, L3_gnn_W_l, L3_gnn_W_r, L3_gnn_W_e, L3_gnn_att, L3_gnn_bias, L3_gnn_ln1_g, L3_gnn_ln1_b, L3_gnn_ln2_g, L3_gnn_ln2_b, L3_gnn_W1, L3_gnn_b1, L3_gnn_W2, L3_gnn_b2):
    import jax
    import jax.numpy as jnp

    def _L0_gnn_ref(x, edge_index, W_msg, b_msg, W_att, b_att, W_ih, b_ih, W_hh, b_hh, gamma, beta):
        import jax, jax.numpy as jnp
        import numpy as np
        N_NODES = 3125
        N_EDGES = 50000
        DIM = 128
        BN_EPS = 1e-05
        num_nodes, d = x.shape
        src = edge_index[0]
        dst = edge_index[1]
        xs = x[src]
        xd = x[dst]
        att = jax.nn.sigmoid(xs @ W_att[:d] + xd @ W_att[d:] + b_att)
        messages = (xs @ W_msg + b_msg) * att
        aggregated = jax.ops.segment_sum(messages, dst, num_segments=num_nodes)
        gi = aggregated @ W_ih.T + b_ih
        gh = x @ W_hh.T + b_hh
        i_r, i_z, i_n = jnp.split(gi, 3, axis=1)
        h_r, h_z, h_n = jnp.split(gh, 3, axis=1)
        r = jax.nn.sigmoid(i_r + h_r)
        z = jax.nn.sigmoid(i_z + h_z)
        n = jnp.tanh(i_n + r * h_n)
        h_new = (1.0 - z) * n + z * x
        mean = jnp.mean(h_new, axis=0)
        var = jnp.var(h_new, axis=0)
        return gamma * (h_new - mean) * jax.lax.rsqrt(var + BN_EPS) + beta

    def _L1_gnn_ref(x, edge_index):
        import jax, jax.numpy as jnp
        import numpy as np
        NUM_LAYERS = 3

        def _scatter_mean_layer(x, src, dst, num_nodes):
            msgs = x[src]
            summed = jax.ops.segment_sum(msgs, dst, num_segments=num_nodes)
            counts = jax.ops.segment_sum(jnp.ones((src.shape[0],), dtype=x.dtype), dst, num_segments=num_nodes)
            return summed / jnp.maximum(counts, 1.0)[:, None]
        src = edge_index[0]
        dst = edge_index[1]
        num_nodes = x.shape[0]
        for _ in range(NUM_LAYERS):
            x = _scatter_mean_layer(x, src, dst, num_nodes)
        return x

    def _L2_gnn_ref(feat, src, dst, W_self, b_self, W1, gamma1, beta1, rm1, rv1, W2, gamma2, beta2, rm2, rv2):
        import jax, jax.numpy as jnp
        import numpy as np
        N_NODES = 3125
        N_EDGES = 50000
        D_IN = 128
        D_OUT = 128
        BN_EPS = 1e-05

        def _bn_eval(x, gamma, beta, rm, rv):
            return (x - rm) * jax.lax.rsqrt(rv + BN_EPS) * gamma + beta
        n = feat.shape[0]
        msg_sum = jax.ops.segment_sum(feat[src], dst, num_segments=n)
        deg = jax.ops.segment_sum(jnp.ones_like(dst, dtype=feat.dtype), dst, num_segments=n)
        h_neigh = msg_sum / jnp.maximum(deg, 1.0)[:, None]
        x = _bn_eval(h_neigh @ W1.T, gamma1, beta1, rm1, rv1)
        x = jax.nn.relu(x)
        x = _bn_eval(x @ W2.T, gamma2, beta2, rm2, rv2)
        h_self = feat @ W_self.T + b_self
        return h_self + x

    def _L3_gnn_ref(x, edge_index, edge_attr, W_l, W_r, W_e, att, bias, ln1_g, ln1_b, ln2_g, ln2_b, W1, b1, W2, b2):
        import jax, jax.numpy as jnp
        import numpy as np
        N = 3125
        E = 625000
        D = 128
        H = 8
        C = D // H
        DE = 32
        NEG_SLOPE = 0.2
        LN_EPS = 1e-05

        def _ln(x, g, b):
            mu = x.mean(-1, keepdims=True)
            var = ((x - mu) ** 2).mean(-1, keepdims=True)
            return (x - mu) * jax.lax.rsqrt(var + LN_EPS) * g + b

        def _gatv2(x, edge_index, edge_attr, W_l, W_r, W_e, att, bias):
            n = x.shape[0]
            loop = jnp.arange(n, dtype=edge_index.dtype)
            src = jnp.concatenate([edge_index[0], loop])
            dst = jnp.concatenate([edge_index[1], loop])
            ea = jnp.concatenate([edge_attr, jnp.broadcast_to(edge_attr.mean(0), (n, edge_attr.shape[1]))], 0)
            x_l = (x @ W_l).reshape(n, H, C)
            x_r = (x @ W_r).reshape(n, H, C)
            e = (ea @ W_e).reshape(-1, H, C)
            m = jax.nn.leaky_relu(x_l[src] + x_r[dst] + e, NEG_SLOPE)
            alpha = jnp.einsum('ehc,hc->eh', m, att)
            amax = jax.ops.segment_max(alpha, dst, num_segments=n)
            expa = jnp.exp(alpha - amax[dst])
            denom = jax.ops.segment_sum(expa, dst, num_segments=n)
            a = expa / (denom[dst] + 1e-16)
            out = jax.ops.segment_sum(x_l[src] * a[:, :, None], dst, num_segments=n)
            return out.reshape(n, D) + bias
        h = x + _gatv2(_ln(x, ln1_g, ln1_b), edge_index, edge_attr, W_l, W_r, W_e, att, bias)
        ff = jax.nn.gelu(_ln(h, ln2_g, ln2_b) @ W1 + b1, approximate=False) @ W2 + b2
        return h + ff
    edge_index = jnp.stack([src, dst])
    h = jnp.maximum(_layernorm(x, axis=-1), 0.0)
    x = x + _L0_gnn_ref(h, edge_index, L0_gnn_W_msg, L0_gnn_b_msg, L0_gnn_W_att, L0_gnn_b_att, L0_gnn_W_ih, L0_gnn_b_ih, L0_gnn_W_hh, L0_gnn_b_hh, L0_gnn_gamma, L0_gnn_beta)
    h = jnp.maximum(_layernorm(x, axis=-1), 0.0)
    x = x + _L1_gnn_ref(h, edge_index)
    h = jnp.maximum(_layernorm(x, axis=-1), 0.0)
    x = x + _L2_gnn_ref(h, src, dst, L2_gnn_W_self, L2_gnn_b_self, L2_gnn_W1, L2_gnn_gamma1, L2_gnn_beta1, L2_gnn_rm1, L2_gnn_rv1, L2_gnn_W2, L2_gnn_gamma2, L2_gnn_beta2, L2_gnn_rm2, L2_gnn_rv2)
    h = jnp.maximum(_layernorm(x, axis=-1), 0.0)
    x = x + _L3_gnn_ref(h, edge_index, edge_attr_32, L3_gnn_W_l, L3_gnn_W_r, L3_gnn_W_e, L3_gnn_att, L3_gnn_bias, L3_gnn_ln1_g, L3_gnn_ln1_b, L3_gnn_ln2_g, L3_gnn_ln2_b, L3_gnn_W1, L3_gnn_b1, L3_gnn_W2, L3_gnn_b2)
    return x

_drawn_inputs = setup_inputs


def setup_inputs(seed=0):
    import zlib

    import numpy as np

    out = dict(_drawn_inputs(seed))
    spreads = {'L0_gnn_gamma': (1.0, 0.2),
     'L0_gnn_beta': (0.0, 0.1),
     'L2_gnn_b_self': (0.0, 0.1),
     'L2_gnn_gamma1': (1.0, 0.2),
     'L2_gnn_beta1': (0.0, 0.1),
     'L2_gnn_rm1': (0.0, 0.1),
     'L2_gnn_rv1': (1.0, 0.6),
     'L2_gnn_gamma2': (1.0, 0.2),
     'L2_gnn_beta2': (0.0, 0.1),
     'L2_gnn_rm2': (0.0, 0.1),
     'L2_gnn_rv2': (1.0, 0.2),
     'L3_gnn_bias': (0.0, 0.1),
     'L3_gnn_ln1_g': (1.0, 0.2),
     'L3_gnn_ln1_b': (0.0, 0.1),
     'L3_gnn_ln2_g': (1.0, 0.2),
     'L3_gnn_ln2_b': (0.0, 0.377),
     'L3_gnn_b1': (0.0, 0.363),
     'L3_gnn_b2': (0.0, 0.1)}
    factors = {'L0_gnn_b_ih': 5.138, 'L0_gnn_b_hh': 5.259}
    for name, (base, spread) in spreads.items():
        noise = np.random.default_rng([zlib.crc32(name.encode()), seed]).standard_normal(out[name].shape)
        drawn = base * np.exp(spread * noise) if base else spread * noise
        out[name] = jnp.asarray(drawn.astype(out[name].dtype))
    for name, factor in factors.items():
        out[name] = (out[name] * factor).astype(out[name].dtype)
    return out
```

```python
from contextlib import ExitStack

import concourse.bass as bass
from concourse import mybir

F32 = mybir.dt.float32
F16 = mybir.dt.float16
I32 = mybir.dt.int32
I16 = mybir.dt.int16
ALU = mybir.AluOpType
ACT = mybir.ActivationFunctionType
AX = mybir.AxisListType

P = 128
D = 128
HEADS = 8
CH = D // HEADS
DE = 32
NEG_SLOPE = 0.2
EPS = 1e-5
DENOM_EPS = 1e-16
FAR = 8192.0
NONE = -3.0e38
F16_SCALE = 4096.0


class Shapes:
    def __init__(self, n_nodes, n_edges):
        self.n = n_nodes
        self.nb = -(-n_nodes // P)
        self.last = n_nodes - (self.nb - 1) * P
        self.edges = n_edges
        self.tiles = -(-n_edges // P)
        self.rows4 = -(-(self.tiles + 1) // 4)
        self.w = 8
        self.windows = -(-n_nodes // self.w)
        self.nc = self.windows * self.w
        self.pad_dst = self.nc - 1
        assert self.pad_dst >= n_nodes
        self.csteps = self.tiles + self.windows - 1
        steps = self.tiles + self.nb - 1
        self.esteps = -(-steps // 16) * 16
        self.run = self.esteps // 16

    def rows(self, b):
        return P if b < self.nb - 1 else self.last


class Core:

    ENGINES = ("tensor", "vector", "scalar", "gpsimd", "sync")

    def __init__(self, nc, ctx):
        self.nc = nc
        self.queue = {e: [] for e in self.ENGINES}
        self.sem = {e: ctx.enter_context(nc.semaphore(f"{e}_done")) for e in self.ENGINES}
        self.count = {e: 0 for e in self.ENGINES}
        self.waited = {e: {} for e in self.ENGINES}
        self.ctx = ctx

    def lane(self, name):
        self.sem[name] = self.ctx.enter_context(self.nc.semaphore(name))
        self.count[name] = 0
        return name

    def wait(self, engine, after):
        for token in after:
            if token is None:
                continue
            name, value = token
            if value > self.waited[engine].get(name, 0):
                self.waited[engine][name] = value
                sem = self.sem[name]
                self.queue[engine].append(lambda e, sem=sem, value=value: e.wait_ge(sem, value))

    def on(self, engine, make, after=()):
        self.wait(engine, after)
        sem = self.sem[engine]
        self.queue[engine].append(lambda e: make(e).then_inc(sem, 1))
        self.count[engine] += 1
        return engine, self.count[engine]

    def dma(self, engine, lane, make, after=()):
        self.wait(engine, after)
        sem = self.sem[lane]
        self.queue[engine].append(lambda e: make(e).then_inc(sem, 16))
        self.count[lane] += 16
        return lane, self.count[lane]

    def step(self, engine, do):
        self.queue[engine].append(do)

    def pe(self, make, after=()):
        return self.on("tensor", make, after)

    def dve(self, make, after=()):
        return self.on("vector", make, after)

    def act(self, make, after=()):
        return self.on("scalar", make, after)

    def pool(self, make, after=()):
        return self.on("gpsimd", make, after)

    def barrier(self):
        everything = [(name, value) for name, value in self.count.items() if value]
        for e in self.ENGINES:
            self.wait(e, everything)

    def emit(self):
        with self.nc.Block() as block:
            for name in self.ENGINES:
                def run(e, name=name):
                    for make in self.queue[name]:
                        make(e)
                {"tensor": block.tensor, "vector": block.vector, "scalar": block.scalar,
                 "gpsimd": block.gpsimd, "sync": block.sync}[name](run)


class Kernel:
    def __init__(self, nc, ctx, s, io, out):
        self.nc, self.ctx, self.s, self.io, self.out = nc, ctx, s, io, out
        self.q = Core(nc, ctx)
        self.psum = ctx.enter_context(nc.psum_tensor("psum", [P, 8, 512], F32))
        self.bank = [self.psum[:, i, :] for i in range(8)]
        self.bank_free = [None] * 8
        self.turn = 0
        self.setup = self.q.lane("setup_loads")
        self.names = 0

    def sb(self, scope, name, shape, dt=F32):
        self.names += 1
        return scope.enter_context(self.nc.sbuf_tensor(f"{name}_{self.names}", shape, dt))

    def dram(self, name, shape, dt=F32):
        return self.nc.dram_tensor(name, shape, dt, kind="Internal").ap()

    def load(self, dst, src, after=()):
        self.q.dma("sync", self.setup, lambda e: e.dma_start(dst, src), after)

    def loaded(self):
        return self.setup, self.q.count[self.setup]

    def next_bank(self):
        self.turn = (self.turn + 1) % 8
        return self.turn

    def transpose_to(self, dst, src, after, copy=None):
        q, i = self.q, self.next_bank()
        k, m = src.free_size(), src.shape[0]
        ps = self.bank[i][0:k, 0:m]
        t = q.pe(lambda e: e.transpose(ps, src, self.ident[0:m, 0:m]), after=list(after) + [self.bank_free[i]])
        if copy is None:
            t = q.dve(lambda e: e.tensor_copy(dst, ps), after=[t])
        else:
            t = copy(ps, t)
        self.bank_free[i] = t
        return t

    def row_of(self, dst, column, after):
        q, i = self.q, self.next_bank()
        ps = self.bank[i][:, 0:P]
        t = q.pe(lambda e: e.matmul(ps, column.to_broadcast([P, P]), self.ident[:, :], start=True, stop=True),
                 after=list(after) + [self.bank_free[i]])
        t = q.dve(lambda e: e.tensor_copy(dst, ps), after=[t])
        self.bank_free[i] = t
        return t

    def constants(self):
        ctx, io, q = self.ctx, self.io, self.q
        self.ident = self.sb(ctx, "ident", [P, P])
        self.eps = self.sb(ctx, "eps", [P, 1])
        self.edge_sum = self.sb(ctx, "edge_sum", [P, 1])
        self.load(self.ident[:, :], io["c_ident"])
        q.dve(lambda e: e.memset(self.eps[:, :], EPS))

    def load_iota(self, scope):
        iota = self.sb(scope, "iota", [P, P])
        self.load(iota[:, :], self.io["c_iota"].partition_broadcast(P))
        return iota

    def path(self, scope, name, shift, windows, nsteps):
        s, q, io = self.s, self.q, self.io
        nch = -(-nsteps // P)
        sb = self.sb
        ends = sb(scope, name + "_ends", [P, s.tiles])
        win = sb(scope, name + "_win", [P, s.tiles], I32)
        junk = sb(scope, name + "_junk", [P, s.tiles])
        step = sb(scope, name + "_step", [P, nch])
        before = sb(scope, name + "_before", [P, nch])
        tile = sb(scope, name + "_tile", [P, nch])
        tile_prev = sb(scope, name + "_tile_prev", [P, nch])
        window = sb(scope, name + "_window", [P, nch])
        keep = sb(scope, name + "_keep", [P, nch])
        index = sb(scope, name + "_index", [P, nch], I32)
        self.load(step[:, :], io["c_step"][:, 0:nch])
        t = q.dve(lambda e: e.tensor_scalar(win[:, :], self.dlast[:, :], shift, None,
                                            ALU.logical_shift_right), after=[self.loaded()])
        t = q.dve(lambda e: e.tensor_copy(ends[:, :], win[:, :]), after=[t])
        t = q.dve(lambda e: e.tensor_tensor(ends[:, :], ends[:, :], self.tile_no[:, :], ALU.add), after=[t])
        t = q.dve(lambda e: e.tensor_scalar(before[:, :], step[:, :], -1.0, None, ALU.add), after=[t])
        for c in range(nch):
            for at, to in ((step, tile), (before, tile_prev)):
                t = q.dve(lambda e, c=c, at=at, to=to: e.tensor_scalar(
                    junk[:, :], ends[:, :], at[:, c:c + 1], None, ALU.is_lt, ALU.add,
                    accum_out=to[:, c:c + 1]), after=[t])
        q.dve(lambda e: e.tensor_copy(index[:, :], tile[:, :]), after=[t])
        t = q.dve(lambda e: e.tensor_tensor(window[:, :], step[:, :], tile[:, :], ALU.subtract))
        t = q.dve(lambda e: e.tensor_tensor(tile_prev[:, :], before[:, :], tile_prev[:, :], ALU.subtract),
                  after=[t])
        t = q.dve(lambda e: e.tensor_scalar(window[:, :], window[:, :], float(windows - 1), None, ALU.min),
                  after=[t])
        done = q.dve(lambda e: e.tensor_tensor(keep[:, :], window[:, :], tile_prev[:, :], ALU.is_equal),
                     after=[t])
        src = sb(scope, name + "_src", [P, nch, P], I32)
        dst = sb(scope, name + "_dst", [P, nch, P], I32)
        lane = q.lane(name + "_edge_rows")
        for c in range(nch):
            for to, table in ((src, io["src_rows"]), (dst, io["dst_rows"])):
                got = q.dma("gpsimd", lane, lambda e, c=c, to=to, table=table: e.indirect_dma_start(
                    to[:, c, :], None, table, bass.IndirectOffsetOnAxis(ap=index[:, c:c + 1], axis=0)),
                    after=[done])
        return nch, tile, window, keep, src, dst, got

    def edge_tables(self):
        s, q, io = self.s, self.q, self.io
        n = s.esteps
        self.e_src = self.dram("e_src", (P, n), I32)
        self.e_rel = self.dram("e_rel", (P, n))
        self.e_rel_rows = self.dram("e_rel_rows", (n, P), I16)
        self.e_dst_flat = self.dram("e_dst_flat", (n * P + 2,))
        self.e_regs = self.dram("e_regs", (2, n), I32)
        self.e_lane = q.lane("edge_tables")
        with ExitStack() as scope:
            sb = self.sb
            nch, tile, window, keep, src, dst, got = self.path(scope, "e", 7, s.nb, n)
            rel = sb(scope, "rel", [P, nch, P])
            dstf = sb(scope, "dstf", [P, nch, P])
            rel16 = sb(scope, "rel16", [P, nch, P], I16)
            srcf = sb(scope, "srcf", [P, nch, P])
            first = sb(scope, "first", [P, nch])
            srct = sb(scope, "srct", [P, nch * P], I32)
            relt = sb(scope, "relt", [P, nch * P])
            rowf = sb(scope, "rowf", [P, 2, nch * P], I32)
            guard = sb(scope, "guard", [1, 1])
            cuts = 8
            wide = -(-s.rows4 // cuts)
            part = sb(scope, "edge_part", [P, 2, wide, P])
            sums = sb(scope, "edge_sums", [P, cuts])
            lanes = [q.lane(f"edge_part{i}") for i in range(2)]
            by_row = io["edge_t"].rearrange("(i j) k e -> (j k) i e", j=4)
            done = []
            for c in range(cuts):
                lo, hi = c * wide, min((c + 1) * wide, s.rows4)
                piece = part[:, c % 2, 0:hi - lo, :]
                t = q.dma("sync", lanes[c % 2], lambda e, piece=piece, lo=lo, hi=hi: e.dma_start(
                    piece, by_row[:, lo:hi, :]), after=[done[c - 2]] if c >= 2 else ())
                done.append(q.act(lambda e, piece=piece, c=c: e.activation(
                    piece, piece, ACT.Copy, accum_out=sums[:, c:c + 1]), after=[t]))
            q.dve(lambda e: e.tensor_reduce(self.edge_sum[:, :], sums[:, :], AX.X, ALU.add), after=[done[-1]])
            a = q.dve(lambda e: e.memset(guard[:, :], -1.0))
            b = q.dve(lambda e: e.tensor_scalar(first[:, :], window[:, :], float(P), None, ALU.mult), after=[a])
            b = q.dve(lambda e: e.tensor_copy(dstf[:, :, :], dst[:, :, :]), after=[got, b])
            t = q.dve(lambda e: e.tensor_copy(srcf[:, :, :], src[:, :, :]))
            for c in range(nch):
                t = q.dve(lambda e, c=c: e.tensor_scalar(rel[:, c, :], dstf[:, c, :], first[:, c:c + 1], None,
                                                         ALU.subtract), after=[b])
            t = q.dve(lambda e: e.tensor_copy(rel16[:, :, :], rel[:, :, :]), after=[t])
            for c in range(nch):
                self.transpose_to(srct[:, c * P:(c + 1) * P], srcf[:, c, :], [t])
                self.transpose_to(relt[:, c * P:(c + 1) * P], rel[:, c, :], [t])
                self.row_of(rowf[:, 0, c * P:(c + 1) * P], tile[:, c:c + 1], [t])
                t2 = self.row_of(rowf[:, 1, c * P:(c + 1) * P], window[:, c:c + 1], [t])

            def store(dst_, src_):
                q.dma("sync", self.e_lane, lambda e: e.dma_start(dst_, src_), after=[t2])
            store(self.e_src, srct[:, 0:n])
            store(self.e_rel, relt[:, 0:n])
            store(self.e_regs[0:1, :], rowf[0:1, 0, 0:n])
            store(self.e_regs[1:2, :], rowf[0:1, 1, 0:n])
            flat = self.e_dst_flat
            store(flat[0:1].rearrange("(a b) -> a b", a=1), guard[:, :])
            store(flat[n * P + 1:n * P + 2].rearrange("(a b) -> a b", a=1), guard[:, :])
            for c in range(nch):
                r = min(P, n - c * P)
                store(self.e_rel_rows[c * P:c * P + r, :], rel16[0:r, c, :])
                store(flat[1 + c * P * P:1 + (c * P + r) * P].rearrange("(v e) -> v e", e=P), dstf[0:r, c, :])
            q.barrier()

    def count_tables(self):
        s, q = self.s, self.q
        w = s.w
        with ExitStack() as scope:
            sb = self.sb
            nch, tile, window, keep, src, dst, got = self.path(scope, "c", 3, s.windows, s.csteps)
            n = nch * P
            self.c_key_d = self.dram("c_key", (P, n))
            self.c_low_d = self.dram("c_low", (P, n))
            self.c_keep_d = self.dram("c_keep", (1, n))
            self.c_win_d = self.dram("c_win", (1, n), I32)
            self.c_lane = q.lane("count_tables")
            high = sb(scope, "high", [P, nch, P], I32)
            low = sb(scope, "low", [P, nch, P], I32)
            lowf = sb(scope, "lowf", [P, nch, P])
            key = sb(scope, "key", [P, nch, P])
            first = sb(scope, "first", [P, nch])
            dstf = sb(scope, "dstf", [P, nch, P])
            out = [sb(scope, "out", [P, n]) for _ in range(3)] + [sb(scope, "outw", [P, n], I32)]
            t = q.dve(lambda e: e.tensor_scalar(high[:, :, :], src[:, :, :], 7, None, ALU.logical_shift_right),
                      after=[got])
            q.dve(lambda e: e.tensor_scalar(low[:, :, :], src[:, :, :], P - 1, None, ALU.bitwise_and))
            q.dve(lambda e: e.tensor_copy(dstf[:, :, :], dst[:, :, :]))
            t = q.dve(lambda e: e.tensor_scalar(first[:, :], window[:, :], float(w), None, ALU.mult))
            t = q.dve(lambda e: e.tensor_copy(key[:, :, :], high[:, :, :]), after=[t])
            t = q.dve(lambda e: e.tensor_copy(lowf[:, :, :], low[:, :, :]), after=[t])
            t = q.dve(lambda e: e.scalar_tensor_tensor(key[:, :, :], key[:, :, :], FAR, dstf[:, :, :],
                                                       ALU.mult, ALU.add), after=[t])
            for c in range(nch):
                t = q.dve(lambda e, c=c: e.tensor_scalar(key[:, c, :], key[:, c, :], first[:, c:c + 1], None,
                                                         ALU.subtract), after=[t])
            for c in range(nch):
                cut = slice(c * P, (c + 1) * P)
                self.transpose_to(out[0][:, cut], key[:, c, :], [t])
                self.transpose_to(out[1][:, cut], lowf[:, c, :], [t])
                self.row_of(out[2][:, cut], keep[:, c:c + 1], [t])
                t2 = self.row_of(out[3][:, cut], window[:, c:c + 1], [t])
            for to, what in ((self.c_key_d, out[0][:, :]), (self.c_low_d, out[1][:, :]),
                             (self.c_keep_d, out[2][0:1, :]), (self.c_win_d, out[3][0:1, :])):
                q.dma("sync", self.c_lane, lambda e, to=to, what=what: e.dma_start(to, what), after=[t2])
            q.barrier()

    def count_matrix(self, counts):
        s, q = self.s, self.q
        w = s.w
        self.counts = counts
        ring = 4
        with ExitStack() as scope:
            sb = self.sb
            far = sb(scope, "far", [P, s.nb * w])
            lows = sb(scope, "lows", [P, ring, P], F16)
            keys = sb(scope, "keys", [P, ring, s.nb * w], F16)
            total = sb(scope, "total", [P, 2, s.nb * w])
            n = self.c_key_d.shape[1]
            c_key, c_low, c_keep = (sb(scope, name, [P, n]) for name in ("c_key", "c_low", "c_keep"))
            c_win = sb(scope, "c_win", [1, n], I32)
            iota = self.load_iota(scope)
            self.load(c_key[:, :], self.c_key_d)
            self.load(c_low[:, :], self.c_low_d)
            self.load(c_keep[:, :], self.c_keep_d[0, :].partition_broadcast(P))
            self.load(c_win[:, :], self.c_win_d)
            self.load(far[:, :], self.io["c_far"].partition_broadcast(P))
            zero = q.dve(lambda e: e.memset(total[:, :, :], 0.0))
            self.wait_setup()
            mm, sums, copies = [], [], []

            def one_hots(i):
                old = mm[i - ring] if i >= ring else None
                a = q.pool(lambda e: e.tensor_scalar(lows[:, i % ring, :], iota[:, :],
                                                     c_low[:, i:i + 1], None, ALU.is_equal), after=[old])
                b = q.dve(lambda e: e.tensor_scalar(keys[:, i % ring, :], far[:, :],
                                                    c_key[:, i:i + 1], None, ALU.is_equal), after=[old])
                return a, b

            hots = {i: one_hots(i) for i in range(2)}
            for i in range(s.csteps):
                ps = self.bank[i % 8][:, 0:s.nb * w]
                a, b = hots.pop(i)
                mm.append(q.pe(lambda e, i=i, ps=ps: e.matmul(
                    ps, lows[:, i % ring, :], keys[:, i % ring, :], start=True, stop=True),
                    after=[a, b, sums[i - 8] if i >= 8 else None]))
                if i + 2 < s.csteps:
                    hots[i + 2] = one_hots(i + 2)
                sums.append(q.dve(lambda e, i=i, ps=ps: e.scalar_tensor_tensor(
                    total[:, i % 2, :], total[:, (i + 1) % 2, :], c_keep[:, i:i + 1], ps,
                    ALU.mult, ALU.add),
                    after=[mm[i], sums[i - 1] if i else zero, copies[i - 2] if i >= 2 else None]))

                def put(e, i=i):
                    at = e.value_load(c_win[0:1, i:i + 1], min_val=0, max_val=s.windows - 1)
                    return e.activation(
                        self.counts[:, :, bass.ds(at * w, w)],
                        total[:, i % 2, :].rearrange("p (h j) -> p h j", j=w), ACT.Copy)
                copies.append(q.act(put, after=[sums[i], copies[i - 1] if i else None]))
            q.barrier()
        self.bank_free = [None] * 8

    def wait_setup(self):
        for e in self.q.ENGINES:
            self.q.wait(e, [self.loaded()])

    def last_dve(self):
        return "vector", self.q.count["vector"]

    def last_act(self):
        return "scalar", self.q.count["scalar"]

    def load_nodes(self, x):
        s, q = self.s, self.q
        t = q.dve(lambda e: e.memset(x[:, s.nb - 1, :], 0.0))
        full = (s.nb - 1) * P
        xin = self.io["x"]
        self.load(x[:, 0:s.nb - 1, :], xin[0:full, :].rearrange("(b l) f -> l b f", l=P))
        self.load(x[0:s.last, s.nb - 1, :], xin[full:s.n, :], after=[t])

    def ln_factors(self, scope, x, after, scale=1.0):
        s, q = self.s, self.q
        stats = self.sb(scope, "ln_stats", [P, s.nb, 6])
        mv = self.sb(scope, "ln_mv", [P, s.nb, 2])
        rstd = self.sb(scope, "ln_rstd", [P, s.nb])
        nbias = self.sb(scope, "ln_nbias", [P, s.nb])
        for b in range(s.nb):
            t = q.dve(lambda e, b=b: e.bn_stats(stats[:, b, :], x[:, b, :]), after=after)
        for b in range(s.nb):
            t = q.dve(lambda e, b=b: e.bn_aggr(mv[:, b, :], stats[:, b, :]), after=[t] if b == 0 else ())
        t = q.act(lambda e: e.activation(rstd[:, :], mv[:, :, 1], ACT.Sqrt, bias=self.eps[:, 0:1]), after=[t])
        t = q.dve(lambda e: e.reciprocal(rstd[:, :], rstd[:, :]), after=[t])
        if scale != 1.0:
            t = q.dve(lambda e: e.tensor_scalar(rstd[:, :], rstd[:, :], scale, None, ALU.mult), after=[t])
        t = q.dve(lambda e: e.scalar_tensor_tensor(nbias[:, :], mv[:, :, 0], -1.0, rstd[:, :],
                                                   ALU.mult, ALU.mult), after=[t])
        return rstd, nbias, t

    def ln_apply(self, y, x, rstd, nbias, func, after):
        q = self.q
        return [q.act(lambda e, b=b: e.activation(y[:, b, :], x[:, b, :], func, bias=nbias[:, b:b + 1],
                                                  scale=rstd[:, b:b + 1]), after=after)
                for b in range(self.s.nb)]

    def split(self, halves, y, rows, b, after):
        q = self.q
        t = q.act(lambda e: e.activation(halves[0:rows, b, 0:D], y, ACT.Copy), after=after)
        return q.dve(lambda e: e.tensor_tensor(halves[0:rows, b, D:2 * D], y, halves[0:rows, b, 0:D],
                                               ALU.subtract), after=[t])

    def hop(self, halves, ready, finish):
        s, q = self.s, self.q
        for b in range(s.nb):
            rows, i = s.rows(b), b % 8
            ps = self.bank[i][0:rows, 0:2 * D + 1]
            for k in range(s.nb):
                t = q.pe(lambda e, b=b, k=k, rows=rows, ps=ps: e.matmul(
                    ps, self.counts[:, k, b * P:b * P + rows], halves[:, k, :],
                    start=k == 0, stop=k == s.nb - 1),
                    after=[self.bank_free[i]] + list(ready) if k == 0 else ())
            self.bank_free[i] = finish(b, rows, self.bank[i], t)

    def layer0(self, x_out):
        s, q, io = self.s, self.q, self.io
        nc = s.nc
        cut = nc // 8
        assert cut * 8 == nc and cut <= 512
        with ExitStack() as scope:
            sb = self.sb
            ht = sb(scope, "ht", [P, s.nb * P])
            nodes = sb(scope, "nodes", [P, s.nb, D])
            qd = x_out[:, :, :].rearrange("p b f -> p (b f)")[:, 0:nc]
            w_msg = sb(scope, "w_msg", [P, D + 1])
            w_dst = sb(scope, "w_dst", [P, 1])
            b_msg = sb(scope, "b_msg", [P, D])
            b_att = sb(scope, "b_att", [P, 1])
            w_ih = sb(scope, "w_ih", [P, 3 * D])
            w_hh = sb(scope, "w_hh", [P, 3 * D])
            cols = sb(scope, "cols", [P, 8])
            bias = sb(scope, "bias", [P, 2])
            ps_src = sb(scope, "ps_src", [P, s.nb])
            self.load_nodes(nodes)
            for dst, src in ((w_msg[:, 0:D], io["L0_gnn_W_msg"]), (w_msg[:, D:D + 1], io["L0_gnn_W_att"][0:D, :]),
                             (w_dst[:, :], io["L0_gnn_W_att"][D:2 * D, :]),
                             (b_msg[:, :], io["L0_gnn_b_msg"].partition_broadcast(P)),
                             (b_att[:, :], io["L0_gnn_b_att"].partition_broadcast(P)),
                             (w_ih[:, :], io["L0_gnn_W_ih_t"]), (w_hh[:, :], io["L0_gnn_W_hh_t"]),
                             (cols[:, 0:3], io["L0_gnn_b_ih_t"]), (cols[:, 3:6], io["L0_gnn_b_hh_t"]),
                             (cols[:, 6:7], self.column("L0_gnn_gamma")), (cols[:, 7:8], self.column("L0_gnn_beta"))):
                self.load(dst, src)
            self.wait_setup()
            rstd, nbias, t = self.ln_factors(scope, nodes, ())
            h = self.ln_apply(nodes, nodes, rstd, nbias, ACT.Relu, [t])
            for b in range(s.nb):
                t = self.transpose_to(ht[:, b * P:(b + 1) * P], nodes[:, b, :], [h[b]])
            q.dve(lambda e: e.tensor_tensor(bias[:, :], cols[:, 0:2], cols[:, 3:5], ALU.add))
            for b in range(s.nb):
                i = self.next_bank()
                ps = self.bank[i]
                t = q.pe(lambda e, b=b, ps=ps: e.matmul(ps[:, 0:D + 1], ht[:, b * P:(b + 1) * P], w_msg[:, :],
                                                        start=True, stop=True), after=[t, self.bank_free[i]])
                q.dve(lambda e, b=b, ps=ps: e.tensor_tensor(nodes[:, b, :], ps[:, 0:D], b_msg[:, :], ALU.add),
                      after=[t])
                self.bank_free[i] = q.dve(lambda e, b=b, ps=ps: e.tensor_tensor(
                    ps_src[:, b:b + 1], ps[:, D:D + 1], b_att[:, :], ALU.add), after=[t])
            messages = self.last_dve()
            for c in range(8):
                i = self.next_bank()
                ps = self.bank[i][:, 0:cut]
                t = q.pe(lambda e, c=c, ps=ps: e.matmul(ps, w_dst[:, 0:1].to_broadcast([P, P]),
                                                        ht[:, c * cut:(c + 1) * cut], start=True, stop=True),
                         after=[self.bank_free[i]])
                qd_done = self.bank_free[i] = q.act(lambda e, c=c, ps=ps: e.activation(
                    qd[:, c * cut:(c + 1) * cut], ps, ACT.Copy), after=[t])
            with ExitStack() as inner:
                ring, parts = 3, 4
                wide = nc // parts
                att = sb(inner, "att", [P, ring, wide])
                used = [None] * ring
                n = 0
                for k in range(s.nb):
                    for c in range(parts):
                        r = n % ring
                        n += 1
                        t = q.act(lambda e, k=k, c=c, r=r: e.activation(
                            att[:, r, :], qd[:, c * wide:(c + 1) * wide], ACT.Sigmoid, bias=ps_src[:, k:k + 1]),
                            after=[messages, qd_done, used[r]])
                        t = q.dve(lambda e, k=k, c=c, r=r: e.tensor_tensor(
                            att[:, r, :], att[:, r, :], self.counts[:, k, c * wide:(c + 1) * wide], ALU.mult),
                            after=[t])
                        for j in range(2):
                            i = 2 * c + j
                            used[r] = q.pe(lambda e, k=k, i=i, j=j, r=r: e.matmul(
                                self.bank[i][:, 0:cut], nodes[:, k, :], att[:, r, j * cut:(j + 1) * cut],
                                start=k == 0, stop=k == s.nb - 1),
                                after=[t, self.bank_free[i] if k == 0 else None])
                sums = used[r]
                agg = qd
                for c in range(8):
                    last_read = ("scalar", q.count["scalar"])
                    t = q.dve(lambda e, c=c: e.tensor_copy(agg[:, c * cut:(c + 1) * cut],
                                                           self.bank[c][:, 0:cut]), after=[sums, last_read])
                    self.bank_free[c] = t
                q.barrier()
            with ExitStack() as inner:
                gate = sb(inner, "gate", [P, 2, 3, cut])
                stats = sb(inner, "stats", [P, 8, 6])
                mv = sb(inner, "mv", [P, 4])
                new = nodes[:, :, :].rearrange("p b f -> p (b f)")
                free = {}
                for c in range(8):
                    cs = slice(c * cut, (c + 1) * cut)
                    g = c % 2
                    rb, zb, nb_, hb = (self.bank[4 * g + j][:, 0:cut] for j in range(4))
                    wait = [free.get(c - 2)]
                    for ps, j in ((rb, 0), (zb, 1)):
                        q.pe(lambda e, ps=ps, j=j, cs=cs: e.matmul(ps, w_ih[:, j * D:(j + 1) * D], agg[:, cs],
                                                                   start=True, stop=False), after=wait)
                        q.pe(lambda e, ps=ps, j=j, cs=cs: e.matmul(ps, w_hh[:, j * D:(j + 1) * D], ht[:, cs],
                                                                   start=False, stop=True))
                    q.pe(lambda e, ps=nb_, cs=cs: e.matmul(ps, w_ih[:, 2 * D:], agg[:, cs], start=True, stop=True))
                    t = q.pe(lambda e, ps=hb, cs=cs: e.matmul(ps, w_hh[:, 2 * D:], ht[:, cs],
                                                              start=True, stop=True))
                    r, z, m = (gate[:, g, j, :] for j in range(3))
                    d = r
                    a = q.act(lambda e, r=r, rb=rb: e.activation(r, rb, ACT.Sigmoid, bias=bias[:, 0:1]),
                              after=[t] + wait)
                    b = q.act(lambda e, z=z, zb=zb: e.activation(z, zb, ACT.Sigmoid, bias=bias[:, 1:2]))
                    t = q.dve(lambda e, m=m, hb=hb, r=r: e.scalar_tensor_tensor(m, hb, cols[:, 5:6], r,
                                                                                ALU.add, ALU.mult), after=[a])
                    t = q.dve(lambda e, m=m, nb_=nb_: e.tensor_tensor(m, m, nb_, ALU.add), after=[t])
                    t = q.act(lambda e, m=m: e.activation(m, m, ACT.Tanh, bias=cols[:, 2:3]), after=[t])
                    t = q.dve(lambda e, m=m, d=d, cs=cs: e.tensor_tensor(d, ht[:, cs], m, ALU.subtract), after=[t])
                    t = q.dve(lambda e, d=d, z=z: e.tensor_tensor(d, d, z, ALU.mult), after=[t, b])
                    t = q.dve(lambda e, d=d, m=m, cs=cs: e.tensor_tensor(new[:, cs], d, m, ALU.add), after=[t])
                    real = min(cut, s.n - c * cut)
                    t = q.dve(lambda e, c=c, real=real: e.bn_stats(stats[:, c, :], new[:, c * cut:c * cut + real]),
                              after=[t])
                    free[c] = t
                t = q.dve(lambda e: e.bn_aggr(mv[:, 0:2], stats[:, :, :].rearrange("p a b -> p (a b)")), after=[t])
                t = q.act(lambda e: e.activation(mv[:, 2:3], mv[:, 1:2], ACT.Sqrt, bias=self.eps[:, 0:1]), after=[t])
                t = q.dve(lambda e: e.reciprocal(mv[:, 2:3], mv[:, 2:3]), after=[t])
                t = q.dve(lambda e: e.tensor_tensor(mv[:, 2:3], mv[:, 2:3], cols[:, 6:7], ALU.mult), after=[t])
                t = q.dve(lambda e: e.scalar_tensor_tensor(mv[:, 3:4], mv[:, 0:1], -1.0, mv[:, 2:3],
                                                           ALU.mult, ALU.mult), after=[t])
                t = q.dve(lambda e: e.tensor_tensor(mv[:, 3:4], mv[:, 3:4], cols[:, 7:8], ALU.add), after=[t])
                for c in range(8):
                    cs = slice(c * cut, (c + 1) * cut)
                    t = q.act(lambda e, cs=cs: e.activation(new[:, cs], new[:, cs], ACT.Identity,
                                                            bias=mv[:, 3:4], scale=mv[:, 2:3]), after=[t])
                q.barrier()
            self.bank_free = [None] * 8
            self.add_transposed(x_out, new, ht, t)
            q.barrier()

    def add_transposed(self, x_out, yt, xbuf, after):
        s, q = self.s, self.q
        xs = xbuf[:, :].rearrange("p (b f) -> p b f", f=D)
        self.load_nodes(xs)
        t = q.dve(lambda e: e.memset(x_out[:, s.nb - 1, :], 0.0))
        for b in range(s.nb):
            rows = s.rows(b)
            self.transpose_to(None, yt[:, b * P:b * P + rows], [after], copy=lambda ps, tk, b=b, rows=rows: q.dve(
                lambda e: e.tensor_tensor(x_out[0:rows, b, :], ps, xs[0:rows, b, :], ALU.add),
                after=[tk, t, self.loaded()]))

    def column(self, name):
        return self.io[name].rearrange("(a b) -> a b", b=1)

    def degree(self, rdeg, b, rows, ps, token):
        q = self.q
        t = q.dve(lambda e: e.tensor_scalar(rdeg[0:rows, b:b + 1], ps[0:rows, 2 * D:2 * D + 1], 1.0, F16_SCALE,
                                            ALU.max, ALU.mult), after=[token])
        return q.dve(lambda e: e.reciprocal(rdeg[0:rows, b:b + 1], rdeg[0:rows, b:b + 1]), after=[t])

    def mean_rows(self, y, ps, rdeg, b, rows, token, tmp):
        q = self.q
        t = q.act(lambda e: e.activation(tmp, ps[0:rows, D:2 * D], ACT.Copy, scale=rdeg[0:rows, b:b + 1]),
                  after=[token])
        return q.dve(lambda e: e.scalar_tensor_tensor(y, ps[0:rows, 0:D], rdeg[0:rows, b:b + 1], tmp,
                                                      ALU.mult, ALU.add), after=[t])

    def halves_of_ln(self, scope, x, halves, hs):
        s, q = self.s, self.q
        rstd, nbias, t = self.ln_factors(scope, x, [self.last_dve()], F16_SCALE)
        h = self.ln_apply(hs, x, rstd, nbias, ACT.Relu, [t])
        for b in range(s.nb):
            t = self.split(halves, hs[:, b, :], P, b, [h[b]])
        t = q.dve(lambda e: e.memset(halves[:, :, 2 * D:2 * D + 1], 1.0))
        return t

    def layer1(self, x, rdeg):
        s, q = self.s, self.q
        with ExitStack() as scope:
            sb = self.sb
            halves = [sb(scope, "halves", [P, s.nb, 2 * D + 1], F16) for _ in range(2)]
            with ExitStack() as inner:
                hs = sb(inner, "hs", [P, s.nb, D])
                ready = self.halves_of_ln(inner, x, halves[0], hs)
                q.dve(lambda e: e.memset(halves[1][:, :, :], 0.0))
                q.barrier()
            tmp = sb(scope, "tmp", [P, 4, 2, D])
            free = [None] * 4
            for n in range(3):
                a, out = halves[n % 2], halves[(n + 1) % 2]

                def finish(b, rows, ps, token, n=n, out=out):
                    k = b % 4
                    if n == 0:
                        token = self.degree(rdeg, b, rows, ps, token)
                    t0, t1 = tmp[0:rows, k, 0, :], tmp[0:rows, k, 1, :]
                    q.wait("scalar", [free[k]])
                    t = self.mean_rows(t1, ps, rdeg, b, rows, token, t0)
                    if n < 2:
                        u = q.dve(lambda e: e.tensor_scalar(t1, t1, F16_SCALE, None, ALU.mult), after=[t])
                        free[k] = self.split(out, t1, rows, b, [u])
                    else:
                        free[k] = q.dve(lambda e: e.tensor_tensor(x[0:rows, b, :], x[0:rows, b, :], t1, ALU.add),
                                        after=[t])
                    return t
                self.hop(a, [ready], finish)
                ready = self.last_dve()
            q.barrier()
            self.bank_free = [None] * 8

    def layer2(self, x, rdeg):
        s, q, io = self.s, self.q, self.io
        cut = s.nc // 8
        with ExitStack() as scope:
            sb = self.sb
            ht = sb(scope, "ht2", [P, s.nb * P])
            mt = sb(scope, "mt", [P, s.nb * P])
            cols = sb(scope, "cols2", [P, 9])
            fac = sb(scope, "fac", [P, 2, 2])
            names = ["gamma1", "beta1", "rm1", "rv1", "gamma2", "beta2", "rm2", "rv2", "b_self"]
            for j, name in enumerate(names):
                self.load(cols[:, j:j + 1], self.column("L2_gnn_" + name))
            self.wait_setup()
            for j in range(2):
                g, b, m, v = (cols[:, 4 * j + i:4 * j + i + 1] for i in range(4))
                f, sh = fac[:, j, 0:1], fac[:, j, 1:2]
                t = q.act(lambda e, f=f, v=v: e.activation(f, v, ACT.Sqrt, bias=self.eps[:, 0:1]))
                t = q.dve(lambda e, f=f: e.reciprocal(f, f), after=[t])
                t = q.dve(lambda e, f=f, g=g: e.tensor_tensor(f, f, g, ALU.mult), after=[t])
                t = q.dve(lambda e, f=f, m=m, sh=sh: e.scalar_tensor_tensor(sh, m, -1.0, f, ALU.mult, ALU.mult),
                          after=[t])
                t = q.dve(lambda e, b=b, sh=sh: e.tensor_tensor(sh, sh, b, ALU.add), after=[t])
            t = q.dve(lambda e: e.tensor_tensor(fac[:, 1, 1:2], fac[:, 1, 1:2], cols[:, 8:9], ALU.add), after=[t])
            with ExitStack() as inner:
                halves = sb(inner, "halves", [P, s.nb, 2 * D + 1], F16)
                hs = mt[:, :].rearrange("p (b f) -> p b f", f=D)
                ready = self.halves_of_ln(inner, x, halves, hs)
                for b in range(s.nb):
                    t = self.transpose_to(ht[:, b * P:(b + 1) * P], hs[:, b, :], [ready])
                q.barrier()
                tmp = sb(inner, "tmp", [P, 2, 2, D])
                free = [None] * 2

                def finish(b, rows, ps, token):
                    k = b % 2
                    t0, t1 = tmp[0:rows, k, 0, :], tmp[0:rows, k, 1, :]
                    q.wait("scalar", [free[k]])
                    t = self.mean_rows(t1, ps, rdeg, b, rows, token, t0)
                    pend.append((b, rows, k, t1, t))
                    if len(pend) > 1:
                        flush()
                    return t

                def flush():
                    b, rows, k, t1, t = pend.pop(0)
                    ps = self.bank[b % 8][:, 384:384 + rows]
                    t = q.pe(lambda e: e.transpose(ps, t1, self.ident[0:rows, 0:rows]), after=[t])
                    t = q.dve(lambda e: e.tensor_copy(mt[:, b * P:b * P + rows], ps), after=[t])
                    free[k] = self.bank_free[b % 8] = t
                pend = []
                self.hop(halves, [ready], finish)
                flush()
                q.dve(lambda e: e.memset(mt[:, s.n:], 0.0))
                q.barrier()
            with ExitStack() as inner:
                mid = sb(inner, "mid", [P, 2, 2, cut])
                w = sb(inner, "w2", [P, 3, D])
                for j, name in enumerate(("W1", "W2", "W_self")):
                    self.load(w[:, j, :], io[f"L2_gnn_{name}_t"])
                self.wait_setup()
                free = {}
                for c in range(8):
                    cs, g = slice(c * cut, (c + 1) * cut), c % 2
                    p1, p2, p3 = (self.bank[4 * g + j][:, 0:cut] for j in range(3))
                    wait = [free.get(c - 2)]
                    t = q.pe(lambda e, p=p1, cs=cs: e.matmul(p, w[:, 0, :], mt[:, cs], start=True, stop=True),
                             after=wait)
                    u = q.pe(lambda e, p=p3, cs=cs: e.matmul(p, w[:, 2, :], ht[:, cs], start=True, stop=True))
                    t = q.act(lambda e, g=g, p=p1: e.activation(mid[:, g, 0, :], p, ACT.Relu, bias=fac[:, 0, 1:2],
                                                                scale=fac[:, 0, 0:1]), after=[t] + wait)
                    v = q.act(lambda e, g=g, p=p3: e.activation(mid[:, g, 1, :], p, ACT.Identity,
                                                                bias=fac[:, 1, 1:2], scale=1.0 / F16_SCALE),
                              after=[u])
                    t = q.pe(lambda e, g=g, p=p2: e.matmul(p, w[:, 1, :], mid[:, g, 0, :], start=True, stop=True),
                             after=[t])
                    free[c] = t = q.dve(lambda e, g=g, p=p2, cs=cs: e.scalar_tensor_tensor(
                        mt[:, cs], p, fac[:, 1, 0:1], mid[:, g, 1, :], ALU.mult, ALU.add), after=[t, v])
                q.barrier()
            self.bank_free = [None] * 8
            for b in range(s.nb):
                rows = s.rows(b)
                self.transpose_to(None, mt[:, b * P:b * P + rows], [t], copy=lambda ps, tk, b=b, rows=rows: q.dve(
                    lambda e: e.tensor_tensor(x[0:rows, b, :], x[0:rows, b, :], ps, ALU.add), after=[tk]))
            q.barrier()

    def layer3(self, x):
        s, q, io = self.s, self.q, self.io
        n, groups = s.esteps, s.esteps // 4
        self.xl = self.dram("x_l", (s.n, D))
        self.gathered = self.dram("gathered", (groups, P, 4 * D))
        with ExitStack() as scope:
            sb = self.sb
            h = sb(scope, "h", [P, s.nb, D])
            alpha = sb(scope, "alpha", [P, s.run, 16, HEADS])
            assert s.run % 4 == 0
            loop = sb(scope, "loop", [P, s.run, 16, HEADS])
            rstd, nbias, t = self.ln_factors(scope, x, [self.last_dve()])
            hd = self.ln_apply(h, x, rstd, nbias, ACT.Relu, [t])
            with ExitStack() as inner:
                xr = self.project(inner, h, hd)
                self.logits(xr, alpha, loop)
                q.barrier()
            self.bank_free = [None] * 8
            self.softmax_numerators(alpha, loop)
            acc = sb(scope, "acc", [P, s.nb, D + 2 * HEADS])
            self.weighted_sums(alpha, loop, acc)
            q.barrier()
            self.bank_free = [None] * 8
            self.feed_forward(x, h, acc)

    def ln_affine_t(self, scope, ut, x, gain, shift, after):
        s, q = self.s, self.q
        tmp = self.sb(scope, "ln_rows", [P, s.nb, D])
        rstd, nbias, t = self.ln_factors(scope, x, after)
        rows = self.ln_apply(tmp, x, rstd, nbias, ACT.Identity, [t])
        for b in range(s.nb):
            t = self.transpose_to(None, tmp[:, b, :], [rows[b]], copy=lambda ps, tk, b=b: q.dve(
                lambda e: e.tensor_scalar(ut[:, b * P:(b + 1) * P], ps, gain, shift, ALU.mult, ALU.add),
                after=[tk, self.loaded()]))
        return t

    def project(self, scope, h, hd):
        s, q, io = self.s, self.q, self.io
        xr = self.sb(scope, "x_r", [P, s.nb, D + HEADS])
        with ExitStack() as inner:
            sb = self.sb
            w = sb(inner, "w_lr", [P, 2 * D])
            cols = sb(inner, "cols3", [P, 2])
            ut = sb(inner, "ut", [P, s.nb * P])
            xl = sb(inner, "xl", [P, s.nb, D])
            w_e = sb(inner, "w_e_rows", [P, D])
            att = sb(inner, "att_rows", [P, D])
            mean = sb(inner, "mean", [P, D])
            z = sb(inner, "z_loop", [P, s.nb, D])
            for k in range(4):
                self.load(w_e[k * DE:(k + 1) * DE, :], io["L3_gnn_W_e"])
            self.load(att[:, :], io["att_row"].partition_broadcast(P))
            self.load(w[:, 0:D], io["L3_gnn_W_l"])
            self.load(w[:, D:2 * D], io["L3_gnn_W_r"])
            self.load(cols[:, 0:1], self.column("L3_gnn_ln1_g"))
            self.load(cols[:, 1:2], self.column("L3_gnn_ln1_b"))
            self.wait_setup()
            t = self.ln_affine_t(inner, ut, h, cols[:, 0:1], cols[:, 1:2], [hd[-1]])
            for b in range(s.nb):
                i = self.next_bank()
                ps = self.bank[i]
                t = q.pe(lambda e, b=b, ps=ps: e.matmul(ps[:, 0:2 * D], ut[:, b * P:(b + 1) * P], w[:, :],
                                                        start=True, stop=True), after=[t, self.bank_free[i]])
                q.dve(lambda e, b=b, ps=ps: e.tensor_copy(xl[:, b, :], ps[:, 0:D]), after=[t])
                t = self.bank_free[i] = q.dve(lambda e, b=b, ps=ps: e.tensor_copy(xr[:, b, 0:D], ps[:, D:2 * D]))
            full = (s.nb - 1) * P
            lane = q.lane("x_l_stores")
            q.dma("sync", lane, lambda e: e.dma_start(
                self.xl[0:full, :].rearrange("(b l) f -> l b f", l=P), xl[:, 0:s.nb - 1, :]), after=[t])
            q.dma("sync", lane, lambda e: e.dma_start(self.xl[full:s.n, :], xl[0:s.last, s.nb - 1, :]))
            i = self.next_bank()
            ps = self.bank[i][:, 0:D]
            u = q.pe(lambda e: e.matmul(ps, self.edge_sum[:, 0:1].to_broadcast([P, P]), w_e[:, :],
                                        start=True, stop=True), after=[self.bank_free[i]])
            u = self.bank_free[i] = q.dve(lambda e: e.tensor_scalar(mean[:, :], ps, 1.0 / s.edges, None, ALU.mult),
                                          after=[u])
            t = q.dve(lambda e: e.tensor_tensor(z[:, :, :], xl[:, :, :], xr[:, :, 0:D], ALU.add), after=[t])
            t = q.dve(lambda e: e.tensor_tensor(z[:, :, :], z[:, :, :], self.rows_of(mean), ALU.add), after=[t, u])
            t = q.dve(lambda e: e.scalar_tensor_tensor(z[:, :, :], z[:, :, :], NEG_SLOPE, z[:, :, :],
                                                       ALU.mult, ALU.max), after=[t])
            t = q.dve(lambda e: e.tensor_tensor(z[:, :, :], z[:, :, :], self.rows_of(att), ALU.mult), after=[t])
            q.dve(lambda e: e.tensor_reduce(xr[:, :, D:], z[:, :, :].rearrange("p b (h c) -> p b h c", c=CH),
                                            AX.X, ALU.add), after=[t])
            q.barrier()
        return xr

    def rows_of(self, row):
        return row[:, :].rearrange("p (o f) -> p o f", o=1).to_broadcast([P, self.s.nb, D])

    def logits(self, xr, alpha, loop):
        s, q, io = self.s, self.q, self.io
        n, groups = s.esteps, s.esteps // 4
        with ExitStack() as scope:
            sb = self.sb
            src = sb(scope, "src", [P, n], I32)
            regs = sb(scope, "regs", [1, 2, n], I32)
            w_e = sb(scope, "w_e", [P, 4, D + HEADS])
            att = sb(scope, "att", [P, D])
            place = sb(scope, "place", [P, 16])
            slots, ahead = 6, 4
            rows = sb(scope, "rows", [P, slots, 4 * D])
            edges = sb(scope, "edges", [P, slots, P])
            rel = sb(scope, "rel", [P, slots, 4 * P], I16)
            hot = sb(scope, "hot", [P, 2, 4 * P])
            z = sb(scope, "z", [P, 2, 4 * D])
            leaky = sb(scope, "leaky", [P, 2, 4 * D])
            self.load(src[:, :], self.e_src)
            self.load(regs[:, :, :], self.e_regs.rearrange("(o a) n -> o a n", o=1))
            t = q.dve(lambda e: e.memset(w_e[:, :, :], 0.0))
            for k in range(4):
                self.load(w_e[k * DE:(k + 1) * DE, k, 0:D], io["L3_gnn_W_e"], after=[t])
            self.load(att[:, :], io["att_row"].partition_broadcast(P))
            self.load(place[:, :], io["c_step"])
            self.wait_setup()
            got = [q.lane(f"rows{i}") for i in range(slots)]
            edge_lane = [q.lane(f"edges{i}") for i in range(slots)]
            rel_lane = [q.lane(f"rel{i}") for i in range(slots)]
            kept = [q.lane(f"kept{i}") for i in range(slots)]
            sums, hots, products, used, parts, loops = [], [], [], [], [], []
            stores = []

            def fetch(g):
                r = g % slots
                old = g - slots
                for k in range(4):
                    v = 4 * g + k
                    rows_in[g] = q.dma("gpsimd", got[r], lambda e, v=v, r=r, k=k: e.indirect_dma_start(
                        rows[:, r, k * D:(k + 1) * D], None, self.xl,
                        bass.IndirectOffsetOnAxis(ap=src[:, v:v + 1], axis=0)),
                        after=[sums[old], stores[old]] if old >= 0 else ())
                    q.wait("sync", [products[old]] if old >= 0 else ())

                    def load_edges(e, v=v, r=r, k=k):
                        tile = e.value_load(regs[0:1, 0, v:v + 1], min_val=0, max_val=s.tiles)
                        return e.dma_start(edges[k * DE:(k + 1) * DE, r, :],
                                           io["edge_t"][bass.ds(tile, 1), :, :].rearrange("o k e -> (o k) e"))
                    edges_in[g] = q.dma("sync", edge_lane[r], load_edges)
                rel_in[g] = q.dma("sync", rel_lane[r], lambda e, g=g, r=r: e.dma_start(
                    rel[:, r, :], self.e_rel_rows[4 * g:4 * g + 4, :].rearrange("v e -> (v e)").partition_broadcast(P)),
                    after=[hots[old]] if old >= 0 else ())

            rows_in, edges_in, rel_in = {}, {}, {}
            for g in range(ahead):
                fetch(g)
            for g in range(groups):
                r, two = g % slots, g % 2
                hots.append(q.dve(lambda e, r=r, two=two: e.tensor_scalar(
                    hot[:, two, :], rel[:, r, :], place[:, 0:1], None, ALU.is_equal),
                    after=[rel_in[g], products[g - 2] if g >= 2 else None]))
                wide = D + HEADS
                pair = self.psum[:, 2 * (g % 4):2 * (g % 4) + 2, 0:2 * wide].rearrange(
                    "p b (v f) -> p b v f", f=wide)
                q.wait("tensor", [hots[g], edges_in[g]] + ([sums[g - 4], loops[g - 4]] if g >= 4 else []))
                for k in range(4):
                    v = 4 * g + k

                    def from_destination(e, v=v, k=k, two=two, pair=pair):
                        b = e.value_load(regs[0:1, 1, v:v + 1], min_val=0, max_val=s.nb - 1)
                        return e.matmul(pair[:, k // 2, k % 2, :], hot[:, two, k * P:(k + 1) * P],
                                        xr[:, bass.ds(b, 1), :].rearrange("p o f -> p (o f)"),
                                        start=True, stop=False)
                    q.pe(from_destination)
                    t = q.pe(lambda e, k=k, r=r, pair=pair: e.matmul(
                        pair[:, k // 2, k % 2, :], edges[:, r, :], w_e[:, k, :], start=False, stop=True))
                products.append(t)
                four = "p (b v f) -> p b v f"
                sums.append(q.dve(lambda e, two=two, r=r, pair=pair, four=four: e.tensor_tensor(
                    z[:, two, :].rearrange(four, b=2, f=D), pair[:, :, :, 0:D],
                    rows[:, r, :].rearrange(four, b=2, f=D), ALU.add),
                    after=[t, rows_in[g], parts[g - 2] if g >= 2 else None]))
                loops.append(q.act(lambda e, g=g, pair=pair: e.activation(
                    self.places(loop, g).rearrange("p (b v) h -> p b v h", b=2), pair[:, :, :, D:], ACT.Copy),
                    after=[sums[g]]))
                stores.append(q.dma("sync", kept[r], lambda e, g=g, r=r: e.dma_start(
                    self.gathered[g, :, :], rows[:, r, :]), after=[rows_in[g]]))
                parts.append(q.dve(lambda e, two=two: e.scalar_tensor_tensor(
                    leaky[:, two, :], z[:, two, :], NEG_SLOPE, z[:, two, :], ALU.mult, ALU.max),
                    after=[sums[g], used[g - 2] if g >= 2 else None]))
                if g >= 1:
                    self.head_sums(alpha, leaky, att, g - 1, parts, used)
                if g + ahead < groups:
                    fetch(g + ahead)
            self.head_sums(alpha, leaky, att, groups - 1, parts, used)
            q.barrier()

    def head_sums(self, alpha, leaky, att, g, parts, used):
        q, two = self.q, g % 2
        view = leaky[:, two, :].rearrange("p (v f) -> p v f", f=D)
        t = q.dve(lambda e: e.tensor_tensor(view, view, att[:, :].rearrange("p (o f) -> p o f", o=1)
                                            .to_broadcast([P, 4, D]), ALU.mult), after=[parts[g]])
        used.append(q.dve(lambda e: e.tensor_reduce(
            self.places(alpha, g),
            leaky[:, two, :].rearrange("p (v h c) -> p v h c", v=4, c=CH), AX.X, ALU.add), after=[t]))

    def places(self, alpha, g):
        c, at = divmod(4 * g, self.s.run)
        return alpha[:, at:at + 4, c, :]

    def softmax_numerators(self, alpha, loop):
        s, q = self.s, self.q
        n = s.run * P
        with ExitStack() as scope:
            sb = self.sb
            a = sb(scope, "a", [P, n])
            top = sb(scope, "top", [P, n])
            dst = sb(scope, "dst", [P, n + 2])
            new = sb(scope, "new", [P, n])
            carry = sb(scope, "carry", [P, 4])
            row = sb(scope, "row", [1, 3, P])
            for c in range(16):
                self.load(dst[8 * c:8 * c + 8, :],
                          self.e_dst_flat[c * n:(c + 1) * n + 2].partition_broadcast(8))
            used = [("vector", q.count["vector"]), ("scalar", q.count["scalar"])]
            for g in range(s.run):
                t = self.transpose_to(a[:, g * P:(g + 1) * P],
                                      alpha[:, g, :, :].rearrange("p c h -> p (c h)"), [])
            self.wait_setup()
            for back in (False, True):
                other = dst[:, 2:n + 2] if back else dst[:, 0:n]
                t = q.dve(lambda e, other=other: e.tensor_tensor(new[:, :], dst[:, 1:n + 1], other,
                                                                 ALU.not_equal), after=[t])
                t = q.dve(lambda e: e.tensor_scalar(new[:, :], new[:, :], NONE, None, ALU.mult), after=[t])
                source = top if back else a
                trial = alpha[:, :, :, :].rearrange("p g c h -> p (g c h)") if back else top[:, :]

                def scan(start, after, to, back=back, source=source, new=new):
                    flip = (lambda m: m[:, ::-1]) if back else (lambda m: m)
                    return q.dve(lambda e: e.tensor_tensor_scan(flip(to), flip(new[:, :]), flip(source[:, :]),
                                                                start, ALU.add, ALU.max), after=after)
                end = (lambda m: m[:, 0:1]) if back else (lambda m: m[:, n - 1:n])
                t = scan(NONE, [t], trial)
                q.dve(lambda e, trial=trial, end=end: e.tensor_copy(carry[:, 0:1], end(trial)), after=[t])
                t = q.dve(lambda e: e.tensor_reduce(carry[:, 1:2], new[:, :], AX.X, ALU.min), after=[t])
                t = q.dve(lambda e: e.tensor_copy(carry[:, 2:3], carry[:, 0:1]), after=[t])
                self.transpose_to(row[:, 0, :], carry[:, 1:2], [t])
                t = self.transpose_to(row[:, 1, :], carry[:, 2:3], [t])
                t = q.dve(lambda e: e.memset(row[:, 2, :], NONE), after=[t])
                for h in range(HEADS):
                    def of(j, h=h, back=back):
                        v = row[:, j, :].rearrange("p (c h) -> p h c", h=HEADS)[:, h, :]
                        return v[:, ::-1] if back else v
                    t = q.dve(lambda e, of=of: e.tensor_tensor_scan(of(1), of(0), of(1), NONE, ALU.add, ALU.max),
                              after=[t])
                if back:
                    t = q.dve(lambda e: e.tensor_copy(row[:, 2, 0:P - HEADS], row[:, 1, HEADS:P]), after=[t])
                else:
                    t = q.dve(lambda e: e.tensor_copy(row[:, 2, HEADS:P], row[:, 1, 0:P - HEADS]), after=[t])
                t = self.transpose_to(carry[:, 3:4], row[:, 2, :], [t])
                t = scan(carry[:, 3:4], [t], top[:, :])
            own = new
            for g in range(s.run):
                u = self.transpose_to(own[:, g * P:(g + 1) * P],
                                      loop[:, g, :, :].rearrange("p c h -> p (c h)"), [t])
            t = q.dve(lambda e: e.tensor_tensor(top[:, :], top[:, :], own[:, :], ALU.max), after=[u])
            t = q.dve(lambda e: e.tensor_tensor(a[:, :], a[:, :], top[:, :], ALU.subtract), after=[t])
            weights = q.act(lambda e: e.activation(a[:, :], a[:, :], ACT.Exp), after=[t])
            t = q.dve(lambda e: e.tensor_tensor(own[:, :], own[:, :], top[:, :], ALU.subtract), after=[t])
            u = q.act(lambda e: e.activation(own[:, :], own[:, :], ACT.Exp), after=[t])
            first = top
            t = q.dve(lambda e: e.tensor_tensor(first[:, :], dst[:, 1:n + 1], dst[:, 0:n], ALU.not_equal),
                      after=[t])
            t = q.dve(lambda e: e.tensor_tensor(own[:, :], own[:, :], first[:, :], ALU.mult), after=[t, u])
            for back_to, rows, ready in ((alpha, a, weights), (loop, own, t)):
                for g in range(s.run):
                    self.transpose_to(back_to[:, g, :, :].rearrange("p c h -> p (c h)"),
                                      rows[:, g * P:(g + 1) * P], [ready])
            q.barrier()
        self.bank_free = [None] * 8

    def weighted_sums(self, alpha, loop, acc):
        s, q, io = self.s, self.q, self.io
        n, groups = s.esteps, s.esteps // 4
        with ExitStack() as scope:
            sb = self.sb
            slots, ahead = 6, 4
            wide = D + 2 * HEADS
            rows = sb(scope, "rows", [P, slots, 4 * D])
            both = sb(scope, "both", [P, 2, 4, wide])
            hot = sb(scope, "hot", [P, 2, 4, P])
            rel = sb(scope, "rel", [P, n])
            win = sb(scope, "win", [1, n], I32)
            iota = self.load_iota(scope)
            self.load(rel[:, :], self.e_rel)
            self.load(win[:, :], self.e_regs[1:2, :])
            t = q.dve(lambda e: e.memset(acc[:, :, :], 0.0))
            self.wait_setup()
            lane = [q.lane(f"again{i}") for i in range(slots)]
            weighted, products, added, rows_in = [], [], [t], {}

            def fetch(g):
                rows_in[g] = q.dma("sync", lane[g % slots], lambda e: e.dma_start(
                    rows[:, g % slots, :], self.gathered[g, :, :]),
                    after=[weighted[g - slots]] if g >= slots else ())
            for g in range(ahead):
                fetch(g)

            def add(g):
                for k in range(4):
                    v = 4 * g + k
                    ps = self.bank[v % 8][:, 0:wide]

                    def put(e, v=v, ps=ps):
                        b = e.value_load(win[0:1, v:v + 1], min_val=0, max_val=s.nb - 1)
                        at = acc[:, bass.ds(b, 1), :].rearrange("p o f -> p (o f)")
                        return e.tensor_tensor(at, at, ps, ALU.add)
                    added.append(q.dve(put, after=[products[v], added[-1]]))

            for g in range(groups):
                two = g % 2
                old = products[4 * (g - 2) + 3] if g >= 2 else None
                w = self.places(alpha, g)
                q.act(lambda e, two=two, w=w: e.activation(both[:, two, :, D:D + HEADS], w, ACT.Copy), after=[old])
                w = self.places(loop, g)
                q.act(lambda e, two=two, w=w: e.activation(both[:, two, :, D + HEADS:], w, ACT.Copy))
                for k in range(4):
                    hots = q.pool(lambda e, two=two, g=g, k=k: e.tensor_scalar(
                        hot[:, two, k, :], iota[:, :], rel[:, 4 * g + k:4 * g + k + 1], None, ALU.is_equal),
                        after=[old])
                weighted.append(q.dve(lambda e, two=two, g=g: e.tensor_tensor(
                    both[:, two, :, 0:D].rearrange("p v (h c) -> p v h c", c=CH),
                    rows[:, g % slots, :].rearrange("p (v h c) -> p v h c", h=HEADS, c=CH),
                    self.places(alpha, g).rearrange("p v (h o) -> p v h o", o=1)
                    .to_broadcast([P, 4, HEADS, CH]), ALU.mult), after=[rows_in[g], old]))
                for k in range(4):
                    v = 4 * g + k
                    products.append(q.pe(lambda e, two=two, k=k, v=v: e.matmul(
                        self.bank[v % 8][:, 0:wide], hot[:, two, k, :], both[:, two, k, :],
                        start=True, stop=True),
                        after=[weighted[g], hots, self.last_act(), added[v - 8 + 1] if v >= 8 else None]))
                if g >= 1:
                    add(g - 1)
                if g + ahead < groups:
                    fetch(g + ahead)
            add(groups - 1)
            q.barrier()

    def feed_forward(self, x, h, acc):
        s, q, io = self.s, self.q, self.io
        with ExitStack() as scope:
            sb = self.sb
            rows = sb(scope, "rows2", [P, 2, D])
            w1 = sb(scope, "w1", [P, 2 * D])
            w2 = sb(scope, "w2f", [P, 2, D])
            cols = sb(scope, "cols4", [P, 4])
            den = sb(scope, "den", [P, s.nb, HEADS])
            ut = sb(scope, "ut2", [P, s.nb * P])
            mid = sb(scope, "mid4", [P, 2, s.nb * P])
            own_xl = ut[:, :].rearrange("p (b f) -> p b f", f=D)
            full = (s.nb - 1) * P
            t = q.dve(lambda e: e.memset(own_xl[:, s.nb - 1, :], 0.0))
            self.load(own_xl[:, 0:s.nb - 1, :], self.xl[0:full, :].rearrange("(b l) f -> l b f", l=P))
            self.load(own_xl[0:s.last, s.nb - 1, :], self.xl[full:s.n, :], after=[t])
            self.load(rows[:, 0, :], io["L3_gnn_bias"].partition_broadcast(P))
            self.load(rows[:, 1, :], io["L3_gnn_b2"].partition_broadcast(P))
            self.load(w1[:, :], io["L3_gnn_W1"])
            self.load(w2[:, :, :], io["L3_gnn_W2"].rearrange("(j k) f -> k j f", k=P))
            self.load(cols[:, 0:1], self.column("L3_gnn_ln2_g"))
            self.load(cols[:, 1:2], self.column("L3_gnn_ln2_b"))
            self.load(cols[:, 2:4], io["L3_gnn_b1_t"])
            self.wait_setup()
            weights, own = acc[:, :, D:D + HEADS], acc[:, :, D + HEADS:]
            t = q.dve(lambda e: e.tensor_scalar(den[:, :, :], weights, 0.0, None, ALU.is_equal))
            t = q.dve(lambda e: e.tensor_tensor(own, own, den[:, :, :], ALU.add), after=[t])
            t = q.dve(lambda e: e.tensor_tensor(den[:, :, :], weights, own, ALU.add), after=[t])
            t = q.dve(lambda e: e.tensor_scalar(den[:, :, :], den[:, :, :], DENOM_EPS, None, ALU.add), after=[t])
            t = q.dve(lambda e: e.reciprocal(den[:, :, :], den[:, :, :]), after=[t])

            def per_head(m):
                return m.rearrange("p b (h o) -> p b h o", o=1).to_broadcast([P, s.nb, HEADS, CH])
            sums = acc[:, :, 0:D].rearrange("p b (h c) -> p b h c", c=CH)
            own_rows = ut[:, :].rearrange("p (b h c) -> p b h c", h=HEADS, c=CH)
            u = q.dve(lambda e: e.tensor_tensor(own_rows, own_rows, per_head(own), ALU.mult), after=[t])
            u = q.dve(lambda e: e.tensor_tensor(sums, sums, own_rows, ALU.add), after=[u])
            u = q.dve(lambda e: e.tensor_tensor(sums, sums, per_head(den[:, :, :]), ALU.mult), after=[u])
            u = q.dve(lambda e: e.tensor_tensor(h[:, :, :], h[:, :, :], acc[:, :, 0:D], ALU.add), after=[u])
            u = q.dve(lambda e: e.tensor_tensor(
                h[:, :, :], h[:, :, :], rows[:, 0:1, :].to_broadcast([P, s.nb, D]), ALU.add), after=[u])
            t = self.ln_affine_t(scope, ut, h, cols[:, 0:1], cols[:, 1:2], [u])
            u = q.dve(lambda e: e.tensor_tensor(x[:, :, :], x[:, :, :], h[:, :, :], ALU.add))
            u = q.dve(lambda e: e.tensor_tensor(
                x[:, :, :], x[:, :, :], rows[:, 1:2, :].to_broadcast([P, s.nb, D]), ALU.add), after=[u])
            wide = 400
            assert wide * 8 == s.nb * P
            mids = []
            for c in range(8):
                for j in range(2):
                    i = self.next_bank()
                    ps = self.bank[i][:, 0:wide]
                    tk = q.pe(lambda e, c=c, j=j, ps=ps: e.matmul(
                        ps, w1[:, j * D:(j + 1) * D], ut[:, c * wide:(c + 1) * wide], start=True, stop=True),
                        after=[t, self.bank_free[i]])
                    m = self.bank_free[i] = q.act(lambda e, c=c, j=j, ps=ps: e.activation(
                        mid[:, j, c * wide:(c + 1) * wide], ps, ACT.Gelu, bias=cols[:, 2 + j:3 + j]), after=[tk])
                mids.append(m)
            for b in range(s.nb):
                i = self.next_bank()
                ps = self.bank[i][:, 0:D]
                for j in range(2):
                    tk = q.pe(lambda e, b=b, j=j, ps=ps: e.matmul(
                        ps, mid[:, j, b * P:(b + 1) * P], w2[:, j, :], start=j == 0, stop=j == 1),
                        after=[mids[min(7, ((b + 1) * P - 1) // wide)], self.bank_free[i]])
                done = self.bank_free[i] = q.dve(lambda e, b=b, ps=ps: e.tensor_tensor(
                    x[:, b, :], x[:, b, :], ps, ALU.add), after=[tk, u])
            self.store_nodes(x, done)

    def store_nodes(self, x, after):
        s, q = self.s, self.q
        lane = q.lane("output")
        full = (s.nb - 1) * P
        q.dma("sync", lane, lambda e: e.dma_start(
            self.out[0:full, :].rearrange("(b l) f -> l b f", l=P), x[:, 0:s.nb - 1, :]), after=[after])
        end = q.dma("sync", lane, lambda e: e.dma_start(self.out[full:s.n, :], x[0:s.last, s.nb - 1, :]))
        q.wait("sync", [end])

    def build(self, stop=9):
        s, q, ctx, io = self.s, self.q, self.ctx, self.io
        self.constants()
        with ExitStack() as scope:
            self.dlast = self.sb(scope, "dlast", [P, s.tiles], I32)
            self.tile_no = self.sb(scope, "tile_no", [P, s.tiles])
            self.load(self.dlast[:, :], io["dst_last"].partition_broadcast(P))
            self.load(self.tile_no[:, :], io["c_tile_no"].partition_broadcast(P))
            self.wait_setup()
            self.edge_tables()
            self.count_tables()
        x = self.sb(ctx, "x", [P, s.nb, D])
        with ExitStack() as scope:
            counts = self.sb(scope, "counts", [P, s.nb, s.nc], F16)
            self.count_matrix(counts)
            self.layer0(x)
            rdeg = self.sb(scope, "rdeg", [P, s.nb])
            if stop >= 1:
                self.layer1(x, rdeg)
            if stop >= 2:
                self.layer2(x, rdeg)
            q.barrier()
        if stop >= 3:
            self.layer3(x)
        else:
            self.store_nodes(x, self.last_dve())
        q.barrier()
        q.emit()


def gnn_program(nc, n_nodes, n_edges, io, out, stop=9):
    with ExitStack() as ctx:
        Kernel(nc, ctx, Shapes(n_nodes, n_edges), io, out).build(stop)


STOP = 9


def layouts(inputs):
    import numpy as np

    s = Shapes(inputs["x"].shape[0], inputs["dst"].shape[0])
    a = {k: np.ascontiguousarray(v) for k, v in inputs.items()}
    src, dst, edge = a.pop("src"), a.pop("dst"), a.pop("edge_attr_32")
    room = (s.tiles + 1) * P - dst.shape[0]
    dst = np.concatenate([dst, np.full(room, s.pad_dst, dst.dtype)]).reshape(s.tiles + 1, P)
    a["dst_rows"] = dst
    a["dst_last"] = np.ascontiguousarray(dst[:s.tiles, P - 1])
    a["src_rows"] = np.concatenate([src, np.zeros(room, src.dtype)]).reshape(s.tiles + 1, P)
    room = s.rows4 * 4 * P - edge.shape[0]
    edge = np.concatenate([edge, np.zeros((room, DE), edge.dtype)]).reshape(s.rows4 * 4, P, DE)
    a["edge_t"] = np.ascontiguousarray(edge.transpose(0, 2, 1))
    for name in ("L0_gnn_W_ih", "L0_gnn_W_hh", "L2_gnn_W1", "L2_gnn_W2", "L2_gnn_W_self"):
        a[name + "_t"] = np.ascontiguousarray(a.pop(name).T)
    for name in ("L0_gnn_b_ih", "L0_gnn_b_hh"):
        a[name + "_t"] = np.ascontiguousarray(a.pop(name).reshape(3, D).T)
    a["L3_gnn_b1_t"] = np.ascontiguousarray(a.pop("L3_gnn_b1").reshape(2, D).T)
    a["att_row"] = a.pop("L3_gnn_att").reshape(D)
    far = np.arange(s.nb)[:, None] * FAR + np.arange(s.w)
    a["c_ident"] = np.eye(P, dtype=np.float32)
    a["c_iota"] = np.arange(P, dtype=np.float32)
    a["c_far"] = far.reshape(-1).astype(np.float32)
    a["c_tile_no"] = np.arange(s.tiles, dtype=np.float32)
    a["c_step"] = np.ascontiguousarray(np.arange(16 * P, dtype=np.float32).reshape(16, P).T)
    return a


def kernel(**inputs):
    import concourse.bacc as bacc
    from concourse.bass_utils import run_bass_kernel_spmd

    arrays = layouts(inputs)
    n_nodes, n_edges = inputs["x"].shape[0], inputs["dst"].shape[0]
    nc = bacc.Bacc("TRN2", target_bir_lowering=False, num_devices=1)
    io = {name: nc.dram_tensor(name, a.shape, mybir.dt.from_np(a.dtype), kind="ExternalInput").ap()
          for name, a in arrays.items()}
    out = nc.dram_tensor("out", (n_nodes, D), F32, kind="ExternalOutput").ap()
    gnn_program(nc, n_nodes, n_edges, io, out, STOP)
    r = run_bass_kernel_spmd(nc, [arrays], core_ids=[0])
    return r.results[0]["out"]
```

```python
from contextlib import ExitStack

import concourse.bass as bass
from concourse import mybir

F32 = mybir.dt.float32
F16 = mybir.dt.float16
I32 = mybir.dt.int32
I16 = mybir.dt.int16
ALU = mybir.AluOpType
ACT = mybir.ActivationFunctionType
AX = mybir.AxisListType

P = 128
D = 128
HEADS = 8
CH = D // HEADS
DE = 32
NEG_SLOPE = 0.2
EPS = 1e-5
DENOM_EPS = 1e-16
NONE = -3.0e38
BANKS = 8
CLEAR = 3
F16_SCALE = 4096.0


class Shapes:
    def __init__(self, n_nodes, n_edges):
        self.n = n_nodes
        self.nb = -(-n_nodes // P)
        self.last = n_nodes - (self.nb - 1) * P
        self.edges = n_edges
        self.tiles = -(-n_edges // P)
        self.quads = -(-self.tiles // 4)
        self.w = 8
        self.windows = -(-n_nodes // self.w)
        self.nc = self.windows * self.w
        self.pad_dst = self.nc - 1
        assert self.pad_dst >= n_nodes
        self.csteps = self.tiles + self.windows - 1
        self.groups = self.quads + self.nb - 1
        self.run = -(-self.groups // 16)
        self.padded = 16 * self.run

    def rows(self, b):
        return P if b < self.nb - 1 else self.last


class Core:

    ENGINES = ("tensor", "vector", "scalar", "gpsimd", "sync")

    def __init__(self, nc, ctx):
        self.nc = nc
        self.queue = {e: [] for e in self.ENGINES}
        self.sem = {e: ctx.enter_context(nc.semaphore(f"{e}_done")) for e in self.ENGINES}
        self.count = {e: 0 for e in self.ENGINES}
        self.waited = {e: {} for e in self.ENGINES}
        self.ctx = ctx

    def lane(self, name):
        self.sem[name] = self.ctx.enter_context(self.nc.semaphore(name))
        self.count[name] = 0
        return name

    def wait(self, engine, after):
        for token in after:
            if token is None:
                continue
            name, value = token
            if value > self.waited[engine].get(name, 0):
                self.waited[engine][name] = value
                sem = self.sem[name]
                self.queue[engine].append(lambda e, sem=sem, value=value: e.wait_ge(sem, value))

    def on(self, engine, make, after=(), late=None):
        self.wait(engine, after)
        sem = self.sem[engine]
        if late is None:
            self.queue[engine].append(lambda e: make(e).then_inc(sem, 1))
        else:
            name, value = late
            self.waited[engine][name] = max(value, self.waited[engine].get(name, 0))
            self.queue[engine].append(lambda e, of=self.sem[name]: make(e)._wait_ge(of, value).then_inc(sem, 1))
        self.count[engine] += 1
        return engine, self.count[engine]

    def dma(self, engine, lane, make, after=()):
        self.wait(engine, after)
        sem = self.sem[lane]
        self.queue[engine].append(lambda e: make(e).then_inc(sem, 16))
        self.count[lane] += 16
        return lane, self.count[lane]

    def step(self, engine, do, after=()):
        self.wait(engine, after)
        self.queue[engine].append(do)

    def pe(self, make, after=()):
        return self.on("tensor", make, after)

    def dve(self, make, after=()):
        return self.on("vector", make, after)

    def act(self, make, after=(), late=None):
        return self.on("scalar", make, after, late)

    def pool(self, make, after=()):
        return self.on("gpsimd", make, after)

    def barrier(self):
        everything = [(name, value) for name, value in self.count.items() if value]
        for e in self.ENGINES:
            self.wait(e, everything)

    def emit(self):
        with self.nc.Block() as block:
            for name in self.ENGINES:
                def run(e, name=name):
                    for make in self.queue[name]:
                        make(e)
                {"tensor": block.tensor, "vector": block.vector, "scalar": block.scalar,
                 "gpsimd": block.gpsimd, "sync": block.sync}[name](run)


class Registers:

    def __init__(self, nc, q, engine, row, n, top, after, at_once=8):
        self.at_once = at_once
        self.nc, self.q, self.engine, self.row, self.n, self.top = nc, q, engine, row, n, top
        self.engine_type = {"tensor": mybir.EngineType.PE, "vector": mybir.EngineType.DVE,
                            "scalar": mybir.EngineType.Activation, "sync": mybir.EngineType.SP}[engine]
        self.values = {}
        self.after = after
        self.fill(0)

    def fill(self, i):
        if i >= self.n:
            return
        hi = min(self.n, i + self.at_once)

        def load(e):
            _, values = self.nc.values_load_multi_w_load_instructions(
                self.row[:, i:hi], engines=[self.engine_type], min_val=0, max_val=self.top,
                skip_runtime_bounds_check_because="the tables are clamped to this range on the chip")
            self.values.update(zip(range(i, hi), values))
        self.q.step(self.engine, load, self.after)

    def prefetch(self, i):
        if i % self.at_once == 0:
            self.fill(i + self.at_once)

    def at(self, i):
        return self.values.pop(i)


class Kernel:
    def __init__(self, nc, ctx, s, io, out):
        self.nc, self.ctx, self.s, self.io, self.out = nc, ctx, s, io, out
        self.q = Core(nc, ctx)
        self.psum = ctx.enter_context(nc.psum_tensor("psum", [P, 8, 512], F32))
        self.bank = [self.psum[:, i, :] for i in range(8)]
        self.bank_free = [None] * 8
        self.turn = 0
        self.setup = self.q.lane("setup_loads")
        self.names = 0

    def sb(self, scope, name, shape, dt=F32):
        self.names += 1
        return scope.enter_context(self.nc.sbuf_tensor(f"{name}_{self.names}", shape, dt))

    def dram(self, name, shape, dt=F32):
        return self.nc.dram_tensor(name, shape, dt, kind="Internal").ap()

    def load(self, dst, src, after=()):
        self.q.dma("sync", self.setup, lambda e: e.dma_start(dst, src), after)

    def loaded(self):
        return self.setup, self.q.count[self.setup]

    def next_bank(self):
        self.turn = (self.turn + 1) % 8
        return self.turn

    def transpose_to(self, dst, src, after, copy=None):
        q, i = self.q, self.next_bank()
        k, m = src.free_size(), src.shape[0]
        ps = self.bank[i][0:k, 0:m]
        t = q.pe(lambda e: e.transpose(ps, src, self.ident[0:m, 0:m]), after=list(after) + [self.bank_free[i]])
        if copy is None:
            t = q.dve(lambda e: e.tensor_copy(dst, ps), after=[t])
        else:
            t = copy(ps, t)
        self.bank_free[i] = t
        return t

    def row_of(self, dst, column, after):
        q, i = self.q, self.next_bank()
        ps = self.bank[i][:, 0:P]
        t = q.pe(lambda e: e.matmul(ps, column.to_broadcast([P, P]), self.ident[:, :], start=True, stop=True),
                 after=list(after) + [self.bank_free[i]])
        t = q.dve(lambda e: e.tensor_copy(dst, ps), after=[t])
        self.bank_free[i] = t
        return t

    def constants(self):
        ctx, io, q = self.ctx, self.io, self.q
        self.ident = self.sb(ctx, "ident", [P, P])
        self.eps = self.sb(ctx, "eps", [P, 1])
        self.edge_sum = self.sb(ctx, "edge_sum", [P, 1])
        self.load(self.ident[:, :], io["c_ident"])
        q.dve(lambda e: e.memset(self.eps[:, :], EPS))

    def load_iota(self, scope):
        iota = self.sb(scope, "iota", [P, P])
        self.load(iota[:, :], self.io["c_iota"].partition_broadcast(P))
        return iota

    def path(self, scope, name, last, src_table, dst_table, shift, windows, nsteps):
        s, q, io = self.s, self.q, self.io
        tiles, width = last.shape[0], src_table.shape[1]
        nch = -(-nsteps // P)
        sb = self.sb
        ends = sb(scope, name + "_ends", [P, tiles])
        tile_no = sb(scope, name + "_tile_no", [P, tiles])
        win = sb(scope, name + "_win", [P, tiles], I32)
        junk = sb(scope, name + "_junk", [P, tiles])
        step = sb(scope, name + "_step", [P, nch])
        before = sb(scope, name + "_before", [P, nch])
        tile = sb(scope, name + "_tile", [P, nch])
        tile_prev = sb(scope, name + "_tile_prev", [P, nch])
        window = sb(scope, name + "_window", [P, nch])
        keep = sb(scope, name + "_keep", [P, nch])
        index = sb(scope, name + "_index", [P, nch], I32)
        self.load(win[:, :], last.partition_broadcast(P))
        self.load(tile_no[:, :], io["c_tile_no"][0:tiles].partition_broadcast(P))
        self.load(step[:, :], io["c_step"][:, 0:nch])
        t = q.dve(lambda e: e.tensor_scalar(win[:, :], win[:, :], shift, None,
                                            ALU.logical_shift_right), after=[self.loaded()])
        t = q.dve(lambda e: e.tensor_copy(ends[:, :], win[:, :]), after=[t])
        t = q.dve(lambda e: e.tensor_tensor(ends[:, :], ends[:, :], tile_no[:, :], ALU.add), after=[t])
        t = q.dve(lambda e: e.tensor_scalar(before[:, :], step[:, :], -1.0, None, ALU.add), after=[t])
        for c in range(nch):
            for at, to in ((step, tile), (before, tile_prev)):
                t = q.dve(lambda e, c=c, at=at, to=to: e.tensor_scalar(
                    junk[:, :], ends[:, :], at[:, c:c + 1], None, ALU.is_lt, ALU.add,
                    accum_out=to[:, c:c + 1]), after=[t])
        have = q.dve(lambda e: e.tensor_copy(index[:, :], tile[:, :]), after=[t])
        t = q.dve(lambda e: e.tensor_tensor(window[:, :], step[:, :], tile[:, :], ALU.subtract))
        t = q.dve(lambda e: e.tensor_tensor(tile_prev[:, :], before[:, :], tile_prev[:, :], ALU.subtract),
                  after=[t])
        t = q.dve(lambda e: e.tensor_scalar(window[:, :], window[:, :], float(windows - 1), 0.0,
                                            ALU.min, ALU.max), after=[t])
        done = q.dve(lambda e: e.tensor_tensor(keep[:, :], window[:, :], tile_prev[:, :], ALU.is_equal),
                     after=[t])
        src = sb(scope, name + "_src", [P, nch, width], I32)
        dst = sb(scope, name + "_dst", [P, nch, width], I32)
        lane = q.lane(name + "_edge_rows")
        for c in range(nch):
            for to, table in ((src, src_table), (dst, dst_table)):
                got = q.dma("gpsimd", lane, lambda e, c=c, to=to, table=table: e.indirect_dma_start(
                    to[:, c, :], None, table, bass.IndirectOffsetOnAxis(ap=index[:, c:c + 1], axis=0)),
                    after=[have])
        q.wait("vector", [done])
        return nch, tile, window, keep, src, dst, got

    def edge_tables(self):
        s, q, io = self.s, self.q, self.io
        n, m = s.padded, s.padded * 4 * P
        self.e_src = self.dram("e_src", (P, 4 * n), I32)
        self.e_rel = self.dram("e_rel", (P, 4 * n))
        self.e_rel_rows = self.dram("e_rel_rows", (n, 4 * P), I16)
        self.e_dst_flat = self.dram("e_dst_flat", (m + 2,))
        self.e_new = [self.dram("e_new_before", (m,)), self.dram("e_new_behind", (m,))]
        self.e_regs = self.dram("e_regs", (2, n), I32)
        self.e_lane = q.lane("edge_tables")
        self.new_lane = q.lane("edge_new")
        with ExitStack() as scope:
            sb = self.sb
            nch, tile, window, keep, src, dst, got = self.path(
                scope, "e", io["dst_quad_last"], io["src_quads"], io["dst_quads"], 7, s.nb, n)
            wide = 4 * P
            rel = sb(scope, "rel", [P, nch, wide])
            dstf = sb(scope, "dstf", [P, nch, wide])
            rel16 = sb(scope, "rel16", [P, nch, wide], I16)
            srcf = sb(scope, "srcf", [P, nch, wide])
            first = sb(scope, "first", [P, nch])
            srct = sb(scope, "srct", [P, nch * P, 4], I32)
            relt = sb(scope, "relt", [P, nch * P, 4])
            rowf = sb(scope, "rowf", [P, 2, nch * P], I32)
            guard = sb(scope, "guard", [1, 1])
            cuts = 8
            share = -(-s.quads // cuts)
            part = sb(scope, "edge_part", [P, 2, share, P])
            sums = sb(scope, "edge_sums", [P, cuts])
            lanes = [q.lane(f"edge_part{i}") for i in range(2)]
            by_row = io["edge_t"].rearrange("i r e -> r i e")
            done = []
            for c in range(cuts):
                lo, hi = c * share, min((c + 1) * share, s.quads)
                piece = part[:, c % 2, 0:hi - lo, :]
                t = q.dma("sync", lanes[c % 2], lambda e, piece=piece, lo=lo, hi=hi: e.dma_start(
                    piece, by_row[:, lo:hi, :]), after=[done[c - 2]] if c >= 2 else ())
                done.append(q.act(lambda e, piece=piece, c=c: e.activation(
                    piece, piece, ACT.Copy, accum_out=sums[:, c:c + 1]), after=[t]))
            q.dve(lambda e: e.tensor_reduce(self.edge_sum[:, :], sums[:, :], AX.X, ALU.add), after=[done[-1]])
            a = q.dve(lambda e: e.memset(guard[:, :], -1.0))
            b = q.dve(lambda e: e.tensor_scalar(first[:, :], window[:, :], float(P), None, ALU.mult), after=[a])
            b = q.dve(lambda e: e.tensor_copy(dstf[:, :, :], dst[:, :, :]), after=[got, b])
            t = q.dve(lambda e: e.tensor_copy(srcf[:, :, :], src[:, :, :]))
            flat = self.e_dst_flat
            rows = [(c, min(P, n - c * P)) for c in range(nch)]

            def store(dst_, src_, after):
                return q.dma("sync", self.e_lane, lambda e: e.dma_start(dst_, src_), after=[after])
            for c, r in rows:
                store(flat[1 + c * P * wide:1 + (c * P + r) * wide].rearrange("(v e) -> v e", e=wide),
                      dstf[0:r, c, :], t)
            store(flat[0:1].rearrange("(a b) -> a b", a=1), guard[:, :], t)
            stored = store(flat[m + 1:m + 2].rearrange("(a b) -> a b", a=1), guard[:, :], t)
            per = m // P
            near = sb(scope, "near", [P, 3, per])
            new = sb(scope, "new", [P, 2, per])
            for j in range(3):
                back = q.dma("sync", self.new_lane, lambda e, j=j: e.dma_start(
                    near[:, j, :], flat[j:j + m].rearrange("(p e) -> p e", p=P)), after=[stored])
            for c in range(nch):
                t = q.dve(lambda e, c=c: e.tensor_scalar(rel[:, c, :], dstf[:, c, :], first[:, c:c + 1], None,
                                                         ALU.subtract), after=[b])
            t = q.dve(lambda e: e.tensor_copy(rel16[:, :, :], rel[:, :, :]), after=[t])
            for c in range(nch):
                for k in range(4):
                    self.transpose_to(srct[:, c * P:(c + 1) * P, k], srcf[:, c, k * P:(k + 1) * P], [t])
                    self.transpose_to(relt[:, c * P:(c + 1) * P, k], rel[:, c, k * P:(k + 1) * P], [t])
                self.row_of(rowf[:, 0, c * P:(c + 1) * P], tile[:, c:c + 1], [t])
                t2 = self.row_of(rowf[:, 1, c * P:(c + 1) * P], window[:, c:c + 1], [t])
            store(self.e_src, srct[:, 0:n, :].rearrange("p g k -> p (g k)"), t2)
            store(self.e_rel, relt[:, 0:n, :].rearrange("p g k -> p (g k)"), t2)
            store(self.e_regs[0:1, :], rowf[0:1, 0, 0:n], t2)
            store(self.e_regs[1:2, :], rowf[0:1, 1, 0:n], t2)
            for c, r in rows:
                store(self.e_rel_rows[c * P:c * P + r, :], rel16[0:r, c, :], t2)
            for j in range(2):
                t = q.dve(lambda e, j=j: e.tensor_tensor(new[:, j, :], near[:, 1, :], near[:, 2 * j, :],
                                                         ALU.not_equal), after=[back])
                t = q.dve(lambda e, j=j: e.tensor_scalar(new[:, j, :], new[:, j, :], NONE, None, ALU.mult),
                          after=[t])
                store(self.e_new[j].rearrange("(p e) -> p e", p=P), new[:, j, :], t)
            q.barrier()

    def count_tables(self):
        s, q, io = self.s, self.q, self.io
        w = s.w
        with ExitStack() as scope:
            sb = self.sb
            nch, tile, window, keep, src, dst, got = self.path(
                scope, "c", io["dst_last"], io["src_rows"], io["dst_rows"], 3, s.windows, s.csteps)
            n = nch * P
            self.c_key_d = self.dram("c_key", (P, n))
            self.c_low_d = self.dram("c_low", (P, n))
            self.c_regs_d = self.dram("c_regs", (4, n), I32)
            self.c_lane = q.lane("count_tables")
            high = sb(scope, "high", [P, nch, P], I32)
            low = sb(scope, "low", [P, nch, P], I32)
            lowf = sb(scope, "lowf", [P, nch, P])
            key = sb(scope, "key", [P, nch, P])
            first = sb(scope, "first", [P, nch])
            dstf = sb(scope, "dstf", [P, nch, P])
            out = [sb(scope, "out", [P, n]) for _ in range(2)]
            bank = sb(scope, "bank", [P, 3, nch], I32)
            steers = sb(scope, "steers", [P, 4, nch])
            regs = sb(scope, "regs", [P, 4, n], I32)
            t = q.dve(lambda e: e.tensor_scalar(high[:, :, :], src[:, :, :], 7, None, ALU.logical_shift_right),
                      after=[got])
            q.dve(lambda e: e.tensor_scalar(low[:, :, :], src[:, :, :], P - 1, None, ALU.bitwise_and))
            q.dve(lambda e: e.tensor_copy(dstf[:, :, :], dst[:, :, :]))
            t = q.dve(lambda e: e.tensor_scalar(first[:, :], window[:, :], float(w), None, ALU.mult))
            t = q.dve(lambda e: e.tensor_copy(key[:, :, :], high[:, :, :]), after=[t])
            t = q.dve(lambda e: e.tensor_copy(lowf[:, :, :], low[:, :, :]), after=[t])
            for c in range(nch):
                t = q.dve(lambda e, c=c: e.tensor_scalar(dstf[:, c, :], dstf[:, c, :], first[:, c:c + 1], -1.0,
                                                         ALU.subtract, ALU.max), after=[t])
                t = q.dve(lambda e, c=c: e.tensor_scalar(dstf[:, c, :], dstf[:, c, :], float(w), None,
                                                         ALU.min), after=[t])
            t = q.dve(lambda e: e.scalar_tensor_tensor(key[:, :, :], key[:, :, :], float(2 * w), dstf[:, :, :],
                                                       ALU.mult, ALU.add), after=[t])
            for j, ahead in enumerate((0, CLEAR, BANKS - 1)):
                t = q.dve(lambda e, j=j, ahead=ahead: e.tensor_scalar(bank[:, j, :], window[:, :], float(ahead),
                                                                      None, ALU.add), after=[t])
            t = q.dve(lambda e: e.tensor_scalar(bank[:, :, :], bank[:, :, :], BANKS - 1, None,
                                                ALU.bitwise_and), after=[t])
            q.dve(lambda e: e.tensor_copy(steers[:, 0:3, :], bank[:, :, :]), after=[t])
            t = q.dve(lambda e: e.tensor_scalar(steers[:, 3, :], window[:, :], 0.0, float(s.windows),
                                                ALU.is_equal, ALU.mult))
            t = q.dve(lambda e: e.scalar_tensor_tensor(steers[:, 3, :], window[:, :], -1.0, steers[:, 3, :],
                                                       ALU.add, ALU.add), after=[t])
            t = q.dve(lambda e: e.tensor_scalar(steers[:, 3, :], steers[:, 3, :], float(w), None, ALU.mult),
                      after=[t])
            for c in range(nch):
                cut = slice(c * P, (c + 1) * P)
                self.transpose_to(out[0][:, cut], key[:, c, :], [t])
                self.transpose_to(out[1][:, cut], lowf[:, c, :], [t])
                for j in range(4):
                    t2 = self.row_of(regs[:, j, cut], steers[:, j, c:c + 1], [t])
            for to, what in ((self.c_key_d, out[0][:, :]), (self.c_low_d, out[1][:, :]),
                             (self.c_regs_d.rearrange("(o a) n -> o a n", o=1),
                              regs[0:1, :, :])):
                q.dma("sync", self.c_lane, lambda e, to=to, what=what: e.dma_start(to, what), after=[t2])
            q.barrier()

    def count_matrix(self, counts):
        s, q = self.s, self.q
        w = s.w
        self.counts = counts
        ring, ahead = 8, 4
        with ExitStack() as scope:
            sb = self.sb
            far32 = sb(scope, "far32", [P, s.nb * w])
            far = sb(scope, "far", [P, s.nb * w], F16)
            lows = sb(scope, "lows", [P, ring, P], F16)
            keys = sb(scope, "keys", [P, ring, s.nb * w], F16)
            none = sb(scope, "none", [P, P], F16)
            n = self.c_key_d.shape[1]
            c_key, c_low = (sb(scope, name, [P, n]) for name in ("c_key", "c_low"))
            c_regs = sb(scope, "c_regs", [1, 4, n], I32)
            iota32 = self.load_iota(scope)
            self.load(c_key[:, :], self.c_key_d)
            self.load(c_low[:, :], self.c_low_d)
            self.load(c_regs[:, :, :], self.c_regs_d.rearrange("(o a) n -> o a n", o=1))
            self.load(far32[:, :], self.io["c_far"].partition_broadcast(P))
            iota = sb(scope, "iota16", [P, P], F16)
            self.wait_setup()
            q.dve(lambda e: e.memset(none[:, :], 0.0))
            q.dve(lambda e: e.tensor_copy(far[:, :], far32[:, :]))
            ready = q.dve(lambda e: e.tensor_copy(iota[:, :], iota32[:, :]))
            q.wait("vector", [ready])
            clear = [q.pe(lambda e, i=i: e.matmul(self.bank[i][:, 0:s.nb * w], none[:, :], far[:, :],
                                                  start=True, stop=True, skip_group_check=True),
                          after=[ready]) for i in range(BANKS)]
            its_bank, cleared, whole, column = (
                Registers(self.nc, q, name, c_regs[0:1, j, :], s.csteps, top, [self.loaded()], 8)
                for j, (name, top) in enumerate((("tensor", BANKS - 1), ("tensor", BANKS - 1),
                                                 ("scalar", BANKS - 1), ("scalar", (s.windows - 1) * w))))
            mm, copies = [], []

            def bank_at(place):
                return self.psum[:, bass.ds(place, 1), 0:s.nb * w].rearrange("p o n -> p (o n)")

            def one_hots(i):
                old = mm[i - ring] if i >= ring else None
                a = q.dve(lambda e: e.tensor_scalar(lows[:, i % ring, :], iota[:, :],
                                                    c_low[:, i:i + 1], None, ALU.is_equal), after=[old])
                b = q.dve(lambda e: e.tensor_scalar(keys[:, i % ring, :], far[:, :],
                                                    c_key[:, i:i + 1], None, ALU.is_equal), after=[old])
                return a, b

            def read_out(e, place, column):
                return e.activation(self.counts[:, :, column], bank_at(place).rearrange("p (h j) -> p h j", j=w),
                                    ACT.Copy)

            hots = {i: one_hots(i) for i in range(ahead)}
            for i in range(s.csteps):
                its_bank.prefetch(i)
                cleared.prefetch(i)
                q.wait("tensor", list(hots.pop(i)) + [clear[BANKS + i - CLEAR]])
                mm.append(q.pe(lambda e, i=i: e.matmul(bank_at(its_bank.at(i)), lows[:, i % ring, :],
                                                       keys[:, i % ring, :], start=False, stop=True,
                                                       skip_group_check=True)))
                clear.append(q.pe(lambda e, i=i: e.matmul(bank_at(cleared.at(i)), none[:, :],
                                                          far[:, :], start=True, stop=True, skip_group_check=True),
                                  after=[copies[i - BANKS + 1 + CLEAR] if i >= BANKS - 1 - CLEAR else None]))
                if i + ahead < s.csteps:
                    hots[i + ahead] = one_hots(i + ahead)
                whole.prefetch(i)
                column.prefetch(i)
                copies.append(q.act(lambda e, i=i: read_out(e, whole.at(i),
                                                            bass.ds(column.at(i), w)),
                                    after=[mm[i - 1] if i else clear[BANKS - 1]],
                                    late=copies[i - 1] if i else None))
            last = s.windows - 1
            q.act(lambda e: read_out(e, last % BANKS, slice(last * w, (last + 1) * w)),
                  after=[mm[-1], copies[-1]])
            q.barrier()
        self.bank_free = [None] * 8

    def wait_setup(self):
        for e in self.q.ENGINES:
            self.q.wait(e, [self.loaded()])

    def last_dve(self):
        return "vector", self.q.count["vector"]

    def last_act(self):
        return "scalar", self.q.count["scalar"]

    def load_nodes(self, x):
        s, q = self.s, self.q
        t = q.dve(lambda e: e.memset(x[:, s.nb - 1, :], 0.0))
        full = (s.nb - 1) * P
        xin = self.io["x"]
        self.load(x[:, 0:s.nb - 1, :], xin[0:full, :].rearrange("(b l) f -> l b f", l=P))
        self.load(x[0:s.last, s.nb - 1, :], xin[full:s.n, :], after=[t])

    def ln_factors(self, scope, x, after, scale=1.0):
        s, q = self.s, self.q
        stats = self.sb(scope, "ln_stats", [P, s.nb, 6])
        mv = self.sb(scope, "ln_mv", [P, s.nb, 2])
        rstd = self.sb(scope, "ln_rstd", [P, s.nb])
        nbias = self.sb(scope, "ln_nbias", [P, s.nb])
        for b in range(s.nb):
            t = q.dve(lambda e, b=b: e.bn_stats(stats[:, b, :], x[:, b, :]), after=after)
        for b in range(s.nb):
            t = q.dve(lambda e, b=b: e.bn_aggr(mv[:, b, :], stats[:, b, :]), after=[t] if b == 0 else ())
        t = q.act(lambda e: e.activation(rstd[:, :], mv[:, :, 1], ACT.Sqrt, bias=self.eps[:, 0:1]), after=[t])
        t = q.dve(lambda e: e.reciprocal(rstd[:, :], rstd[:, :]), after=[t])
        if scale != 1.0:
            t = q.dve(lambda e: e.tensor_scalar(rstd[:, :], rstd[:, :], scale, None, ALU.mult), after=[t])
        t = q.dve(lambda e: e.scalar_tensor_tensor(nbias[:, :], mv[:, :, 0], -1.0, rstd[:, :],
                                                   ALU.mult, ALU.mult), after=[t])
        return rstd, nbias, t

    def ln_apply(self, y, x, rstd, nbias, func, after):
        q = self.q
        return [q.act(lambda e, b=b: e.activation(y[:, b, :], x[:, b, :], func, bias=nbias[:, b:b + 1],
                                                  scale=rstd[:, b:b + 1]), after=after)
                for b in range(self.s.nb)]

    def split(self, halves, y, rows, b, after):
        q = self.q
        t = q.act(lambda e: e.activation(halves[0:rows, b, 0:D], y, ACT.Copy), after=after)
        return q.dve(lambda e: e.tensor_tensor(halves[0:rows, b, D:2 * D], y, halves[0:rows, b, 0:D],
                                               ALU.subtract), after=[t])

    def hop(self, halves, ready, finish):
        s, q = self.s, self.q
        for b in range(s.nb):
            rows, i = s.rows(b), b % 8
            ps = self.bank[i][0:rows, 0:2 * D + 1]
            for k in range(s.nb):
                t = q.pe(lambda e, b=b, k=k, rows=rows, ps=ps: e.matmul(
                    ps, self.counts[:, k, b * P:b * P + rows], halves[:, k, :],
                    start=k == 0, stop=k == s.nb - 1),
                    after=[self.bank_free[i]] + list(ready) if k == 0 else ())
            self.bank_free[i] = finish(b, rows, self.bank[i], t)

    def layer0(self, x_out):
        s, q, io = self.s, self.q, self.io
        nc = s.nc
        cut = nc // 8
        assert cut * 8 == nc and cut <= 512
        with ExitStack() as scope:
            sb = self.sb
            ht = sb(scope, "ht", [P, s.nb * P])
            nodes = sb(scope, "nodes", [P, s.nb, D])
            qd = x_out[:, :, :].rearrange("p b f -> p (b f)")[:, 0:nc]
            w_msg = sb(scope, "w_msg", [P, D + 1])
            w_dst = sb(scope, "w_dst", [P, 1])
            b_msg = sb(scope, "b_msg", [P, D])
            b_att = sb(scope, "b_att", [P, 1])
            w_ih = sb(scope, "w_ih", [P, 3 * D])
            w_hh = sb(scope, "w_hh", [P, 3 * D])
            cols = sb(scope, "cols", [P, 8])
            bias = sb(scope, "bias", [P, 2])
            ps_src = sb(scope, "ps_src", [P, s.nb])
            self.load_nodes(nodes)
            for dst, src in ((w_msg[:, 0:D], io["L0_gnn_W_msg"]), (w_msg[:, D:D + 1], io["L0_gnn_W_att"][0:D, :]),
                             (w_dst[:, :], io["L0_gnn_W_att"][D:2 * D, :]),
                             (b_msg[:, :], io["L0_gnn_b_msg"].partition_broadcast(P)),
                             (b_att[:, :], io["L0_gnn_b_att"].partition_broadcast(P)),
                             (w_ih[:, :], io["L0_gnn_W_ih_t"]), (w_hh[:, :], io["L0_gnn_W_hh_t"]),
                             (cols[:, 0:3], io["L0_gnn_b_ih_t"]), (cols[:, 3:6], io["L0_gnn_b_hh_t"]),
                             (cols[:, 6:7], self.column("L0_gnn_gamma")), (cols[:, 7:8], self.column("L0_gnn_beta"))):
                self.load(dst, src)
            self.wait_setup()
            rstd, nbias, t = self.ln_factors(scope, nodes, ())
            h = self.ln_apply(nodes, nodes, rstd, nbias, ACT.Relu, [t])
            for b in range(s.nb):
                t = self.transpose_to(ht[:, b * P:(b + 1) * P], nodes[:, b, :], [h[b]])
            q.dve(lambda e: e.tensor_tensor(bias[:, :], cols[:, 0:2], cols[:, 3:5], ALU.add))
            for b in range(s.nb):
                i = self.next_bank()
                ps = self.bank[i]
                t = q.pe(lambda e, b=b, ps=ps: e.matmul(ps[:, 0:D + 1], ht[:, b * P:(b + 1) * P], w_msg[:, :],
                                                        start=True, stop=True), after=[t, self.bank_free[i]])
                q.dve(lambda e, b=b, ps=ps: e.tensor_tensor(nodes[:, b, :], ps[:, 0:D], b_msg[:, :], ALU.add),
                      after=[t])
                self.bank_free[i] = q.dve(lambda e, b=b, ps=ps: e.tensor_tensor(
                    ps_src[:, b:b + 1], ps[:, D:D + 1], b_att[:, :], ALU.add), after=[t])
            messages = self.last_dve()
            for c in range(8):
                i = self.next_bank()
                ps = self.bank[i][:, 0:cut]
                t = q.pe(lambda e, c=c, ps=ps: e.matmul(ps, w_dst[:, 0:1].to_broadcast([P, P]),
                                                        ht[:, c * cut:(c + 1) * cut], start=True, stop=True),
                         after=[self.bank_free[i]])
                qd_done = self.bank_free[i] = q.act(lambda e, c=c, ps=ps: e.activation(
                    qd[:, c * cut:(c + 1) * cut], ps, ACT.Copy), after=[t])
            with ExitStack() as inner:
                ring, parts = 3, 4
                wide = nc // parts
                att = sb(inner, "att", [P, ring, wide])
                used = [None] * ring
                n = 0
                for k in range(s.nb):
                    for c in range(parts):
                        r = n % ring
                        n += 1
                        t = q.act(lambda e, k=k, c=c, r=r: e.activation(
                            att[:, r, :], qd[:, c * wide:(c + 1) * wide], ACT.Sigmoid, bias=ps_src[:, k:k + 1]),
                            after=[messages, qd_done, used[r]])
                        t = q.dve(lambda e, k=k, c=c, r=r: e.tensor_tensor(
                            att[:, r, :], att[:, r, :], self.counts[:, k, c * wide:(c + 1) * wide], ALU.mult),
                            after=[t])
                        for j in range(2):
                            i = 2 * c + j
                            used[r] = q.pe(lambda e, k=k, i=i, j=j, r=r: e.matmul(
                                self.bank[i][:, 0:cut], nodes[:, k, :], att[:, r, j * cut:(j + 1) * cut],
                                start=k == 0, stop=k == s.nb - 1),
                                after=[t, self.bank_free[i] if k == 0 else None])
                sums = used[r]
                agg = qd
                for c in range(8):
                    last_read = ("scalar", q.count["scalar"])
                    t = q.dve(lambda e, c=c: e.tensor_copy(agg[:, c * cut:(c + 1) * cut],
                                                           self.bank[c][:, 0:cut]), after=[sums, last_read])
                    self.bank_free[c] = t
                q.barrier()
            with ExitStack() as inner:
                gate = sb(inner, "gate", [P, 2, 3, cut])
                stats = sb(inner, "stats", [P, 8, 6])
                mv = sb(inner, "mv", [P, 4])
                new = nodes[:, :, :].rearrange("p b f -> p (b f)")
                free = {}
                for c in range(8):
                    cs = slice(c * cut, (c + 1) * cut)
                    g = c % 2
                    rb, zb, nb_, hb = (self.bank[4 * g + j][:, 0:cut] for j in range(4))
                    wait = [free.get(c - 2)]
                    for ps, j in ((rb, 0), (zb, 1)):
                        q.pe(lambda e, ps=ps, j=j, cs=cs: e.matmul(ps, w_ih[:, j * D:(j + 1) * D], agg[:, cs],
                                                                   start=True, stop=False), after=wait)
                        q.pe(lambda e, ps=ps, j=j, cs=cs: e.matmul(ps, w_hh[:, j * D:(j + 1) * D], ht[:, cs],
                                                                   start=False, stop=True))
                    q.pe(lambda e, ps=nb_, cs=cs: e.matmul(ps, w_ih[:, 2 * D:], agg[:, cs], start=True, stop=True))
                    t = q.pe(lambda e, ps=hb, cs=cs: e.matmul(ps, w_hh[:, 2 * D:], ht[:, cs],
                                                              start=True, stop=True))
                    r, z, m = (gate[:, g, j, :] for j in range(3))
                    d = r
                    a = q.act(lambda e, r=r, rb=rb: e.activation(r, rb, ACT.Sigmoid, bias=bias[:, 0:1]),
                              after=[t] + wait)
                    b = q.act(lambda e, z=z, zb=zb: e.activation(z, zb, ACT.Sigmoid, bias=bias[:, 1:2]))
                    t = q.dve(lambda e, m=m, hb=hb, r=r: e.scalar_tensor_tensor(m, hb, cols[:, 5:6], r,
                                                                                ALU.add, ALU.mult), after=[a])
                    t = q.dve(lambda e, m=m, nb_=nb_: e.tensor_tensor(m, m, nb_, ALU.add), after=[t])
                    t = q.act(lambda e, m=m: e.activation(m, m, ACT.Tanh, bias=cols[:, 2:3]), after=[t])
                    t = q.dve(lambda e, m=m, d=d, cs=cs: e.tensor_tensor(d, ht[:, cs], m, ALU.subtract), after=[t])
                    t = q.dve(lambda e, d=d, z=z: e.tensor_tensor(d, d, z, ALU.mult), after=[t, b])
                    t = q.dve(lambda e, d=d, m=m, cs=cs: e.tensor_tensor(new[:, cs], d, m, ALU.add), after=[t])
                    real = min(cut, s.n - c * cut)
                    t = q.dve(lambda e, c=c, real=real: e.bn_stats(stats[:, c, :], new[:, c * cut:c * cut + real]),
                              after=[t])
                    free[c] = t
                t = q.dve(lambda e: e.bn_aggr(mv[:, 0:2], stats[:, :, :].rearrange("p a b -> p (a b)")), after=[t])
                t = q.act(lambda e: e.activation(mv[:, 2:3], mv[:, 1:2], ACT.Sqrt, bias=self.eps[:, 0:1]), after=[t])
                t = q.dve(lambda e: e.reciprocal(mv[:, 2:3], mv[:, 2:3]), after=[t])
                t = q.dve(lambda e: e.tensor_tensor(mv[:, 2:3], mv[:, 2:3], cols[:, 6:7], ALU.mult), after=[t])
                t = q.dve(lambda e: e.scalar_tensor_tensor(mv[:, 3:4], mv[:, 0:1], -1.0, mv[:, 2:3],
                                                           ALU.mult, ALU.mult), after=[t])
                t = q.dve(lambda e: e.tensor_tensor(mv[:, 3:4], mv[:, 3:4], cols[:, 7:8], ALU.add), after=[t])
                for c in range(8):
                    cs = slice(c * cut, (c + 1) * cut)
                    t = q.act(lambda e, cs=cs: e.activation(new[:, cs], new[:, cs], ACT.Identity,
                                                            bias=mv[:, 3:4], scale=mv[:, 2:3]), after=[t])
                q.barrier()
            self.bank_free = [None] * 8
            self.add_transposed(x_out, new, ht, t)
            q.barrier()

    def add_transposed(self, x_out, yt, xbuf, after):
        s, q = self.s, self.q
        xs = xbuf[:, :].rearrange("p (b f) -> p b f", f=D)
        self.load_nodes(xs)
        t = q.dve(lambda e: e.memset(x_out[:, s.nb - 1, :], 0.0))
        for b in range(s.nb):
            rows = s.rows(b)
            self.transpose_to(None, yt[:, b * P:b * P + rows], [after], copy=lambda ps, tk, b=b, rows=rows: q.dve(
                lambda e: e.tensor_tensor(x_out[0:rows, b, :], ps, xs[0:rows, b, :], ALU.add),
                after=[tk, t, self.loaded()]))

    def column(self, name):
        return self.io[name].rearrange("(a b) -> a b", b=1)

    def degree(self, rdeg, b, rows, ps, token):
        q = self.q
        t = q.dve(lambda e: e.tensor_scalar(rdeg[0:rows, b:b + 1], ps[0:rows, 2 * D:2 * D + 1], 1.0, F16_SCALE,
                                            ALU.max, ALU.mult), after=[token])
        return q.dve(lambda e: e.reciprocal(rdeg[0:rows, b:b + 1], rdeg[0:rows, b:b + 1]), after=[t])

    def mean_rows(self, y, ps, rdeg, b, rows, token, tmp):
        q = self.q
        t = q.act(lambda e: e.activation(tmp, ps[0:rows, D:2 * D], ACT.Copy, scale=rdeg[0:rows, b:b + 1]),
                  after=[token])
        return q.dve(lambda e: e.scalar_tensor_tensor(y, ps[0:rows, 0:D], rdeg[0:rows, b:b + 1], tmp,
                                                      ALU.mult, ALU.add), after=[t])

    def halves_of_ln(self, scope, x, halves, hs):
        s, q = self.s, self.q
        rstd, nbias, t = self.ln_factors(scope, x, [self.last_dve()], F16_SCALE)
        h = self.ln_apply(hs, x, rstd, nbias, ACT.Relu, [t])
        for b in range(s.nb):
            t = self.split(halves, hs[:, b, :], P, b, [h[b]])
        t = q.dve(lambda e: e.memset(halves[:, :, 2 * D:2 * D + 1], 1.0))
        return t

    def layer1(self, x, rdeg):
        s, q = self.s, self.q
        with ExitStack() as scope:
            sb = self.sb
            halves = [sb(scope, "halves", [P, s.nb, 2 * D + 1], F16) for _ in range(2)]
            with ExitStack() as inner:
                hs = sb(inner, "hs", [P, s.nb, D])
                ready = self.halves_of_ln(inner, x, halves[0], hs)
                q.dve(lambda e: e.memset(halves[1][:, :, :], 0.0))
                q.barrier()
            tmp = sb(scope, "tmp", [P, 4, 2, D])
            free = [None] * 4
            for n in range(3):
                a, out = halves[n % 2], halves[(n + 1) % 2]

                def finish(b, rows, ps, token, n=n, out=out):
                    k = b % 4
                    if n == 0:
                        token = self.degree(rdeg, b, rows, ps, token)
                    t0, t1 = tmp[0:rows, k, 0, :], tmp[0:rows, k, 1, :]
                    q.wait("scalar", [free[k]])
                    t = self.mean_rows(t1, ps, rdeg, b, rows, token, t0)
                    if n < 2:
                        u = q.dve(lambda e: e.tensor_scalar(t1, t1, F16_SCALE, None, ALU.mult), after=[t])
                        free[k] = self.split(out, t1, rows, b, [u])
                    else:
                        free[k] = q.dve(lambda e: e.tensor_tensor(x[0:rows, b, :], x[0:rows, b, :], t1, ALU.add),
                                        after=[t])
                    return t
                self.hop(a, [ready], finish)
                ready = self.last_dve()
            q.barrier()
            self.bank_free = [None] * 8

    def layer2(self, x, rdeg):
        s, q, io = self.s, self.q, self.io
        cut = s.nc // 8
        with ExitStack() as scope:
            sb = self.sb
            ht = sb(scope, "ht2", [P, s.nb * P])
            mt = sb(scope, "mt", [P, s.nb * P])
            cols = sb(scope, "cols2", [P, 9])
            fac = sb(scope, "fac", [P, 2, 2])
            names = ["gamma1", "beta1", "rm1", "rv1", "gamma2", "beta2", "rm2", "rv2", "b_self"]
            for j, name in enumerate(names):
                self.load(cols[:, j:j + 1], self.column("L2_gnn_" + name))
            self.wait_setup()
            for j in range(2):
                g, b, m, v = (cols[:, 4 * j + i:4 * j + i + 1] for i in range(4))
                f, sh = fac[:, j, 0:1], fac[:, j, 1:2]
                t = q.act(lambda e, f=f, v=v: e.activation(f, v, ACT.Sqrt, bias=self.eps[:, 0:1]))
                t = q.dve(lambda e, f=f: e.reciprocal(f, f), after=[t])
                t = q.dve(lambda e, f=f, g=g: e.tensor_tensor(f, f, g, ALU.mult), after=[t])
                t = q.dve(lambda e, f=f, m=m, sh=sh: e.scalar_tensor_tensor(sh, m, -1.0, f, ALU.mult, ALU.mult),
                          after=[t])
                t = q.dve(lambda e, b=b, sh=sh: e.tensor_tensor(sh, sh, b, ALU.add), after=[t])
            t = q.dve(lambda e: e.tensor_tensor(fac[:, 1, 1:2], fac[:, 1, 1:2], cols[:, 8:9], ALU.add), after=[t])
            with ExitStack() as inner:
                halves = sb(inner, "halves", [P, s.nb, 2 * D + 1], F16)
                hs = mt[:, :].rearrange("p (b f) -> p b f", f=D)
                ready = self.halves_of_ln(inner, x, halves, hs)
                for b in range(s.nb):
                    t = self.transpose_to(ht[:, b * P:(b + 1) * P], hs[:, b, :], [ready])
                q.barrier()
                tmp = sb(inner, "tmp", [P, 2, 2, D])
                free = [None] * 2

                def finish(b, rows, ps, token):
                    k = b % 2
                    t0, t1 = tmp[0:rows, k, 0, :], tmp[0:rows, k, 1, :]
                    q.wait("scalar", [free[k]])
                    t = self.mean_rows(t1, ps, rdeg, b, rows, token, t0)
                    pend.append((b, rows, k, t1, t))
                    if len(pend) > 1:
                        flush()
                    return t

                def flush():
                    b, rows, k, t1, t = pend.pop(0)
                    ps = self.bank[b % 8][:, 384:384 + rows]
                    t = q.pe(lambda e: e.transpose(ps, t1, self.ident[0:rows, 0:rows]), after=[t])
                    t = q.dve(lambda e: e.tensor_copy(mt[:, b * P:b * P + rows], ps), after=[t])
                    free[k] = self.bank_free[b % 8] = t
                pend = []
                self.hop(halves, [ready], finish)
                flush()
                q.dve(lambda e: e.memset(mt[:, s.n:], 0.0))
                q.barrier()
            with ExitStack() as inner:
                mid = sb(inner, "mid", [P, 2, 2, cut])
                w = sb(inner, "w2", [P, 3, D])
                for j, name in enumerate(("W1", "W2", "W_self")):
                    self.load(w[:, j, :], io[f"L2_gnn_{name}_t"])
                self.wait_setup()
                free = {}
                for c in range(8):
                    cs, g = slice(c * cut, (c + 1) * cut), c % 2
                    p1, p2, p3 = (self.bank[4 * g + j][:, 0:cut] for j in range(3))
                    wait = [free.get(c - 2)]
                    t = q.pe(lambda e, p=p1, cs=cs: e.matmul(p, w[:, 0, :], mt[:, cs], start=True, stop=True),
                             after=wait)
                    u = q.pe(lambda e, p=p3, cs=cs: e.matmul(p, w[:, 2, :], ht[:, cs], start=True, stop=True))
                    t = q.act(lambda e, g=g, p=p1: e.activation(mid[:, g, 0, :], p, ACT.Relu, bias=fac[:, 0, 1:2],
                                                                scale=fac[:, 0, 0:1]), after=[t] + wait)
                    v = q.act(lambda e, g=g, p=p3: e.activation(mid[:, g, 1, :], p, ACT.Identity,
                                                                bias=fac[:, 1, 1:2], scale=1.0 / F16_SCALE),
                              after=[u])
                    t = q.pe(lambda e, g=g, p=p2: e.matmul(p, w[:, 1, :], mid[:, g, 0, :], start=True, stop=True),
                             after=[t])
                    free[c] = t = q.dve(lambda e, g=g, p=p2, cs=cs: e.scalar_tensor_tensor(
                        mt[:, cs], p, fac[:, 1, 0:1], mid[:, g, 1, :], ALU.mult, ALU.add), after=[t, v])
                q.barrier()
            self.bank_free = [None] * 8
            for b in range(s.nb):
                rows = s.rows(b)
                self.transpose_to(None, mt[:, b * P:b * P + rows], [t], copy=lambda ps, tk, b=b, rows=rows: q.dve(
                    lambda e: e.tensor_tensor(x[0:rows, b, :], x[0:rows, b, :], ps, ALU.add), after=[tk]))
            q.barrier()

    def layer3(self, x):
        s, q, io = self.s, self.q, self.io
        groups = s.groups
        self.xl = self.dram("x_l", (s.n, D))
        self.gathered = self.dram("gathered", (groups, P, 4 * D))
        with ExitStack() as scope:
            sb = self.sb
            h = sb(scope, "h", [P, s.nb, D])
            alpha = sb(scope, "alpha", [P, 4 * s.run, 16, HEADS])
            loop = sb(scope, "loop", [P, 4 * s.run, 16, HEADS])
            rstd, nbias, t = self.ln_factors(scope, x, [self.last_dve()])
            hd = self.ln_apply(h, x, rstd, nbias, ACT.Relu, [t])
            with ExitStack() as inner:
                xr = self.project(inner, h, hd)
                self.logits(xr, alpha, loop)
                q.barrier()
            self.bank_free = [None] * 8
            self.softmax_numerators(alpha, loop)
            acc = sb(scope, "acc", [P, s.nb, D + 2 * HEADS])
            self.weighted_sums(alpha, loop, acc)
            q.barrier()
            self.bank_free = [None] * 8
            self.feed_forward(x, h, acc)

    def ln_affine_t(self, scope, ut, x, gain, shift, after):
        s, q = self.s, self.q
        tmp = self.sb(scope, "ln_rows", [P, s.nb, D])
        rstd, nbias, t = self.ln_factors(scope, x, after)
        rows = self.ln_apply(tmp, x, rstd, nbias, ACT.Identity, [t])
        for b in range(s.nb):
            t = self.transpose_to(None, tmp[:, b, :], [rows[b]], copy=lambda ps, tk, b=b: q.dve(
                lambda e: e.tensor_scalar(ut[:, b * P:(b + 1) * P], ps, gain, shift, ALU.mult, ALU.add),
                after=[tk, self.loaded()]))
        return t

    def project(self, scope, h, hd):
        s, q, io = self.s, self.q, self.io
        xr = self.sb(scope, "x_r", [P, s.nb, D + HEADS])
        with ExitStack() as inner:
            sb = self.sb
            w = sb(inner, "w_lr", [P, 2 * D])
            cols = sb(inner, "cols3", [P, 2])
            ut = sb(inner, "ut", [P, s.nb * P])
            xl = sb(inner, "xl", [P, s.nb, D])
            w_e = sb(inner, "w_e_rows", [P, D])
            att = sb(inner, "att_rows", [P, D])
            mean = sb(inner, "mean", [P, D])
            z = sb(inner, "z_loop", [P, s.nb, D])
            for k in range(4):
                self.load(w_e[k * DE:(k + 1) * DE, :], io["L3_gnn_W_e"])
            self.load(att[:, :], io["att_row"].partition_broadcast(P))
            self.load(w[:, 0:D], io["L3_gnn_W_l"])
            self.load(w[:, D:2 * D], io["L3_gnn_W_r"])
            self.load(cols[:, 0:1], self.column("L3_gnn_ln1_g"))
            self.load(cols[:, 1:2], self.column("L3_gnn_ln1_b"))
            self.wait_setup()
            t = self.ln_affine_t(inner, ut, h, cols[:, 0:1], cols[:, 1:2], [hd[-1]])
            for b in range(s.nb):
                i = self.next_bank()
                ps = self.bank[i]
                t = q.pe(lambda e, b=b, ps=ps: e.matmul(ps[:, 0:2 * D], ut[:, b * P:(b + 1) * P], w[:, :],
                                                        start=True, stop=True), after=[t, self.bank_free[i]])
                q.dve(lambda e, b=b, ps=ps: e.tensor_copy(xl[:, b, :], ps[:, 0:D]), after=[t])
                t = self.bank_free[i] = q.dve(lambda e, b=b, ps=ps: e.tensor_copy(xr[:, b, 0:D], ps[:, D:2 * D]))
            full = (s.nb - 1) * P
            lane = q.lane("x_l_stores")
            q.dma("sync", lane, lambda e: e.dma_start(
                self.xl[0:full, :].rearrange("(b l) f -> l b f", l=P), xl[:, 0:s.nb - 1, :]), after=[t])
            q.dma("sync", lane, lambda e: e.dma_start(self.xl[full:s.n, :], xl[0:s.last, s.nb - 1, :]))
            i = self.next_bank()
            ps = self.bank[i][:, 0:D]
            u = q.pe(lambda e: e.matmul(ps, self.edge_sum[:, 0:1].to_broadcast([P, P]), w_e[:, :],
                                        start=True, stop=True), after=[self.bank_free[i]])
            u = self.bank_free[i] = q.dve(lambda e: e.tensor_scalar(mean[:, :], ps, 1.0 / s.edges, None, ALU.mult),
                                          after=[u])
            t = q.dve(lambda e: e.tensor_tensor(z[:, :, :], xl[:, :, :], xr[:, :, 0:D], ALU.add), after=[t])
            t = q.dve(lambda e: e.tensor_tensor(z[:, :, :], z[:, :, :], self.rows_of(mean), ALU.add), after=[t, u])
            t = q.dve(lambda e: e.scalar_tensor_tensor(z[:, :, :], z[:, :, :], NEG_SLOPE, z[:, :, :],
                                                       ALU.mult, ALU.max), after=[t])
            t = q.dve(lambda e: e.tensor_tensor(z[:, :, :], z[:, :, :], self.rows_of(att), ALU.mult), after=[t])
            q.dve(lambda e: e.tensor_reduce(xr[:, :, D:], z[:, :, :].rearrange("p b (h c) -> p b h c", c=CH),
                                            AX.X, ALU.add), after=[t])
            q.barrier()
        return xr

    def rows_of(self, row):
        return row[:, :].rearrange("p (o f) -> p o f", o=1).to_broadcast([P, self.s.nb, D])

    def logits(self, xr, alpha, loop):
        s, q, io = self.s, self.q, self.io
        groups = s.groups
        with ExitStack() as scope:
            sb = self.sb
            src = sb(scope, "src", [P, 4 * s.padded], I32)
            regs = sb(scope, "regs", [1, 2, s.padded], I32)
            w_e = sb(scope, "w_e", [P, 4, D + HEADS])
            att = sb(scope, "att", [P, D])
            place = sb(scope, "place", [P, 16])
            slots, ahead = 6, 4
            rows = sb(scope, "rows", [P, slots, 4 * D])
            edges = sb(scope, "edges", [P, slots, P])
            rel = sb(scope, "rel", [P, slots, 4 * P], I16)
            hot = sb(scope, "hot", [P, 2, 4 * P])
            z = sb(scope, "z", [P, 2, 4 * D])
            leaky = sb(scope, "leaky", [P, 2, 4 * D])
            self.load(src[:, :], self.e_src)
            self.load(regs[:, :, :], self.e_regs.rearrange("(o a) n -> o a n", o=1))
            t = q.dve(lambda e: e.memset(w_e[:, :, :], 0.0))
            for k in range(4):
                self.load(w_e[k * DE:(k + 1) * DE, k, 0:D], io["L3_gnn_W_e"], after=[t])
            self.load(att[:, :], io["att_row"].partition_broadcast(P))
            self.load(place[:, :], io["c_step"])
            self.wait_setup()
            for m in (alpha, loop):
                for g in range(groups, s.padded):
                    q.dve(lambda e, m=m, g=g: e.memset(self.places(m, g), 0.0))
            quad = Registers(self.nc, q, "sync", regs[0:1, 0, :], groups, s.quads, [self.loaded()])
            block = Registers(self.nc, q, "tensor", regs[0:1, 1, :], groups, s.nb - 1, [self.loaded()])
            got = [q.lane(f"rows{i}") for i in range(slots)]
            edge_lane = [q.lane(f"edges{i}") for i in range(slots)]
            rel_lane = [q.lane(f"rel{i}") for i in range(slots)]
            kept = [q.lane(f"kept{i}") for i in range(slots)]
            sums, hots, products, used, parts, loops = [], [], [], [], [], []
            stores = []

            def fetch(g):
                r = g % slots
                old = g - slots
                for k in range(4):
                    v = 4 * g + k
                    rows_in[g] = q.dma("gpsimd", got[r], lambda e, v=v, r=r, k=k: e.indirect_dma_start(
                        rows[:, r, k * D:(k + 1) * D], None, self.xl,
                        bass.IndirectOffsetOnAxis(ap=src[:, v:v + 1], axis=0)),
                        after=[sums[old], stores[old]] if old >= 0 else ())
                quad.prefetch(g)
                edges_in[g] = q.dma("sync", edge_lane[r], lambda e, g=g, r=r: e.dma_start(
                    edges[:, r, :], io["edge_t"][bass.ds(quad.at(g), 1), :, :].rearrange("o r e -> (o r) e")),
                    after=[products[old]] if old >= 0 else ())
                rel_in[g] = q.dma("sync", rel_lane[r], lambda e, g=g, r=r: e.dma_start(
                    rel[:, r, :], self.e_rel_rows[g, :].partition_broadcast(P)),
                    after=[hots[old]] if old >= 0 else ())

            rows_in, edges_in, rel_in, here = {}, {}, {}, {}
            for g in range(ahead):
                fetch(g)
            four = "p (b v f) -> p b v f"
            wide = D + HEADS

            def pair_of(g):
                return self.psum[:, 2 * (g % 4):2 * (g % 4) + 2, 0:2 * wide].rearrange(
                    "p b (v f) -> p b v f", f=wide)

            def multiply(g):
                r, two, pair = g % slots, g % 2, pair_of(g)
                hots.append(q.dve(lambda e: e.tensor_scalar(
                    hot[:, two, :], rel[:, r, :], place[:, 0:1], None, ALU.is_equal),
                    after=[rel_in[g], products[g - 2] if g >= 2 else None]))
                block.prefetch(g)
                q.wait("tensor", [hots[g], edges_in[g]] + ([sums[g - 4], loops[g - 4]] if g >= 4 else []))
                q.step("tensor", lambda e: here.update({g: xr[:, bass.ds(block.at(g), 1), :].rearrange(
                    "p o f -> p (o f)")}))
                for k in range(4):
                    q.pe(lambda e, k=k: e.matmul(pair[:, k // 2, k % 2, :], hot[:, two, k * P:(k + 1) * P],
                                                 here[g], start=True, stop=False))
                    t = q.pe(lambda e, k=k: e.matmul(pair[:, k // 2, k % 2, :], edges[:, r, :], w_e[:, k, :],
                                                     start=False, stop=True))
                products.append(t)

            multiply(0)
            for g in range(groups):
                r, two, pair = g % slots, g % 2, pair_of(g)
                if g + 1 < groups:
                    multiply(g + 1)
                sums.append(q.dve(lambda e, two=two, r=r, pair=pair: e.tensor_tensor(
                    z[:, two, :].rearrange(four, b=2, f=D), pair[:, :, :, 0:D],
                    rows[:, r, :].rearrange(four, b=2, f=D), ALU.add),
                    after=[products[g], rows_in[g], parts[g - 2] if g >= 2 else None]))
                loops.append(q.act(lambda e, g=g, pair=pair: e.activation(
                    self.places(loop, g).rearrange("p (b v) h -> p b v h", b=2), pair[:, :, :, D:], ACT.Copy),
                    after=[sums[g]]))
                stores.append(q.dma("sync", kept[r], lambda e, g=g, r=r: e.dma_start(
                    self.gathered[g, :, :], rows[:, r, :]), after=[rows_in[g]]))
                if g >= 1:
                    self.head_sums(alpha, leaky, att, g - 1, parts, used)
                parts.append(q.dve(lambda e, two=two: e.scalar_tensor_tensor(
                    leaky[:, two, :], z[:, two, :], NEG_SLOPE, z[:, two, :], ALU.mult, ALU.max),
                    after=[sums[g], used[g - 2] if g >= 2 else None]))
                if g + ahead < groups:
                    fetch(g + ahead)
            self.head_sums(alpha, leaky, att, groups - 1, parts, used)
            q.barrier()

    def head_sums(self, alpha, leaky, att, g, parts, used):
        q, two = self.q, g % 2
        view = leaky[:, two, :].rearrange("p (v f) -> p v f", f=D)
        t = q.dve(lambda e: e.tensor_tensor(view, view, att[:, :].rearrange("p (o f) -> p o f", o=1)
                                            .to_broadcast([P, 4, D]), ALU.mult), after=[parts[g]])
        used.append(q.dve(lambda e: e.tensor_reduce(
            self.places(alpha, g),
            leaky[:, two, :].rearrange("p (v h c) -> p v h c", v=4, c=CH), AX.X, ALU.add), after=[t]))

    def places(self, alpha, g):
        c, at = divmod(g, self.s.run)
        return alpha[:, 4 * at:4 * at + 4, c, :]

    def softmax_numerators(self, alpha, loop):
        s, q = self.s, self.q
        tiles = 4 * s.run
        n = tiles * P
        with ExitStack() as scope:
            sb = self.sb
            a = sb(scope, "a", [P, n])
            top = sb(scope, "top", [P, n])
            new = sb(scope, "new", [P, n])
            carry = sb(scope, "carry", [P, 4])
            row = sb(scope, "row", [1, 3, P])
            new_lane = q.lane("new_rows")

            def load_new(j, after):
                for c in range(16):
                    t = q.dma("sync", new_lane, lambda e, c=c: e.dma_start(
                        new[8 * c:8 * c + 8, :], self.e_new[j][c * n:(c + 1) * n].partition_broadcast(8)),
                        after=[after])
                return t
            fresh = load_new(0, None)
            used = [("vector", q.count["vector"]), ("scalar", q.count["scalar"])]
            for g in range(tiles):
                t = self.transpose_to(a[:, g * P:(g + 1) * P],
                                      alpha[:, g, :, :].rearrange("p c h -> p (c h)"), [])
            self.wait_setup()
            for back in (False, True):
                if back:
                    fresh = load_new(1, t)
                source = top if back else a
                trial = alpha[:, :, :, :].rearrange("p g c h -> p (g c h)") if back else top[:, :]

                def scan(start, after, to, back=back, source=source, new=new):
                    flip = (lambda m: m[:, ::-1]) if back else (lambda m: m)
                    return q.dve(lambda e: e.tensor_tensor_scan(flip(to), flip(new[:, :]), flip(source[:, :]),
                                                                start, ALU.add, ALU.max), after=after)
                end = (lambda m: m[:, 0:1]) if back else (lambda m: m[:, n - 1:n])
                t = scan(NONE, [t, fresh], trial)
                q.dve(lambda e, trial=trial, end=end: e.tensor_copy(carry[:, 0:1], end(trial)), after=[t])
                t = q.dve(lambda e: e.tensor_reduce(carry[:, 1:2], new[:, :], AX.X, ALU.min), after=[t])
                t = q.dve(lambda e: e.tensor_copy(carry[:, 2:3], carry[:, 0:1]), after=[t])
                self.transpose_to(row[:, 0, :], carry[:, 1:2], [t])
                t = self.transpose_to(row[:, 1, :], carry[:, 2:3], [t])
                t = q.dve(lambda e: e.memset(row[:, 2, :], NONE), after=[t])
                for h in range(HEADS):
                    def of(j, h=h, back=back):
                        v = row[:, j, :].rearrange("p (c h) -> p h c", h=HEADS)[:, h, :]
                        return v[:, ::-1] if back else v
                    t = q.dve(lambda e, of=of: e.tensor_tensor_scan(of(1), of(0), of(1), NONE, ALU.add, ALU.max),
                              after=[t])
                if back:
                    t = q.dve(lambda e: e.tensor_copy(row[:, 2, 0:P - HEADS], row[:, 1, HEADS:P]), after=[t])
                else:
                    t = q.dve(lambda e: e.tensor_copy(row[:, 2, HEADS:P], row[:, 1, 0:P - HEADS]), after=[t])
                t = self.transpose_to(carry[:, 3:4], row[:, 2, :], [t])
                t = scan(carry[:, 3:4], [t], top[:, :])
            own = alpha[:, :, :, :].rearrange("p g c h -> p (g c h)")
            fresh = load_new(0, t)
            for g in range(tiles):
                u = self.transpose_to(own[:, g * P:(g + 1) * P],
                                      loop[:, g, :, :].rearrange("p c h -> p (c h)"), [t])
            t = q.dve(lambda e: e.tensor_tensor(top[:, :], top[:, :], own, ALU.max), after=[u])
            t = q.dve(lambda e: e.tensor_tensor(a[:, :], a[:, :], top[:, :], ALU.subtract), after=[t])
            weights = q.act(lambda e: e.activation(a[:, :], a[:, :], ACT.Exp), after=[t])
            t = q.dve(lambda e: e.tensor_tensor(own, own, top[:, :], ALU.subtract), after=[t])
            u = q.act(lambda e: e.activation(own, own, ACT.Exp), after=[t])
            t = q.dve(lambda e: e.scalar_tensor_tensor(own, new[:, :], 0.0, own,
                                                       ALU.is_lt, ALU.mult), after=[fresh, u])
            for back_to, rows, ready in ((loop, own, t), (alpha, a, weights)):
                for g in range(tiles):
                    self.transpose_to(back_to[:, g, :, :].rearrange("p c h -> p (c h)"),
                                      rows[:, g * P:(g + 1) * P], [ready])
            q.barrier()
        self.bank_free = [None] * 8

    def weighted_sums(self, alpha, loop, acc):
        s, q, io = self.s, self.q, self.io
        groups = s.groups
        with ExitStack() as scope:
            sb = self.sb
            slots, ahead = 6, 4
            wide = D + 2 * HEADS
            rows = sb(scope, "rows", [P, slots, 4 * D])
            both = sb(scope, "both", [P, 2, 4, wide])
            hot = sb(scope, "hot", [P, 2, 4, P])
            rel = sb(scope, "rel", [P, 4 * s.padded])
            win = sb(scope, "win", [1, s.padded], I32)
            iota = self.load_iota(scope)
            self.load(rel[:, :], self.e_rel)
            self.load(win[:, :], self.e_regs[1:2, :])
            t = q.dve(lambda e: e.memset(acc[:, :, :], 0.0))
            self.wait_setup()
            block = Registers(self.nc, q, "vector", win[0:1, :], groups, s.nb - 1, [self.loaded()])
            lane = [q.lane(f"again{i}") for i in range(slots)]
            weighted, products, added, rows_in = [], [], [t], {}

            def fetch(g):
                rows_in[g] = q.dma("sync", lane[g % slots], lambda e: e.dma_start(
                    rows[:, g % slots, :], self.gathered[g, :, :]),
                    after=[weighted[g - slots]] if g >= slots else ())
            for g in range(ahead):
                fetch(g)

            def add(g):
                ps = self.bank[g % 8][:, 0:wide]
                block.prefetch(g)

                def put(e):
                    at = acc[:, bass.ds(block.at(g), 1), :].rearrange("p o f -> p (o f)")
                    return e.tensor_tensor(at, at, ps, ALU.add)
                added.append(q.dve(put, after=[products[g], added[-1]]))

            for g in range(groups):
                two = g % 2
                old = products[g - 2] if g >= 2 else None
                w = self.places(alpha, g)
                q.act(lambda e, two=two, w=w: e.activation(both[:, two, :, D:D + HEADS], w, ACT.Copy), after=[old])
                w = self.places(loop, g)
                q.act(lambda e, two=two, w=w: e.activation(both[:, two, :, D + HEADS:], w, ACT.Copy))
                for k in range(4):
                    pool_hots, dve_hots = (q.on("gpsimd" if k_ < 2 else "vector", lambda e, k_=k_, two=two, g=g:
                                                e.tensor_scalar(hot[:, two, k_, :], iota[:, :],
                                                                rel[:, 4 * g + k_:4 * g + k_ + 1], None,
                                                                ALU.is_equal), after=[old])
                                           for k_ in (k, k + 2)) if k < 2 else (pool_hots, dve_hots)
                weighted.append(q.dve(lambda e, two=two, g=g: e.tensor_tensor(
                    both[:, two, :, 0:D].rearrange("p v (h c) -> p v h c", c=CH),
                    rows[:, g % slots, :].rearrange("p (v h c) -> p v h c", h=HEADS, c=CH),
                    self.places(alpha, g).rearrange("p v (h o) -> p v h o", o=1)
                    .to_broadcast([P, 4, HEADS, CH]), ALU.mult), after=[rows_in[g], old]))
                for k in range(4):
                    t = q.pe(lambda e, two=two, k=k, g=g: e.matmul(
                        self.bank[g % 8][:, 0:wide], hot[:, two, k, :], both[:, two, k, :],
                        start=k == 0, stop=k == 3),
                        after=[weighted[g], pool_hots, dve_hots, self.last_act(),
                               added[g - 8 + 1] if g >= 8 else None])
                products.append(t)
                if g >= 1:
                    add(g - 1)
                if g + ahead < groups:
                    fetch(g + ahead)
            add(groups - 1)
            q.barrier()

    def feed_forward(self, x, h, acc):
        s, q, io = self.s, self.q, self.io
        with ExitStack() as scope:
            sb = self.sb
            rows = sb(scope, "rows2", [P, 2, D])
            w1 = sb(scope, "w1", [P, 2 * D])
            w2 = sb(scope, "w2f", [P, 2, D])
            cols = sb(scope, "cols4", [P, 4])
            den = sb(scope, "den", [P, s.nb, HEADS])
            ut = sb(scope, "ut2", [P, s.nb * P])
            mid = sb(scope, "mid4", [P, 2, s.nb * P])
            own_xl = ut[:, :].rearrange("p (b f) -> p b f", f=D)
            full = (s.nb - 1) * P
            t = q.dve(lambda e: e.memset(own_xl[:, s.nb - 1, :], 0.0))
            self.load(own_xl[:, 0:s.nb - 1, :], self.xl[0:full, :].rearrange("(b l) f -> l b f", l=P))
            self.load(own_xl[0:s.last, s.nb - 1, :], self.xl[full:s.n, :], after=[t])
            self.load(rows[:, 0, :], io["L3_gnn_bias"].partition_broadcast(P))
            self.load(rows[:, 1, :], io["L3_gnn_b2"].partition_broadcast(P))
            self.load(w1[:, :], io["L3_gnn_W1"])
            self.load(w2[:, :, :], io["L3_gnn_W2"].rearrange("(j k) f -> k j f", k=P))
            self.load(cols[:, 0:1], self.column("L3_gnn_ln2_g"))
            self.load(cols[:, 1:2], self.column("L3_gnn_ln2_b"))
            self.load(cols[:, 2:4], io["L3_gnn_b1_t"])
            self.wait_setup()
            weights, own = acc[:, :, D:D + HEADS], acc[:, :, D + HEADS:]
            t = q.dve(lambda e: e.tensor_scalar(den[:, :, :], weights, 0.0, None, ALU.is_equal))
            t = q.dve(lambda e: e.tensor_tensor(own, own, den[:, :, :], ALU.add), after=[t])
            t = q.dve(lambda e: e.tensor_tensor(den[:, :, :], weights, own, ALU.add), after=[t])
            t = q.dve(lambda e: e.tensor_scalar(den[:, :, :], den[:, :, :], DENOM_EPS, None, ALU.add), after=[t])
            t = q.dve(lambda e: e.reciprocal(den[:, :, :], den[:, :, :]), after=[t])

            def per_head(m):
                return m.rearrange("p b (h o) -> p b h o", o=1).to_broadcast([P, s.nb, HEADS, CH])
            sums = acc[:, :, 0:D].rearrange("p b (h c) -> p b h c", c=CH)
            own_rows = ut[:, :].rearrange("p (b h c) -> p b h c", h=HEADS, c=CH)
            u = q.dve(lambda e: e.tensor_tensor(own_rows, own_rows, per_head(own), ALU.mult), after=[t])
            u = q.dve(lambda e: e.tensor_tensor(sums, sums, own_rows, ALU.add), after=[u])
            u = q.dve(lambda e: e.tensor_tensor(sums, sums, per_head(den[:, :, :]), ALU.mult), after=[u])
            u = q.dve(lambda e: e.tensor_tensor(h[:, :, :], h[:, :, :], acc[:, :, 0:D], ALU.add), after=[u])
            u = q.dve(lambda e: e.tensor_tensor(
                h[:, :, :], h[:, :, :], rows[:, 0:1, :].to_broadcast([P, s.nb, D]), ALU.add), after=[u])
            t = self.ln_affine_t(scope, ut, h, cols[:, 0:1], cols[:, 1:2], [u])
            u = q.dve(lambda e: e.tensor_tensor(x[:, :, :], x[:, :, :], h[:, :, :], ALU.add))
            u = q.dve(lambda e: e.tensor_tensor(
                x[:, :, :], x[:, :, :], rows[:, 1:2, :].to_broadcast([P, s.nb, D]), ALU.add), after=[u])
            wide = 400
            assert wide * 8 == s.nb * P
            mids = []
            for c in range(8):
                for j in range(2):
                    i = self.next_bank()
                    ps = self.bank[i][:, 0:wide]
                    tk = q.pe(lambda e, c=c, j=j, ps=ps: e.matmul(
                        ps, w1[:, j * D:(j + 1) * D], ut[:, c * wide:(c + 1) * wide], start=True, stop=True),
                        after=[t, self.bank_free[i]])
                    m = self.bank_free[i] = q.act(lambda e, c=c, j=j, ps=ps: e.activation(
                        mid[:, j, c * wide:(c + 1) * wide], ps, ACT.Gelu, bias=cols[:, 2 + j:3 + j]), after=[tk])
                mids.append(m)
            for b in range(s.nb):
                i = self.next_bank()
                ps = self.bank[i][:, 0:D]
                for j in range(2):
                    tk = q.pe(lambda e, b=b, j=j, ps=ps: e.matmul(
                        ps, mid[:, j, b * P:(b + 1) * P], w2[:, j, :], start=j == 0, stop=j == 1),
                        after=[mids[min(7, ((b + 1) * P - 1) // wide)], self.bank_free[i]])
                done = self.bank_free[i] = q.dve(lambda e, b=b, ps=ps: e.tensor_tensor(
                    x[:, b, :], x[:, b, :], ps, ALU.add), after=[tk, u])
            self.store_nodes(x, done)

    def store_nodes(self, x, after):
        s, q = self.s, self.q
        lane = q.lane("output")
        full = (s.nb - 1) * P
        q.dma("sync", lane, lambda e: e.dma_start(
            self.out[0:full, :].rearrange("(b l) f -> l b f", l=P), x[:, 0:s.nb - 1, :]), after=[after])
        end = q.dma("sync", lane, lambda e: e.dma_start(self.out[full:s.n, :], x[0:s.last, s.nb - 1, :]))
        q.wait("sync", [end])

    def build(self):
        s, q, ctx, io = self.s, self.q, self.ctx, self.io
        self.constants()
        self.edge_tables()
        self.count_tables()
        x = self.sb(ctx, "x", [P, s.nb, D])
        with ExitStack() as scope:
            counts = self.sb(scope, "counts", [P, s.nb, s.nc], F16)
            self.count_matrix(counts)
            self.layer0(x)
            rdeg = self.sb(scope, "rdeg", [P, s.nb])
            self.layer1(x, rdeg)
            self.layer2(x, rdeg)
            q.barrier()
        self.layer3(x)
        q.barrier()
        q.emit()


def gnn_program(nc, n_nodes, n_edges, io, out):
    with ExitStack() as ctx:
        Kernel(nc, ctx, Shapes(n_nodes, n_edges), io, out).build()




def layouts(inputs):
    import numpy as np

    s = Shapes(inputs["x"].shape[0], inputs["dst"].shape[0])
    a = {k: np.ascontiguousarray(v) for k, v in inputs.items()}
    src, dst, edge = a.pop("src"), a.pop("dst"), a.pop("edge_attr_32")
    total = (s.quads + 1) * 4 * P
    room = total - dst.shape[0]
    dst = np.concatenate([dst, np.full(room, s.pad_dst, dst.dtype)])
    src = np.concatenate([src, np.zeros(room, src.dtype)])
    a["dst_rows"], a["src_rows"] = dst.reshape(-1, P), src.reshape(-1, P)
    a["dst_quads"], a["src_quads"] = dst.reshape(-1, 4 * P), src.reshape(-1, 4 * P)
    a["dst_last"] = np.ascontiguousarray(a["dst_rows"][:s.tiles, -1])
    a["dst_quad_last"] = np.ascontiguousarray(a["dst_quads"][:s.quads, -1])
    edge = np.concatenate([edge, np.zeros((room, DE), edge.dtype)]).reshape(s.quads + 1, 4, P, DE)
    a["edge_t"] = np.ascontiguousarray(edge.transpose(0, 1, 3, 2)).reshape(s.quads + 1, 4 * DE, P)
    for name in ("L0_gnn_W_ih", "L0_gnn_W_hh", "L2_gnn_W1", "L2_gnn_W2", "L2_gnn_W_self"):
        a[name + "_t"] = np.ascontiguousarray(a.pop(name).T)
    for name in ("L0_gnn_b_ih", "L0_gnn_b_hh"):
        a[name + "_t"] = np.ascontiguousarray(a.pop(name).reshape(3, D).T)
    a["L3_gnn_b1_t"] = np.ascontiguousarray(a.pop("L3_gnn_b1").reshape(2, D).T)
    a["att_row"] = a.pop("L3_gnn_att").reshape(D)
    far = np.arange(s.nb)[:, None] * 2.0 * s.w + np.arange(s.w)
    a["c_ident"] = np.eye(P, dtype=np.float32)
    a["c_iota"] = np.arange(P, dtype=np.float32)
    a["c_far"] = far.reshape(-1).astype(np.float32)
    a["c_tile_no"] = np.arange(s.tiles, dtype=np.float32)
    a["c_step"] = np.ascontiguousarray(np.arange(16 * P, dtype=np.float32).reshape(16, P).T)
    return a


def kernel(**inputs):
    import concourse.bacc as bacc
    from concourse.bass_utils import run_bass_kernel_spmd

    arrays = layouts(inputs)
    n_nodes, n_edges = inputs["x"].shape[0], inputs["dst"].shape[0]
    nc = bacc.Bacc("TRN2", target_bir_lowering=False, num_devices=1)
    io = {name: nc.dram_tensor(name, a.shape, mybir.dt.from_np(a.dtype), kind="ExternalInput").ap()
          for name, a in arrays.items()}
    out = nc.dram_tensor("out", (n_nodes, D), F32, kind="ExternalOutput").ap()
    gnn_program(nc, n_nodes, n_edges, io, out)
    r = run_bass_kernel_spmd(nc, [arrays], core_ids=[0])
    return r.results[0]["out"]
```

```python
from contextlib import ExitStack

import concourse.bass as bass
from concourse import mybir

F32 = mybir.dt.float32
F16 = mybir.dt.float16
BF16 = mybir.dt.bfloat16
I32 = mybir.dt.int32
I16 = mybir.dt.int16
ALU = mybir.AluOpType
ACT = mybir.ActivationFunctionType
AX = mybir.AxisListType

P = 128
D = 128
HEADS = 8
CH = D // HEADS
DE = 32
NEG_SLOPE = 0.2
EPS = 1e-5
DENOM_EPS = 1e-16
NONE = -3.0e38
BANKS = 8
CLEAR = 3
F16_SCALE = 4096.0


class Shapes:
    def __init__(self, n_nodes, n_edges):
        self.n = n_nodes
        self.nb = -(-n_nodes // P)
        self.last = n_nodes - (self.nb - 1) * P
        self.edges = n_edges
        self.tiles = -(-n_edges // P)
        self.quads = -(-self.tiles // 4)
        self.w = 8
        self.windows = -(-n_nodes // self.w)
        self.nc = self.windows * self.w
        self.pad_dst = self.nc - 1
        assert self.pad_dst >= n_nodes
        self.csteps = self.tiles + self.windows - 1
        self.groups = self.quads + self.nb - 1
        self.run = -(-self.groups // 16)
        self.padded = 16 * self.run

    def rows(self, b):
        return P if b < self.nb - 1 else self.last


class Core:

    ENGINES = ("tensor", "vector", "scalar", "gpsimd", "sync")

    def __init__(self, nc, ctx):
        self.nc = nc
        self.queue = {e: [] for e in self.ENGINES}
        self.sem = {e: ctx.enter_context(nc.semaphore(f"{e}_done")) for e in self.ENGINES}
        self.count = {e: 0 for e in self.ENGINES}
        self.waited = {e: {} for e in self.ENGINES}
        self.ctx = ctx

    def lane(self, name):
        self.sem[name] = self.ctx.enter_context(self.nc.semaphore(name))
        self.count[name] = 0
        return name

    def wait(self, engine, after):
        for token in after:
            if token is None:
                continue
            name, value = token
            if value > self.waited[engine].get(name, 0):
                self.waited[engine][name] = value
                sem = self.sem[name]
                self.queue[engine].append(lambda e, sem=sem, value=value: e.wait_ge(sem, value))

    def on(self, engine, make, after=(), late=None):
        self.wait(engine, after)
        sem = self.sem[engine]
        if late is None:
            self.queue[engine].append(lambda e: make(e).then_inc(sem, 1))
        else:
            name, value = late
            self.waited[engine][name] = max(value, self.waited[engine].get(name, 0))
            self.queue[engine].append(lambda e, of=self.sem[name]: make(e)._wait_ge(of, value).then_inc(sem, 1))
        self.count[engine] += 1
        return engine, self.count[engine]

    def dma(self, engine, lane, make, after=()):
        self.wait(engine, after)
        sem = self.sem[lane]
        self.queue[engine].append(lambda e: make(e).then_inc(sem, 16))
        self.count[lane] += 16
        return lane, self.count[lane]

    def step(self, engine, do, after=()):
        self.wait(engine, after)
        self.queue[engine].append(do)

    def pe(self, make, after=()):
        return self.on("tensor", make, after)

    def dve(self, make, after=()):
        return self.on("vector", make, after)

    def act(self, make, after=(), late=None):
        return self.on("scalar", make, after, late)

    def pool(self, make, after=()):
        return self.on("gpsimd", make, after)

    def barrier(self):
        everything = [(name, value) for name, value in self.count.items() if value]
        for e in self.ENGINES:
            self.wait(e, everything)

    def emit(self):
        with self.nc.Block() as block:
            for name in self.ENGINES:
                def run(e, name=name):
                    for make in self.queue[name]:
                        make(e)
                {"tensor": block.tensor, "vector": block.vector, "scalar": block.scalar,
                 "gpsimd": block.gpsimd, "sync": block.sync}[name](run)


class Registers:

    def __init__(self, nc, q, engine, row, n, top, after, at_once=8):
        self.at_once = at_once
        self.nc, self.q, self.engine, self.row, self.n, self.top = nc, q, engine, row, n, top
        self.engine_type = {"tensor": mybir.EngineType.PE, "vector": mybir.EngineType.DVE,
                            "scalar": mybir.EngineType.Activation, "sync": mybir.EngineType.SP}[engine]
        self.values = {}
        self.after = after
        self.fill(0)

    def fill(self, i):
        if i >= self.n:
            return
        hi = min(self.n, i + self.at_once)

        def load(e):
            _, values = self.nc.values_load_multi_w_load_instructions(
                self.row[:, i:hi], engines=[self.engine_type], min_val=0, max_val=self.top,
                skip_runtime_bounds_check_because="the tables are clamped to this range on the chip")
            self.values.update(zip(range(i, hi), values))
        self.q.step(self.engine, load, self.after)

    def prefetch(self, i):
        if i % self.at_once == 0:
            self.fill(i + self.at_once)

    def at(self, i):
        return self.values.pop(i)


class Kernel:
    def __init__(self, nc, ctx, s, io, out):
        self.nc, self.ctx, self.s, self.io, self.out = nc, ctx, s, io, out
        self.q = Core(nc, ctx)
        self.psum = ctx.enter_context(nc.psum_tensor("psum", [P, 8, 512], F32))
        self.bank = [self.psum[:, i, :] for i in range(8)]
        self.bank_free = [None] * 8
        self.turn = 0
        self.setup = self.q.lane("setup_loads")
        self.names = 0

    def sb(self, scope, name, shape, dt=F32):
        self.names += 1
        return scope.enter_context(self.nc.sbuf_tensor(f"{name}_{self.names}", shape, dt))

    def dram(self, name, shape, dt=F32):
        return self.nc.dram_tensor(name, shape, dt, kind="Internal").ap()

    def load(self, dst, src, after=()):
        self.q.dma("sync", self.setup, lambda e: e.dma_start(dst, src), after)

    def loaded(self):
        return self.setup, self.q.count[self.setup]

    def next_bank(self):
        self.turn = (self.turn + 1) % 8
        return self.turn

    def transpose_to(self, dst, src, after, copy=None):
        q, i = self.q, self.next_bank()
        k, m = src.free_size(), src.shape[0]
        ps = self.bank[i][0:k, 0:m]
        t = q.pe(lambda e: e.transpose(ps, src, self.ident[0:m, 0:m]), after=list(after) + [self.bank_free[i]])
        if copy is None:
            t = q.dve(lambda e: e.tensor_copy(dst, ps), after=[t])
        else:
            t = copy(ps, t)
        self.bank_free[i] = t
        return t

    def constants(self):
        ctx, io, q = self.ctx, self.io, self.q
        self.ident = self.sb(ctx, "ident", [P, P])
        self.eps = self.sb(ctx, "eps", [P, 1])
        self.edge_sum = self.sb(ctx, "edge_sum", [P, 1])
        self.load(self.ident[:, :], io["c_ident"])
        q.wait("tensor", [self.loaded()])
        q.dve(lambda e: e.memset(self.eps[:, :], EPS))

    def load_iota(self, scope):
        iota = self.sb(scope, "iota", [P, P])
        self.load(iota[:, :], self.io["c_iota"].partition_broadcast(P))
        return iota

    def path(self, scope, name, last, src_table, dst_table, shift, windows, nsteps):
        s, q, io = self.s, self.q, self.io
        tiles, width = last.shape[0], src_table.shape[1]
        nch = -(-nsteps // P)
        sb = self.sb
        ends = sb(scope, name + "_ends", [P, tiles])
        tile_no = sb(scope, name + "_tile_no", [P, tiles])
        win = sb(scope, name + "_win", [P, tiles], I32)
        junk = sb(scope, name + "_junk", [P, tiles])
        step = sb(scope, name + "_step", [P, nch])
        tile = sb(scope, name + "_tile", [P, nch])
        window = sb(scope, name + "_window", [P, nch])
        index = sb(scope, name + "_index", [P, nch], I32)
        loads = q.lane(name + "_loads")
        for to, what in ((win, last.partition_broadcast(P)),
                         (tile_no, io["c_tile_no"][0:tiles].partition_broadcast(P)),
                         (step, io["c_step"][:, 0:nch])):
            loaded = q.dma("sync", loads, lambda e, to=to, what=what: e.dma_start(to[:, :], what))
        t = q.dve(lambda e: e.tensor_scalar(win[:, :], win[:, :], shift, None,
                                            ALU.logical_shift_right), after=[loaded])
        t = q.dve(lambda e: e.tensor_copy(ends[:, :], win[:, :]), after=[t])
        t = q.dve(lambda e: e.tensor_tensor(ends[:, :], ends[:, :], tile_no[:, :], ALU.add), after=[t])
        src = sb(scope, name + "_src", [P, nch, width], I32)
        dst = sb(scope, name + "_dst", [P, nch, width], I32)
        lane = q.lane(name + "_edge_rows")
        for c in range(nch):
            t = q.dve(lambda e, c=c: e.tensor_scalar(junk[:, :], ends[:, :], step[:, c:c + 1], None, ALU.is_lt,
                                                     ALU.add, accum_out=tile[:, c:c + 1]), after=[t])
            t = q.dve(lambda e, c=c: e.tensor_copy(index[:, c:c + 1], tile[:, c:c + 1]), after=[t])
            for to, table in ((src, src_table), (dst, dst_table)):
                got = q.dma("gpsimd", lane, lambda e, c=c, to=to, table=table: e.indirect_dma_start(
                    to[:, c, :], None, table, bass.IndirectOffsetOnAxis(ap=index[:, c:c + 1], axis=0)),
                    after=[t])
        t = q.dve(lambda e: e.tensor_tensor(window[:, :], step[:, :], tile[:, :], ALU.subtract), after=[t])
        t = q.dve(lambda e: e.tensor_scalar(window[:, :], window[:, :], float(windows - 1), 0.0,
                                            ALU.min, ALU.max), after=[t])
        return nch, tile, window, src, dst, got, t

    def tables(self):
        s, q, io = self.s, self.q, self.io
        with ExitStack() as scope:
            counts = self.path(scope, "c", io["dst_last"], io["src_rows"], io["dst_rows"], 3, s.windows, s.csteps)
            edges = self.path(scope, "e", io["dst_quad_last"], io["src_quads"], io["dst_quads"], 7, s.nb, s.padded)
            self.count_tables(scope, counts)
            self.edge_tables(scope, edges)
            q.barrier()

    def edge_tables(self, scope, path):
        s, q = self.s, self.q
        n, m = s.padded, s.padded * 4 * P
        self.e_src = self.dram("e_src", (P, 4 * n), I32)
        self.e_rel = self.dram("e_rel", (P, 4 * n))
        self.e_rel_rows = self.dram("e_rel_rows", (n, 4 * P), I16)
        self.e_dst_flat = self.dram("e_dst_flat", (m + 2,))
        self.e_new = [self.dram("e_new_before", (m,), BF16), self.dram("e_new_behind", (m,), BF16)]
        self.e_any_new = self.dram("e_any_new", (2, P))
        self.e_regs = self.dram("e_regs", (2, path[0] * P), I32)
        self.e_lane = q.lane("edge_tables")
        self.new_lane = q.lane("edge_new")
        sb = self.sb
        nch, tile, window, src, dst, got, known = path
        wide = 4 * P
        rel = sb(scope, "rel", [P, nch, wide])
        dstf = sb(scope, "dstf", [P, nch, wide])
        rel16 = sb(scope, "rel16", [P, nch, wide], I16)
        srcf = sb(scope, "srcf", [P, nch, wide])
        first = sb(scope, "first", [P, nch])
        srct = sb(scope, "srct", [P, nch * P, 4], I32)
        relt = sb(scope, "relt", [P, nch * P, 4])
        pair = sb(scope, "pair", [P, 2, nch])
        rowf = sb(scope, "rowf", [2 * nch, P], I32)
        guard = sb(scope, "guard", [1, 1])
        a = q.dve(lambda e: e.memset(guard[:, :], -1.0), after=[known])
        b = q.dve(lambda e: e.tensor_scalar(first[:, :], window[:, :], float(P), None, ALU.mult), after=[a])
        b = q.dve(lambda e: e.tensor_copy(dstf[:, :, :], dst[:, :, :]), after=[got, b])
        t = q.dve(lambda e: e.tensor_copy(srcf[:, :, :], src[:, :, :]))
        flat = self.e_dst_flat
        rows = [(c, min(P, n - c * P)) for c in range(nch)]

        def store(dst_, src_, after):
            return q.dma("sync", self.e_lane, lambda e: e.dma_start(dst_, src_), after=[after])
        for c, r in rows:
            store(flat[1 + c * P * wide:1 + (c * P + r) * wide].rearrange("(v e) -> v e", e=wide),
                  dstf[0:r, c, :], t)
        store(flat[0:1].rearrange("(a b) -> a b", a=1), guard[:, :], t)
        stored = store(flat[m + 1:m + 2].rearrange("(a b) -> a b", a=1), guard[:, :], t)
        per = m // P
        near = sb(scope, "near", [P, 3, per])
        new = sb(scope, "new", [P, 2, per])
        new16 = sb(scope, "new16", [P, 2, per], BF16)
        any_new = sb(scope, "any_new", [P, 2])
        for j in range(3):
            back = q.dma("sync", self.new_lane, lambda e, j=j: e.dma_start(
                near[:, j, :], flat[j:j + m].rearrange("(p e) -> p e", p=P)), after=[stored])
        for c in range(nch):
            t = q.dve(lambda e, c=c: e.tensor_scalar(rel[:, c, :], dstf[:, c, :], first[:, c:c + 1], None,
                                                     ALU.subtract), after=[b])
        t = q.dve(lambda e: e.tensor_copy(rel16[:, :, :], rel[:, :, :]), after=[t])
        for c in range(nch):
            for k in range(4):
                self.transpose_to(srct[:, c * P:(c + 1) * P, k], srcf[:, c, k * P:(k + 1) * P], [t])
                self.transpose_to(relt[:, c * P:(c + 1) * P, k], rel[:, c, k * P:(k + 1) * P], [t])
        q.dve(lambda e: e.tensor_copy(pair[:, 0, :], tile[:, :]))
        t2 = q.dve(lambda e: e.tensor_copy(pair[:, 1, :], window[:, :]))
        t2 = self.transpose_to(rowf[:, :], pair[:, :, :].rearrange("p a c -> p (a c)"), [t2])
        store(self.e_src, srct[:, 0:n, :].rearrange("p g k -> p (g k)"), t2)
        store(self.e_rel, relt[:, 0:n, :].rearrange("p g k -> p (g k)"), t2)
        store(self.e_regs.rearrange("a (c s) -> (a c) s", s=P), rowf[:, :], t2)
        for c, r in rows:
            store(self.e_rel_rows[c * P:c * P + r, :], rel16[0:r, c, :], t2)
        for j in range(2):
            t = q.dve(lambda e, j=j: e.tensor_tensor(new[:, j, :], near[:, 1, :], near[:, 2 * j, :],
                                                     ALU.not_equal), after=[back])
            t = q.dve(lambda e, j=j: e.tensor_scalar(new[:, j, :], new[:, j, :], NONE, None, ALU.mult),
                      after=[t])
            u = q.dve(lambda e, j=j: e.tensor_copy(new16[:, j, :], new[:, j, :]), after=[t])
            store(self.e_new[j].rearrange("(p e) -> p e", p=P), new16[:, j, :], u)
            t = q.dve(lambda e, j=j: e.tensor_reduce(any_new[:, j:j + 1], new[:, j, :], AX.X, ALU.min), after=[t])
            store(self.e_any_new[j].rearrange("(p o) -> p o", o=1), any_new[:, j:j + 1], t)

    def count_tables(self, scope, path):
        s, q, io = self.s, self.q, self.io
        w = s.w
        sb = self.sb
        nch, tile, window, src, dst, got, known = path
        n = nch * P
        self.c_key_d = self.dram("c_key", (P, n))
        self.c_low_d = self.dram("c_low", (P, n))
        self.c_regs_d = self.dram("c_regs", (4, n), I32)
        self.c_lane = q.lane("count_tables")
        high = sb(scope, "high", [P, nch, P], I32)
        low = sb(scope, "low", [P, nch, P], I32)
        lowf = sb(scope, "lowf", [P, nch, P])
        key = sb(scope, "key", [P, nch, P])
        first = sb(scope, "first", [P, nch])
        dstf = sb(scope, "dstf", [P, nch, P])
        out = [sb(scope, "out", [P, n]) for _ in range(2)]
        bank = sb(scope, "bank", [P, 3, nch], I32)
        steers = sb(scope, "steers", [P, 4, nch])
        regs = sb(scope, "regs", [4 * nch, P], I32)
        t = q.dve(lambda e: e.tensor_scalar(high[:, :, :], src[:, :, :], 7, None, ALU.logical_shift_right),
                  after=[got, known])
        q.dve(lambda e: e.tensor_scalar(low[:, :, :], src[:, :, :], P - 1, None, ALU.bitwise_and))
        q.dve(lambda e: e.tensor_copy(dstf[:, :, :], dst[:, :, :]))
        t = q.dve(lambda e: e.tensor_scalar(first[:, :], window[:, :], float(w), None, ALU.mult))
        t = q.dve(lambda e: e.tensor_copy(key[:, :, :], high[:, :, :]), after=[t])
        t = q.dve(lambda e: e.tensor_copy(lowf[:, :, :], low[:, :, :]), after=[t])
        for c in range(nch):
            t = q.dve(lambda e, c=c: e.tensor_scalar(dstf[:, c, :], dstf[:, c, :], first[:, c:c + 1], -1.0,
                                                     ALU.subtract, ALU.max), after=[t])
            t = q.dve(lambda e, c=c: e.tensor_scalar(dstf[:, c, :], dstf[:, c, :], float(w), None,
                                                     ALU.min), after=[t])
        t = q.dve(lambda e: e.scalar_tensor_tensor(key[:, :, :], key[:, :, :], float(2 * w), dstf[:, :, :],
                                                   ALU.mult, ALU.add), after=[t])
        for j, ahead in enumerate((0, CLEAR, BANKS - 1)):
            t = q.dve(lambda e, j=j, ahead=ahead: e.tensor_scalar(bank[:, j, :], window[:, :], float(ahead),
                                                                  None, ALU.add), after=[t])
        t = q.dve(lambda e: e.tensor_scalar(bank[:, :, :], bank[:, :, :], BANKS - 1, None,
                                            ALU.bitwise_and), after=[t])
        q.dve(lambda e: e.tensor_copy(steers[:, 0:3, :], bank[:, :, :]), after=[t])
        t = q.dve(lambda e: e.tensor_scalar(steers[:, 3, :], window[:, :], 0.0, float(s.windows),
                                            ALU.is_equal, ALU.mult))
        t = q.dve(lambda e: e.scalar_tensor_tensor(steers[:, 3, :], window[:, :], -1.0, steers[:, 3, :],
                                                   ALU.add, ALU.add), after=[t])
        t = q.dve(lambda e: e.tensor_scalar(steers[:, 3, :], steers[:, 3, :], float(w), None, ALU.mult),
                  after=[t])
        for c in range(nch):
            cut = slice(c * P, (c + 1) * P)
            self.transpose_to(out[0][:, cut], key[:, c, :], [t])
            self.transpose_to(out[1][:, cut], lowf[:, c, :], [t])
        t2 = self.transpose_to(regs[:, :], steers[:, :, :].rearrange("p a c -> p (a c)"), [t])
        for to, what in ((self.c_key_d, out[0][:, :]), (self.c_low_d, out[1][:, :]),
                         (self.c_regs_d.rearrange("a (c s) -> (a c) s", s=P), regs[:, :])):
            q.dma("sync", self.c_lane, lambda e, to=to, what=what: e.dma_start(to, what), after=[t2])

    def count_matrix(self, counts):
        s, q = self.s, self.q
        w = s.w
        self.counts = counts
        ring, ahead = 8, 4
        with ExitStack() as scope:
            sb = self.sb
            far32 = sb(scope, "far32", [P, s.nb * w])
            far = sb(scope, "far", [P, s.nb * w], F16)
            lows = sb(scope, "lows", [P, ring, P], F16)
            keys = sb(scope, "keys", [P, ring, s.nb * w], F16)
            none = sb(scope, "none", [P, P], F16)
            n = self.c_key_d.shape[1]
            c_key, c_low = (sb(scope, name, [P, n]) for name in ("c_key", "c_low"))
            c_regs = sb(scope, "c_regs", [1, 4, n], I32)
            iota32 = self.load_iota(scope)
            self.load(c_key[:, :], self.c_key_d)
            self.load(c_low[:, :], self.c_low_d)
            self.load(c_regs[:, :, :], self.c_regs_d.rearrange("(o a) n -> o a n", o=1))
            self.load(far32[:, :], self.io["c_far"].partition_broadcast(P))
            iota = sb(scope, "iota16", [P, P], F16)
            self.wait_setup()
            q.dve(lambda e: e.memset(none[:, :], 0.0))
            q.dve(lambda e: e.tensor_copy(far[:, :], far32[:, :]))
            ready = q.dve(lambda e: e.tensor_copy(iota[:, :], iota32[:, :]))
            q.wait("vector", [ready])
            clear = [q.pe(lambda e, i=i: e.matmul(self.bank[i][:, 0:s.nb * w], none[:, :], far[:, :],
                                                  start=True, stop=True, skip_group_check=True),
                          after=[ready]) for i in range(BANKS)]
            its_bank, cleared, whole, column = (
                Registers(self.nc, q, name, c_regs[0:1, j, :], s.csteps, top, [self.loaded()], 12)
                for j, (name, top) in enumerate((("tensor", BANKS - 1), ("tensor", BANKS - 1),
                                                 ("scalar", BANKS - 1), ("scalar", (s.windows - 1) * w))))
            mm, copies = [], []

            def bank_at(place):
                return self.psum[:, bass.ds(place, 1), 0:s.nb * w].rearrange("p o n -> p (o n)")

            def one_hots(i):
                old = mm[i - ring] if i >= ring else None
                a = q.dve(lambda e: e.tensor_scalar(lows[:, i % ring, :], iota[:, :],
                                                    c_low[:, i:i + 1], None, ALU.is_equal), after=[old])
                b = q.dve(lambda e: e.tensor_scalar(keys[:, i % ring, :], far[:, :],
                                                    c_key[:, i:i + 1], None, ALU.is_equal), after=[old])
                return a, b

            def read_out(e, place, column):
                return e.activation(self.counts[:, :, column], bank_at(place).rearrange("p (h j) -> p h j", j=w),
                                    ACT.Copy)

            hots = {i: one_hots(i) for i in range(ahead)}
            for i in range(s.csteps):
                its_bank.prefetch(i)
                cleared.prefetch(i)
                q.wait("tensor", list(hots.pop(i)) + [clear[BANKS + i - CLEAR]])
                mm.append(q.pe(lambda e, i=i: e.matmul(bank_at(its_bank.at(i)), lows[:, i % ring, :],
                                                       keys[:, i % ring, :], start=False, stop=True,
                                                       skip_group_check=True)))
                clear.append(q.pe(lambda e, i=i: e.matmul(bank_at(cleared.at(i)), none[:, :],
                                                          far[:, :], start=True, stop=True, skip_group_check=True),
                                  after=[copies[i - BANKS + 1 + CLEAR] if i >= BANKS - 1 - CLEAR else None]))
                if i + ahead < s.csteps:
                    hots[i + ahead] = one_hots(i + ahead)
                whole.prefetch(i)
                column.prefetch(i)
                copies.append(q.act(lambda e, i=i: read_out(e, whole.at(i),
                                                            bass.ds(column.at(i), w)),
                                    after=[mm[i - 1] if i else clear[BANKS - 1]],
                                    late=copies[i - 1] if i else None))
            last = s.windows - 1
            q.act(lambda e: read_out(e, last % BANKS, slice(last * w, (last + 1) * w)),
                  after=[mm[-1], copies[-1]])
            q.barrier()
        self.bank_free = [None] * 8

    def wait_setup(self):
        for e in self.q.ENGINES:
            self.q.wait(e, [self.loaded()])

    def last_dve(self):
        return "vector", self.q.count["vector"]

    def load_nodes(self, x):
        s, q = self.s, self.q
        t = q.dve(lambda e: e.memset(x[:, s.nb - 1, :], 0.0))
        full = (s.nb - 1) * P
        xin = self.io["x"]
        self.load(x[:, 0:s.nb - 1, :], xin[0:full, :].rearrange("(b l) f -> l b f", l=P))
        self.load(x[0:s.last, s.nb - 1, :], xin[full:s.n, :], after=[t])

    def ln_factors(self, scope, x, after, scale=1.0):
        s, q = self.s, self.q
        stats = self.sb(scope, "ln_stats", [P, s.nb, 6])
        mv = self.sb(scope, "ln_mv", [P, s.nb, 2])
        rstd = self.sb(scope, "ln_rstd", [P, s.nb])
        nbias = self.sb(scope, "ln_nbias", [P, s.nb])
        for b in range(s.nb):
            t = q.dve(lambda e, b=b: e.bn_stats(stats[:, b, :], x[:, b, :]),
                      after=after[b:b + 1] if len(after) == s.nb else after)
        for b in range(s.nb):
            t = q.dve(lambda e, b=b: e.bn_aggr(mv[:, b, :], stats[:, b, :]), after=[t] if b == 0 else ())
        t = q.act(lambda e: e.activation(rstd[:, :], mv[:, :, 1], ACT.Sqrt, bias=self.eps[:, 0:1]), after=[t])
        t = q.dve(lambda e: e.reciprocal(rstd[:, :], rstd[:, :]), after=[t])
        if scale != 1.0:
            t = q.dve(lambda e: e.tensor_scalar(rstd[:, :], rstd[:, :], scale, None, ALU.mult), after=[t])
        t = q.dve(lambda e: e.scalar_tensor_tensor(nbias[:, :], mv[:, :, 0], -1.0, rstd[:, :],
                                                   ALU.mult, ALU.mult), after=[t])
        return rstd, nbias, t

    def ln_apply(self, y, x, rstd, nbias, func, after):
        q = self.q
        return [q.act(lambda e, b=b: e.activation(y[:, b, :], x[:, b, :], func, bias=nbias[:, b:b + 1],
                                                  scale=rstd[:, b:b + 1]), after=after)
                for b in range(self.s.nb)]

    def split(self, halves, y, rows, b, after):
        q = self.q
        t = q.act(lambda e: e.activation(halves[0:rows, b, 0:D], y, ACT.Copy), after=after)
        return q.dve(lambda e: e.tensor_tensor(halves[0:rows, b, D:2 * D], y, halves[0:rows, b, 0:D],
                                               ALU.subtract), after=[t])

    def hop(self, halves, ready, finish):
        s, q = self.s, self.q
        for b in range(s.nb):
            rows, i = s.rows(b), b % 8
            ps = self.bank[i][0:rows, 0:2 * D + 1]
            for k in range(s.nb):
                t = q.pe(lambda e, b=b, k=k, rows=rows, ps=ps: e.matmul(
                    ps, self.counts[:, k, b * P:b * P + rows], halves[:, k, :],
                    start=k == 0, stop=k == s.nb - 1),
                    after=[self.bank_free[i]] + list(ready) if k == 0 else ())
            self.bank_free[i] = finish(b, rows, self.bank[i], t)

    def layer0(self, x_out):
        s, q, io = self.s, self.q, self.io
        nc = s.nc
        cut = nc // 8
        assert cut * 8 == nc and cut <= 512
        with ExitStack() as scope:
            sb = self.sb
            ht = sb(scope, "ht", [P, s.nb * P])
            nodes = sb(scope, "nodes", [P, s.nb, D])
            qd = x_out[:, :, :].rearrange("p b f -> p (b f)")[:, 0:nc]
            w_msg = sb(scope, "w_msg", [P, D + 1])
            w_dst = sb(scope, "w_dst", [P, 1])
            b_msg = sb(scope, "b_msg", [P, D])
            b_att = sb(scope, "b_att", [P, 1])
            w_ih = sb(scope, "w_ih", [P, 3 * D])
            w_hh = sb(scope, "w_hh", [P, 3 * D])
            cols = sb(scope, "cols", [P, 8])
            bias = sb(scope, "bias", [P, 2])
            ps_src = sb(scope, "ps_src", [P, s.nb])
            self.load_nodes(nodes)
            for dst, src in ((w_msg[:, 0:D], io["L0_gnn_W_msg"]), (w_msg[:, D:D + 1], io["L0_gnn_W_att"][0:D, :]),
                             (w_dst[:, :], io["L0_gnn_W_att"][D:2 * D, :]),
                             (b_msg[:, :], io["L0_gnn_b_msg"].partition_broadcast(P)),
                             (b_att[:, :], io["L0_gnn_b_att"].partition_broadcast(P)),
                             (w_ih[:, :], io["L0_gnn_W_ih_t"]), (w_hh[:, :], io["L0_gnn_W_hh_t"]),
                             (cols[:, 0:3], io["L0_gnn_b_ih_t"]), (cols[:, 3:6], io["L0_gnn_b_hh_t"]),
                             (cols[:, 6:7], self.column("L0_gnn_gamma")), (cols[:, 7:8], self.column("L0_gnn_beta"))):
                self.load(dst, src)
            self.wait_setup()
            rstd, nbias, t = self.ln_factors(scope, nodes, ())
            h = self.ln_apply(nodes, nodes, rstd, nbias, ACT.Relu, [t])
            for b in range(s.nb):
                t = self.transpose_to(ht[:, b * P:(b + 1) * P], nodes[:, b, :], [h[b]])
            q.dve(lambda e: e.tensor_tensor(bias[:, :], cols[:, 0:2], cols[:, 3:5], ALU.add))
            ready = t
            for b in range(s.nb):
                i = self.next_bank()
                ps = self.bank[i]
                t = q.pe(lambda e, b=b, ps=ps: e.matmul(ps[:, 0:D + 1], ht[:, b * P:(b + 1) * P], w_msg[:, :],
                                                        start=True, stop=True), after=[ready, self.bank_free[i]])
                q.dve(lambda e, b=b, ps=ps: e.tensor_tensor(nodes[:, b, :], ps[:, 0:D], b_msg[:, :], ALU.add),
                      after=[t])
                self.bank_free[i] = q.dve(lambda e, b=b, ps=ps: e.tensor_tensor(
                    ps_src[:, b:b + 1], ps[:, D:D + 1], b_att[:, :], ALU.add), after=[t])
            messages = self.last_dve()
            for c in range(8):
                i = self.next_bank()
                ps = self.bank[i][:, 0:cut]
                t = q.pe(lambda e, c=c, ps=ps: e.matmul(ps, w_dst[:, 0:1].to_broadcast([P, P]),
                                                        ht[:, c * cut:(c + 1) * cut], start=True, stop=True),
                         after=[self.bank_free[i]])
                qd_done = self.bank_free[i] = q.act(lambda e, c=c, ps=ps: e.activation(
                    qd[:, c * cut:(c + 1) * cut], ps, ACT.Copy), after=[t])
            with ExitStack() as inner:
                ring, parts = 3, 4
                wide = nc // parts
                att = sb(inner, "att", [P, ring, wide])
                used = [None] * ring
                n = 0
                for k in range(s.nb):
                    for c in range(parts):
                        r = n % ring
                        n += 1
                        t = q.act(lambda e, k=k, c=c, r=r: e.activation(
                            att[:, r, :], qd[:, c * wide:(c + 1) * wide], ACT.Sigmoid, bias=ps_src[:, k:k + 1]),
                            after=[messages, qd_done, used[r]])
                        t = q.dve(lambda e, k=k, c=c, r=r: e.tensor_tensor(
                            att[:, r, :], att[:, r, :], self.counts[:, k, c * wide:(c + 1) * wide], ALU.mult),
                            after=[t])
                        for j in range(2):
                            i = 2 * c + j
                            used[r] = q.pe(lambda e, k=k, i=i, j=j, r=r: e.matmul(
                                self.bank[i][:, 0:cut], nodes[:, k, :], att[:, r, j * cut:(j + 1) * cut],
                                start=k == 0, stop=k == s.nb - 1),
                                after=[t, self.bank_free[i] if k == 0 else None])
                sums = used[r]
                agg = qd
                for c in range(8):
                    last_read = ("scalar", q.count["scalar"])
                    t = q.dve(lambda e, c=c: e.tensor_copy(agg[:, c * cut:(c + 1) * cut],
                                                           self.bank[c][:, 0:cut]), after=[sums, last_read])
                    self.bank_free[c] = t
                q.barrier()
            with ExitStack() as inner:
                gate = sb(inner, "gate", [P, 2, 3, cut])
                stats = sb(inner, "stats", [P, 8, 6])
                mv = sb(inner, "mv", [P, 4])
                new = nodes[:, :, :].rearrange("p b f -> p (b f)")
                free = {}
                for c in range(8):
                    cs = slice(c * cut, (c + 1) * cut)
                    g = c % 2
                    rb, zb, nb_, hb = (self.bank[4 * g + j][:, 0:cut] for j in range(4))
                    wait = [free.get(c - 2)]
                    for ps, j in ((rb, 0), (zb, 1)):
                        q.pe(lambda e, ps=ps, j=j, cs=cs: e.matmul(ps, w_ih[:, j * D:(j + 1) * D], agg[:, cs],
                                                                   start=True, stop=False), after=wait)
                        q.pe(lambda e, ps=ps, j=j, cs=cs: e.matmul(ps, w_hh[:, j * D:(j + 1) * D], ht[:, cs],
                                                                   start=False, stop=True))
                    q.pe(lambda e, ps=nb_, cs=cs: e.matmul(ps, w_ih[:, 2 * D:], agg[:, cs], start=True, stop=True))
                    t = q.pe(lambda e, ps=hb, cs=cs: e.matmul(ps, w_hh[:, 2 * D:], ht[:, cs],
                                                              start=True, stop=True))
                    r, z, m = (gate[:, g, j, :] for j in range(3))
                    d = r
                    a = q.act(lambda e, r=r, rb=rb: e.activation(r, rb, ACT.Sigmoid, bias=bias[:, 0:1]),
                              after=[t] + wait)
                    b = q.act(lambda e, z=z, zb=zb: e.activation(z, zb, ACT.Sigmoid, bias=bias[:, 1:2]))
                    t = q.dve(lambda e, m=m, hb=hb, r=r: e.scalar_tensor_tensor(m, hb, cols[:, 5:6], r,
                                                                                ALU.add, ALU.mult), after=[a])
                    t = q.dve(lambda e, m=m, nb_=nb_: e.tensor_tensor(m, m, nb_, ALU.add), after=[t])
                    t = q.act(lambda e, m=m: e.activation(m, m, ACT.Tanh, bias=cols[:, 2:3]), after=[t])
                    t = q.dve(lambda e, m=m, d=d, cs=cs: e.tensor_tensor(d, ht[:, cs], m, ALU.subtract), after=[t])
                    t = q.dve(lambda e, d=d, z=z: e.tensor_tensor(d, d, z, ALU.mult), after=[t, b])
                    t = q.dve(lambda e, d=d, m=m, cs=cs: e.tensor_tensor(new[:, cs], d, m, ALU.add), after=[t])
                    real = min(cut, s.n - c * cut)
                    t = q.dve(lambda e, c=c, real=real: e.bn_stats(stats[:, c, :], new[:, c * cut:c * cut + real]),
                              after=[t])
                    free[c] = t
                t = q.dve(lambda e: e.bn_aggr(mv[:, 0:2], stats[:, :, :].rearrange("p a b -> p (a b)")), after=[t])
                t = q.act(lambda e: e.activation(mv[:, 2:3], mv[:, 1:2], ACT.Sqrt, bias=self.eps[:, 0:1]), after=[t])
                t = q.dve(lambda e: e.reciprocal(mv[:, 2:3], mv[:, 2:3]), after=[t])
                t = q.dve(lambda e: e.tensor_tensor(mv[:, 2:3], mv[:, 2:3], cols[:, 6:7], ALU.mult), after=[t])
                t = q.dve(lambda e: e.scalar_tensor_tensor(mv[:, 3:4], mv[:, 0:1], -1.0, mv[:, 2:3],
                                                           ALU.mult, ALU.mult), after=[t])
                t = q.dve(lambda e: e.tensor_tensor(mv[:, 3:4], mv[:, 3:4], cols[:, 7:8], ALU.add), after=[t])
                for c in range(8):
                    cs = slice(c * cut, (c + 1) * cut)
                    t = q.act(lambda e, cs=cs: e.activation(new[:, cs], new[:, cs], ACT.Identity,
                                                            bias=mv[:, 3:4], scale=mv[:, 2:3]), after=[t])
                q.barrier()
            self.bank_free = [None] * 8
            self.add_transposed(x_out, new, ht, t)
            q.barrier()

    def add_transposed(self, x_out, yt, xbuf, after):
        s, q = self.s, self.q
        xs = xbuf[:, :].rearrange("p (b f) -> p b f", f=D)
        self.load_nodes(xs)
        t = q.dve(lambda e: e.memset(x_out[:, s.nb - 1, :], 0.0))
        for b in range(s.nb):
            rows = s.rows(b)
            self.transpose_to(None, yt[:, b * P:b * P + rows], [after], copy=lambda ps, tk, b=b, rows=rows: q.dve(
                lambda e: e.tensor_tensor(x_out[0:rows, b, :], ps, xs[0:rows, b, :], ALU.add),
                after=[tk, t, self.loaded()]))

    def column(self, name):
        return self.io[name].rearrange("(a b) -> a b", b=1)

    def degree(self, rdeg, b, rows, ps, token):
        q = self.q
        t = q.dve(lambda e: e.tensor_scalar(rdeg[0:rows, b:b + 1], ps[0:rows, 2 * D:2 * D + 1], 1.0, F16_SCALE,
                                            ALU.max, ALU.mult), after=[token])
        return q.dve(lambda e: e.reciprocal(rdeg[0:rows, b:b + 1], rdeg[0:rows, b:b + 1]), after=[t])

    def mean_rows(self, y, ps, rdeg, b, rows, token, tmp):
        q = self.q
        t = q.act(lambda e: e.activation(tmp, ps[0:rows, D:2 * D], ACT.Copy, scale=rdeg[0:rows, b:b + 1]),
                  after=[token])
        return q.dve(lambda e: e.scalar_tensor_tensor(y, ps[0:rows, 0:D], rdeg[0:rows, b:b + 1], tmp,
                                                      ALU.mult, ALU.add), after=[t])

    def halves_of_ln(self, scope, x, halves, hs):
        s, q = self.s, self.q
        rstd, nbias, t = self.ln_factors(scope, x, [self.last_dve()], F16_SCALE)
        h = []
        for b in range(s.nb + 1):
            if b < s.nb:
                h.append(q.act(lambda e, b=b: e.activation(hs[:, b, :], x[:, b, :], ACT.Relu,
                                                           bias=nbias[:, b:b + 1], scale=rstd[:, b:b + 1]), after=[t]))
            if b:
                self.split(halves, hs[:, b - 1, :], P, b - 1, [h[b - 1]])
        t = q.dve(lambda e: e.memset(halves[:, :, 2 * D:2 * D + 1], 1.0))
        return t

    def layer1(self, x, rdeg):
        s, q = self.s, self.q
        with ExitStack() as scope:
            sb = self.sb
            halves = [sb(scope, "halves", [P, s.nb, 2 * D + 1], F16) for _ in range(2)]
            with ExitStack() as inner:
                hs = sb(inner, "hs", [P, s.nb, D])
                q.pool(lambda e: e.memset(halves[1][:, :, :], 0.0))
                ready = self.halves_of_ln(inner, x, halves[0], hs)
                q.barrier()
            tmp = sb(scope, "tmp", [P, 4, 2, D])
            free = [None] * 4
            cuts = s.nb
            share = -(-s.quads // cuts)
            part = sb(scope, "edge_part", [P, 2, share, P])
            sums = sb(scope, "edge_sums", [P, cuts])
            lanes = [q.lane(f"edge_part{i}") for i in range(2)]
            by_row = self.io["edge_t"].rearrange("i r e -> r i e")
            summed = []

            def sum_part(c):
                lo, hi = c * share, min((c + 1) * share, s.quads)
                if lo >= hi:
                    return
                piece = part[:, c % 2, 0:hi - lo, :]
                t = q.dma("sync", lanes[c % 2], lambda e: e.dma_start(piece, by_row[:, lo:hi, :]),
                          after=[summed[c - 2]] if c >= 2 else ())
                summed.append(q.act(lambda e: e.activation(piece, piece, ACT.Copy, accum_out=sums[:, c:c + 1]),
                                    after=[t]))
            for n in range(3):
                a, out = halves[n % 2], halves[(n + 1) % 2]

                def finish(b, rows, ps, token, n=n, out=out):
                    k = b % 4
                    if n == 0:
                        token = self.degree(rdeg, b, rows, ps, token)
                    t0, t1 = tmp[0:rows, k, 0, :], tmp[0:rows, k, 1, :]
                    q.wait("scalar", [free[k]])
                    t = self.mean_rows(t1, ps, rdeg, b, rows, token, t0)
                    if n == 1:
                        sum_part(b)
                    if n < 2:
                        u = q.dve(lambda e: e.tensor_scalar(t1, t1, F16_SCALE, None, ALU.mult), after=[t])
                        free[k] = self.split(out, t1, rows, b, [u])
                    else:
                        free[k] = q.dve(lambda e: e.tensor_tensor(x[0:rows, b, :], x[0:rows, b, :], t1, ALU.add),
                                        after=[t])
                    return t
                self.hop(a, [ready], finish)
                ready = self.last_dve()
            q.dve(lambda e: e.tensor_reduce(self.edge_sum[:, :], sums[:, 0:len(summed)], AX.X, ALU.add),
                  after=[summed[-1]])
            q.barrier()
            self.bank_free = [None] * 8

    def layer2(self, x, rdeg):
        s, q, io = self.s, self.q, self.io
        cut = s.nc // 8
        with ExitStack() as scope:
            sb = self.sb
            ht = sb(scope, "ht2", [P, s.nb * P])
            mt = sb(scope, "mt", [P, s.nb * P])
            cols = sb(scope, "cols2", [P, 9])
            fac = sb(scope, "fac", [P, 2, 2])
            names = ["gamma1", "beta1", "rm1", "rv1", "gamma2", "beta2", "rm2", "rv2", "b_self"]
            for j, name in enumerate(names):
                self.load(cols[:, j:j + 1], self.column("L2_gnn_" + name))
            self.wait_setup()
            for j in range(2):
                g, b, m, v = (cols[:, 4 * j + i:4 * j + i + 1] for i in range(4))
                f, sh = fac[:, j, 0:1], fac[:, j, 1:2]
                t = q.act(lambda e, f=f, v=v: e.activation(f, v, ACT.Sqrt, bias=self.eps[:, 0:1]))
                t = q.dve(lambda e, f=f: e.reciprocal(f, f), after=[t])
                t = q.dve(lambda e, f=f, g=g: e.tensor_tensor(f, f, g, ALU.mult), after=[t])
                t = q.dve(lambda e, f=f, m=m, sh=sh: e.scalar_tensor_tensor(sh, m, -1.0, f, ALU.mult, ALU.mult),
                          after=[t])
                t = q.dve(lambda e, b=b, sh=sh: e.tensor_tensor(sh, sh, b, ALU.add), after=[t])
            t = q.dve(lambda e: e.tensor_tensor(fac[:, 1, 1:2], fac[:, 1, 1:2], cols[:, 8:9], ALU.add), after=[t])
            with ExitStack() as inner:
                halves = sb(inner, "halves", [P, s.nb, 2 * D + 1], F16)
                hs = mt[:, :].rearrange("p (b f) -> p b f", f=D)
                ready = self.halves_of_ln(inner, x, halves, hs)
                for b in range(s.nb):
                    t = self.transpose_to(ht[:, b * P:(b + 1) * P], hs[:, b, :], [ready])
                q.barrier()
                tmp = sb(inner, "tmp", [P, 2, 2, D])
                free = [None] * 2

                def finish(b, rows, ps, token):
                    k = b % 2
                    t0, t1 = tmp[0:rows, k, 0, :], tmp[0:rows, k, 1, :]
                    q.wait("scalar", [free[k]])
                    t = self.mean_rows(t1, ps, rdeg, b, rows, token, t0)
                    pend.append((b, rows, k, t1, t))
                    if len(pend) > 1:
                        flush()
                    return t

                def flush():
                    b, rows, k, t1, t = pend.pop(0)
                    ps = self.bank[b % 8][:, 384:384 + rows]
                    t = q.pe(lambda e: e.transpose(ps, t1, self.ident[0:rows, 0:rows]), after=[t])
                    t = q.dve(lambda e: e.tensor_copy(mt[:, b * P:b * P + rows], ps), after=[t])
                    free[k] = self.bank_free[b % 8] = t
                pend = []
                self.hop(halves, [ready], finish)
                flush()
                q.dve(lambda e: e.memset(mt[:, s.n:], 0.0))
                q.barrier()
            with ExitStack() as inner:
                mid = sb(inner, "mid", [P, 2, 2, cut])
                w = sb(inner, "w2", [P, 3, D])
                for j, name in enumerate(("W1", "W2", "W_self")):
                    self.load(w[:, j, :], io[f"L2_gnn_{name}_t"])
                self.wait_setup()
                free = {}
                for c in range(8):
                    cs, g = slice(c * cut, (c + 1) * cut), c % 2
                    p1, p2, p3 = (self.bank[4 * g + j][:, 0:cut] for j in range(3))
                    wait = [free.get(c - 2)]
                    t = q.pe(lambda e, p=p1, cs=cs: e.matmul(p, w[:, 0, :], mt[:, cs], start=True, stop=True),
                             after=wait)
                    u = q.pe(lambda e, p=p3, cs=cs: e.matmul(p, w[:, 2, :], ht[:, cs], start=True, stop=True))
                    t = q.act(lambda e, g=g, p=p1: e.activation(mid[:, g, 0, :], p, ACT.Relu, bias=fac[:, 0, 1:2],
                                                                scale=fac[:, 0, 0:1]), after=[t] + wait)
                    v = q.act(lambda e, g=g, p=p3: e.activation(mid[:, g, 1, :], p, ACT.Identity,
                                                                bias=fac[:, 1, 1:2], scale=1.0 / F16_SCALE),
                              after=[u])
                    t = q.pe(lambda e, g=g, p=p2: e.matmul(p, w[:, 1, :], mid[:, g, 0, :], start=True, stop=True),
                             after=[t])
                    free[c] = t = q.dve(lambda e, g=g, p=p2, cs=cs: e.scalar_tensor_tensor(
                        mt[:, cs], p, fac[:, 1, 0:1], mid[:, g, 1, :], ALU.mult, ALU.add), after=[t, v])
                q.barrier()
            self.bank_free = [None] * 8
            for b in range(s.nb):
                rows = s.rows(b)
                self.transpose_to(None, mt[:, b * P:b * P + rows], [t], copy=lambda ps, tk, b=b, rows=rows: q.dve(
                    lambda e: e.tensor_tensor(x[0:rows, b, :], x[0:rows, b, :], ps, ALU.add), after=[tk]))
            q.barrier()

    def layer3(self, x):
        s, q, io = self.s, self.q, self.io
        groups = s.groups
        self.xl = self.dram("x_l", (s.n, D))
        self.gathered = self.dram("gathered", (groups, P, 4 * D))
        with ExitStack() as scope:
            sb = self.sb
            h = sb(scope, "h", [P, s.nb, D])
            alpha = sb(scope, "alpha", [P, 4 * s.run, 16, HEADS])
            loop = sb(scope, "loop", [P, 4 * s.run, 16, HEADS])
            rstd, nbias, t = self.ln_factors(scope, x, [self.last_dve()])
            hd = self.ln_apply(h, x, rstd, nbias, ACT.Relu, [t])
            with ExitStack() as inner:
                xr = self.project(inner, h, hd)
                self.logits(xr, alpha, loop)
                q.barrier()
            self.bank_free = [None] * 8
            ut = sb(scope, "ut2", [P, s.nb * P])
            rows = sb(scope, "rows2", [P, 2, D])
            own_xl = ut[:, :].rearrange("p (b f) -> p b f", f=D)
            full = (s.nb - 1) * P
            t = q.dve(lambda e: e.memset(own_xl[:, s.nb - 1, :], 0.0))
            lane = q.lane("feed_forward_loads")
            for to, what in ((own_xl[0:s.last, s.nb - 1, :], self.xl[full:s.n, :]),
                             (own_xl[:, 0:s.nb - 1, :], self.xl[0:full, :].rearrange("(b l) f -> l b f", l=P)),
                             (rows[:, 0, :], io["L3_gnn_bias"].partition_broadcast(P)),
                             (rows[:, 1, :], io["L3_gnn_b2"].partition_broadcast(P))):
                loaded = q.dma("sync", lane, lambda e, to=to, what=what: e.dma_start(to, what), after=[t])
            q.pool(lambda e: e.tensor_tensor(x[:, :, :], x[:, :, :], rows[:, 1:2, :].to_broadcast([P, s.nb, D]), ALU.add),
                   after=[loaded])
            q.pool(lambda e: e.tensor_tensor(h[:, :, :], h[:, :, :], rows[:, 0:1, :].to_broadcast([P, s.nb, D]), ALU.add))
            acc = sb(scope, "acc", [P, s.nb, D + 2 * HEADS])
            q.pool(lambda e: e.memset(acc[:, :, :], 0.0))
            self.softmax_numerators(alpha, loop)
            self.weighted_sums(alpha, loop, acc)
            q.barrier()
            self.bank_free = [None] * 8
            self.feed_forward(x, h, acc, ut)

    def ln_affine_t(self, scope, ut, x, gain, shift, after):
        s, q = self.s, self.q
        tmp = self.sb(scope, "ln_rows", [P, s.nb, D])
        rstd, nbias, t = self.ln_factors(scope, x, after)
        rows = self.ln_apply(tmp, x, rstd, nbias, ACT.Identity, [t])
        return [self.transpose_to(None, tmp[:, b, :], [rows[b]], copy=lambda ps, tk, b=b: q.dve(
            lambda e: e.tensor_scalar(ut[:, b * P:(b + 1) * P], ps, gain, shift, ALU.mult, ALU.add),
            after=[tk, self.loaded()])) for b in range(s.nb)]

    def project(self, scope, h, hd):
        s, q, io = self.s, self.q, self.io
        xr = self.sb(scope, "x_r", [P, s.nb, D + HEADS])
        with ExitStack() as inner:
            sb = self.sb
            w = sb(inner, "w_lr", [P, 2 * D])
            cols = sb(inner, "cols3", [P, 2])
            ut = sb(inner, "ut", [P, s.nb * P])
            xl = sb(inner, "xl", [P, s.nb, D])
            w_e = sb(inner, "w_e_rows", [P, D])
            att = sb(inner, "att_rows", [P, D])
            mean = sb(inner, "mean", [P, D])
            z = sb(inner, "z_loop", [P, s.nb, D])
            for k in range(4):
                self.load(w_e[k * DE:(k + 1) * DE, :], io["L3_gnn_W_e"])
            self.load(att[:, :], io["att_row"].partition_broadcast(P))
            self.load(w[:, 0:D], io["L3_gnn_W_l"])
            self.load(w[:, D:2 * D], io["L3_gnn_W_r"])
            self.load(cols[:, 0:1], self.column("L3_gnn_ln1_g"))
            self.load(cols[:, 1:2], self.column("L3_gnn_ln1_b"))
            self.wait_setup()
            i = self.next_bank()
            pm = self.bank[i][:, 0:D]
            u = q.pe(lambda e: e.matmul(pm, self.edge_sum[:, 0:1].to_broadcast([P, P]), w_e[:, :],
                                        start=True, stop=True), after=[self.bank_free[i]])
            u = self.bank_free[i] = q.dve(lambda e: e.tensor_scalar(mean[:, :], pm, 1.0 / s.edges, None, ALU.mult),
                                          after=[u])
            q.wait("vector", [u])
            turned = self.ln_affine_t(inner, ut, h, cols[:, 0:1], cols[:, 1:2], hd)
            lane = q.lane("x_l_stores")
            part = 5
            for b in range(s.nb):
                i = self.next_bank()
                ps = self.bank[i]
                t = q.pe(lambda e, b=b, ps=ps: e.matmul(ps[:, 0:2 * D], ut[:, b * P:(b + 1) * P], w[:, :],
                                                        start=True, stop=True), after=[turned[b], self.bank_free[i]])
                q.dve(lambda e, b=b, ps=ps: e.tensor_copy(xl[:, b, :], ps[:, 0:D]), after=[t])
                t = self.bank_free[i] = q.dve(lambda e, b=b, ps=ps: e.tensor_copy(xr[:, b, 0:D], ps[:, D:2 * D]))
                if (b + 1) % part and b + 1 < s.nb:
                    continue
                lo = b // part * part
                full = min(b + 1, s.nb - 1)
                q.dma("sync", lane, lambda e, lo=lo, full=full: e.dma_start(
                    self.xl[lo * P:full * P, :].rearrange("(b l) f -> l b f", l=P), xl[:, lo:full, :]), after=[t])
                if b + 1 == s.nb:
                    q.dma("sync", lane, lambda e: e.dma_start(self.xl[full * P:s.n, :], xl[0:s.last, full, :]))
                zs, few = z[:, lo:b + 1, :], b + 1 - lo
                q.dve(lambda e, zs=zs, lo=lo, b=b: e.tensor_tensor(zs, xl[:, lo:b + 1, :], xr[:, lo:b + 1, 0:D],
                                                                   ALU.add), after=[t])
                t = self.last_dve()
                t = q.dve(lambda e, zs=zs, few=few: e.tensor_tensor(zs, zs, self.rows_of(mean, few), ALU.add),
                          after=[t])
                t = q.dve(lambda e, zs=zs: e.scalar_tensor_tensor(zs, zs, NEG_SLOPE, zs, ALU.mult, ALU.max),
                          after=[t])
                t = q.dve(lambda e, zs=zs, few=few: e.tensor_tensor(zs, zs, self.rows_of(att, few), ALU.mult),
                          after=[t])
                q.dve(lambda e, zs=zs, lo=lo, b=b: e.tensor_reduce(
                    xr[:, lo:b + 1, D:], zs.rearrange("p b (h c) -> p b h c", c=CH), AX.X, ALU.add), after=[t])
            q.barrier()
        return xr

    def rows_of(self, row, blocks):
        return row[:, :].rearrange("p (o f) -> p o f", o=1).to_broadcast([P, blocks, D])

    def logits(self, xr, alpha, loop):
        s, q, io = self.s, self.q, self.io
        groups = s.groups
        with ExitStack() as scope:
            sb = self.sb
            src = sb(scope, "src", [P, 4 * s.padded], I32)
            regs = sb(scope, "regs", [1, 2, s.padded], I32)
            w_e = sb(scope, "w_e", [P, 4, D + HEADS])
            att = sb(scope, "att", [P, D])
            place = sb(scope, "place", [P, 16])
            slots, ahead = 6, 4
            rows = sb(scope, "rows", [P, slots, 4 * D])
            edges = sb(scope, "edges", [P, slots, P])
            rel = sb(scope, "rel", [P, slots, 4 * P], I16)
            hot = sb(scope, "hot", [P, 2, 4 * P])
            z = sb(scope, "z", [P, 2, 4 * D])
            leaky = sb(scope, "leaky", [P, 2, 4 * D])
            self.load(src[:, :], self.e_src)
            self.load(regs[:, :, :], self.e_regs[:, 0:s.padded].rearrange("(o a) n -> o a n", o=1))
            t = q.dve(lambda e: e.memset(w_e[:, :, :], 0.0))
            for k in range(4):
                self.load(w_e[k * DE:(k + 1) * DE, k, 0:D], io["L3_gnn_W_e"], after=[t])
            self.load(att[:, :], io["att_row"].partition_broadcast(P))
            self.load(place[:, :], io["c_step"])
            self.wait_setup()
            for m in (alpha, loop):
                for g in range(groups, s.padded):
                    q.dve(lambda e, m=m, g=g: e.memset(self.places(m, g), 0.0))
            quad = Registers(self.nc, q, "sync", regs[0:1, 0, :], groups, s.quads, [self.loaded()])
            block = Registers(self.nc, q, "tensor", regs[0:1, 1, :], groups, s.nb - 1, [self.loaded()])
            got = [q.lane(f"rows{i}") for i in range(slots)]
            edge_lane = [q.lane(f"edges{i}") for i in range(slots)]
            rel_lane = [q.lane(f"rel{i}") for i in range(slots)]
            kept = [q.lane(f"kept{i}") for i in range(slots)]
            sums, hots, products, used, parts, loops = [], [], [], [], [], []
            stores = []

            def fetch(g):
                r = g % slots
                old = g - slots
                for k in range(4):
                    v = 4 * g + k
                    rows_in[g] = q.dma("gpsimd", got[r], lambda e, v=v, r=r, k=k: e.indirect_dma_start(
                        rows[:, r, k * D:(k + 1) * D], None, self.xl,
                        bass.IndirectOffsetOnAxis(ap=src[:, v:v + 1], axis=0)),
                        after=[sums[old], stores[old]] if old >= 0 else ())
                quad.prefetch(g)
                edges_in[g] = q.dma("sync", edge_lane[r], lambda e, g=g, r=r: e.dma_start(
                    edges[:, r, :], io["edge_t"][bass.ds(quad.at(g), 1), :, :].rearrange("o r e -> (o r) e")),
                    after=[products[old]] if old >= 0 else ())
                rel_in[g] = q.dma("sync", rel_lane[r], lambda e, g=g, r=r: e.dma_start(
                    rel[:, r, :], self.e_rel_rows[g, :].partition_broadcast(P)),
                    after=[hots[old]] if old >= 0 else ())

            rows_in, edges_in, rel_in, here = {}, {}, {}, {}
            for g in range(ahead):
                fetch(g)
            four = "p (b v f) -> p b v f"
            wide = D + HEADS

            def pair_of(g):
                return self.psum[:, 2 * (g % 4):2 * (g % 4) + 2, 0:2 * wide].rearrange(
                    "p b (v f) -> p b v f", f=wide)

            def multiply(g):
                r, two, pair = g % slots, g % 2, pair_of(g)
                hots.append(q.dve(lambda e: e.tensor_scalar(
                    hot[:, two, :], rel[:, r, :], place[:, 0:1], None, ALU.is_equal),
                    after=[rel_in[g], products[g - 2] if g >= 2 else None]))
                block.prefetch(g)
                q.wait("tensor", [hots[g], edges_in[g]] + ([sums[g - 4], loops[g - 4]] if g >= 4 else []))
                q.step("tensor", lambda e: here.update({g: xr[:, bass.ds(block.at(g), 1), :].rearrange(
                    "p o f -> p (o f)")}))
                for k in range(4):
                    q.pe(lambda e, k=k: e.matmul(pair[:, k // 2, k % 2, :], hot[:, two, k * P:(k + 1) * P],
                                                 here[g], start=True, stop=False))
                    t = q.pe(lambda e, k=k: e.matmul(pair[:, k // 2, k % 2, :], edges[:, r, :], w_e[:, k, :],
                                                     start=False, stop=True))
                products.append(t)

            multiply(0)
            for g in range(groups):
                r, two, pair = g % slots, g % 2, pair_of(g)
                if g + 1 < groups:
                    multiply(g + 1)
                sums.append(q.dve(lambda e, two=two, r=r, pair=pair: e.tensor_tensor(
                    z[:, two, :].rearrange(four, b=2, f=D), pair[:, :, :, 0:D],
                    rows[:, r, :].rearrange(four, b=2, f=D), ALU.add),
                    after=[products[g], rows_in[g], parts[g - 2] if g >= 2 else None]))
                loops.append(q.act(lambda e, g=g, pair=pair: e.activation(
                    self.places(loop, g).rearrange("p (b v) h -> p b v h", b=2), pair[:, :, :, D:], ACT.Copy),
                    after=[sums[g]]))
                stores.append(q.dma("sync", kept[r], lambda e, g=g, r=r: e.dma_start(
                    self.gathered[g, :, :], rows[:, r, :]), after=[rows_in[g]]))
                if g >= 1:
                    self.head_sums(alpha, leaky, att, g - 1, parts, used)
                parts.append(q.dve(lambda e, two=two: e.scalar_tensor_tensor(
                    leaky[:, two, :], z[:, two, :], NEG_SLOPE, z[:, two, :], ALU.mult, ALU.max),
                    after=[sums[g], used[g - 2] if g >= 2 else None]))
                if g + ahead < groups:
                    fetch(g + ahead)
            self.head_sums(alpha, leaky, att, groups - 1, parts, used)
            q.barrier()

    def head_sums(self, alpha, leaky, att, g, parts, used):
        q, two = self.q, g % 2
        view = leaky[:, two, :].rearrange("p (v f) -> p v f", f=D)
        t = q.dve(lambda e: e.tensor_tensor(view, view, att[:, :].rearrange("p (o f) -> p o f", o=1)
                                            .to_broadcast([P, 4, D]), ALU.mult), after=[parts[g]])
        used.append(q.dve(lambda e: e.tensor_reduce(
            self.places(alpha, g),
            leaky[:, two, :].rearrange("p (v h c) -> p v h c", v=4, c=CH), AX.X, ALU.add), after=[t]))

    def places(self, alpha, g):
        c, at = divmod(g, self.s.run)
        return alpha[:, 4 * at:4 * at + 4, c, :]

    def turn_tile(self, g, dst, src, last, after=()):
        on = self.q.act if g % 2 else self.q.dve
        move = (lambda e, ps: e.activation(dst, ps, ACT.Copy)) if g % 2 else (lambda e, ps: e.tensor_copy(dst, ps))
        return last + [self.transpose_to(dst, src, list(after), copy=lambda ps, t: on(
            lambda e: move(e, ps), after=[t]))]

    def softmax_numerators(self, alpha, loop):
        s, q = self.s, self.q
        tiles = 4 * s.run
        n = tiles * P
        with ExitStack() as scope:
            sb = self.sb
            top = sb(scope, "top", [P, n])
            trial = sb(scope, "trial", [P, n])
            new = sb(scope, "new", [P, 2, n], BF16)
            carry = sb(scope, "carry", [P, 2])
            row = sb(scope, "row", [1, 2, P])
            any_new = sb(scope, "any_new", [1, 2, P])
            begins = sb(scope, "begins", [1, 2, 16])
            fresh = []
            for j in range(2):
                lane = q.lane(f"new_rows{j}")
                for c in range(16):
                    t = q.dma("sync", lane, lambda e, c=c, j=j: e.dma_start(
                        new[8 * c:8 * c + 8, j, :], self.e_new[j][c * n:(c + 1) * n].partition_broadcast(8)))
                fresh.append(t)
            self.load(any_new[:, :, :], self.e_any_new.rearrange("(o a) n -> o a n", o=1))

            def flat(m):
                return m[:, :, :, :].rearrange("p g c h -> p (g c h)")

            def tile(m, g):
                return m[:, g, :, :].rearrange("p c h -> p (c h)")
            a, own = flat(alpha), flat(loop)
            turned = [None, None]
            for g in range(tiles):
                turned = self.turn_tile(g, tile(alpha, g), tile(alpha, g), turned[1:])
            own_turned = None
            for g in range(tiles):
                own_turned = self.transpose_to(None, tile(loop, g), [], copy=lambda ps, tk, g=g: q.act(
                    lambda e: e.activation(tile(loop, g), ps, ACT.Copy), after=[tk]))
            self.wait_setup()
            q.dve(lambda e: e.tensor_reduce(begins[:, :, :], any_new[:, :, :].rearrange(
                "o j (c k) -> o j c k", k=P // 16), AX.X, ALU.min))
            for back in (False, True):
                source = top[:, :] if back else a

                def scan(start, after, to, back=back, source=source):
                    flip = (lambda m: m[:, ::-1]) if back else (lambda m: m)
                    return q.dve(lambda e: e.tensor_tensor_scan(flip(to), flip(new[:, int(back), :]), flip(source),
                                                                start, ALU.add, ALU.max), after=after)
                at = slice(0, 1) if back else slice(n - 1, n)
                t = scan(NONE, turned + [fresh[back]], trial[:, :])
                t = q.dve(lambda e, at=at: e.tensor_copy(carry[:, 0:1], trial[:, at]), after=[t])
                t = self.transpose_to(row[:, 0, :], carry[:, 0:1], [t])
                t = q.dve(lambda e: e.memset(row[:, 1, :], NONE), after=[t])
                for h in range(HEADS):
                    def of(m, back=back):
                        return m[:, ::-1] if back else m
                    last = row[:, 0, :].rearrange("p (c h) -> p h c", h=HEADS)[:, h, :]
                    t = q.dve(lambda e, of=of, last=last, back=back: e.tensor_tensor_scan(
                        of(last), of(begins[:, int(back), :]), of(last), NONE, ALU.add, ALU.max), after=[t])
                if back:
                    t = q.dve(lambda e: e.tensor_copy(row[:, 1, 0:P - HEADS], row[:, 0, HEADS:P]), after=[t])
                else:
                    t = q.dve(lambda e: e.tensor_copy(row[:, 1, HEADS:P], row[:, 0, 0:P - HEADS]), after=[t])
                t = self.transpose_to(carry[:, 1:2], row[:, 1, :], [t])
                t = scan(carry[:, 1:2], [t], top[:, :])
                turned = [t]
            cuts = 4
            share = tiles // cuts
            done = []

            def turn_back(c):
                for m, ready in zip((alpha, loop), done[c]):
                    turned = [ready, ready]
                    for g in range(c * share, (c + 1) * share):
                        turned = self.turn_tile(g, tile(m, g), tile(m, g), turned[1:], [ready])
            for c in range(cuts):
                s_ = slice(c * share * P, (c + 1) * share * P)
                m = q.dve(lambda e, s_=s_: e.tensor_tensor(top[:, s_], top[:, s_], own[:, s_], ALU.max),
                          after=[t, own_turned])
                u = q.dve(lambda e, s_=s_: e.tensor_tensor(own[:, s_], own[:, s_], top[:, s_], ALU.subtract),
                          after=[m])
                u = q.act(lambda e, s_=s_: e.activation(own[:, s_], own[:, s_], ACT.Exp), after=[u])
                weights = q.dve(lambda e, s_=s_: e.tensor_tensor(a[:, s_], a[:, s_], top[:, s_], ALU.subtract),
                                after=[m])
                weights = q.act(lambda e, s_=s_: e.activation(a[:, s_], a[:, s_], ACT.Exp), after=[weights])
                u = q.dve(lambda e, s_=s_: e.scalar_tensor_tensor(own[:, s_], new[:, 0, s_], 0.0, own[:, s_],
                                                                  ALU.is_lt, ALU.mult), after=[u])
                done.append((weights, u))
                if c:
                    turn_back(c - 1)
            turn_back(cuts - 1)
            q.barrier()
        self.bank_free = [None] * 8

    def weighted_sums(self, alpha, loop, acc):
        s, q, io = self.s, self.q, self.io
        groups = s.groups
        with ExitStack() as scope:
            sb = self.sb
            slots, ahead, deep = 6, 4, 4
            wide = D + 2 * HEADS
            rows = sb(scope, "rows", [P, slots, 4 * D])
            both = sb(scope, "both", [P, deep, 4, wide])
            hot = sb(scope, "hot", [P, deep, 4, P])
            rel = sb(scope, "rel", [P, 4 * s.padded])
            win = sb(scope, "win", [1, s.padded], I32)
            iota = self.load_iota(scope)
            self.load(rel[:, :], self.e_rel)
            self.load(win[:, :], self.e_regs[1:2, 0:s.padded])
            minus_rel = sb(scope, "minus_rel", [P, 4 * s.padded])
            apart = sb(scope, "apart", [P, 2, P])
            self.wait_setup()
            minus = q.dve(lambda e: e.tensor_scalar(minus_rel[:, :], rel[:, :], -1.0, None, ALU.mult))
            block = Registers(self.nc, q, "vector", win[0:1, :], groups, s.nb - 1, [self.loaded()])
            lane = [q.lane(f"again{i}") for i in range(slots)]
            weighted, products, added, rows_in = [], [], [None], {}

            def fetch(g):
                rows_in[g] = q.dma("sync", lane[g % slots], lambda e: e.dma_start(
                    rows[:, g % slots, :], self.gathered[g, :, :]),
                    after=[weighted[g - slots]] if g >= slots else ())
            for g in range(ahead):
                fetch(g)

            def add(g):
                ps = self.bank[g % 8][:, 0:wide]
                block.prefetch(g)

                def put(e):
                    at = acc[:, bass.ds(block.at(g), 1), :].rearrange("p o f -> p (o f)")
                    return e.tensor_tensor(at, at, ps, ALU.add)
                added.append(q.dve(put, after=[products[g], added[-1]]))

            far = {}

            def find_apart(g):
                far[g] = q.act(lambda e: e.activation(apart[:, g % 2, :], iota[:, :], ACT.Abs,
                                                      bias=minus_rel[:, 4 * g + 3:4 * g + 4]),
                               after=[minus, hots_by_act[g - 2] if g >= 2 else None])
            hots_by_act = []
            find_apart(0)
            for g in range(groups):
                at = g % deep
                old = products[g - deep] if g >= deep else None
                w = self.places(alpha, g)
                q.act(lambda e, at=at, w=w: e.activation(both[:, at, :, D:D + HEADS], w, ACT.Copy), after=[old])
                w = self.places(loop, g)
                q.act(lambda e, at=at, w=w: e.activation(both[:, at, :, D + HEADS:], w, ACT.Copy))
                hots = [q.on(name, lambda e, k=k, at=at, g=g: e.tensor_scalar(
                    hot[:, at, k, :], iota[:, :], rel[:, 4 * g + k:4 * g + k + 1], None, ALU.is_equal),
                    after=[old]) for k, name in enumerate(("gpsimd", "gpsimd" if g % 5 else "vector", "vector"))]
                hots_by_act.append(q.act(lambda e, at=at, g=g: e.activation(
                    hot[:, at, 3, :], apart[:, g % 2, :], ACT.Relu, bias=1.0, scale=-1.0), after=[far[g]]))
                if g + 1 < groups:
                    find_apart(g + 1)
                weighted.append(q.dve(lambda e, at=at, g=g: e.tensor_tensor(
                    both[:, at, :, 0:D].rearrange("p v (h c) -> p v h c", c=CH),
                    rows[:, g % slots, :].rearrange("p (v h c) -> p v h c", h=HEADS, c=CH),
                    self.places(alpha, g).rearrange("p v (h o) -> p v h o", o=1)
                    .to_broadcast([P, 4, HEADS, CH]), ALU.mult), after=[rows_in[g], old]))
                for k in range(4):
                    t = q.pe(lambda e, at=at, k=k, g=g: e.matmul(
                        self.bank[g % 8][:, 0:wide], hot[:, at, k, :], both[:, at, k, :],
                        start=k == 0, stop=k == 3),
                        after=[weighted[g], hots[0], hots[1], hots[2], hots_by_act[g],
                               added[g - 8 + 1] if g >= 8 else None])
                products.append(t)
                if g >= 2:
                    add(g - 2)
                if g + ahead < groups:
                    fetch(g + ahead)
            add(groups - 2)
            add(groups - 1)
            q.barrier()

    def feed_forward(self, x, h, acc, ut):
        s, q, io = self.s, self.q, self.io
        with ExitStack() as scope:
            sb = self.sb
            w1 = sb(scope, "w1", [P, 2 * D])
            w2 = sb(scope, "w2f", [P, 2, D])
            cols = sb(scope, "cols4", [P, 4])
            den = sb(scope, "den", [P, s.nb, HEADS])
            mid = sb(scope, "mid4", [P, 2, s.nb * P])
            self.load(w1[:, :], io["L3_gnn_W1"])
            self.load(w2[:, :, :], io["L3_gnn_W2"].rearrange("(j k) f -> k j f", k=P))
            self.load(cols[:, 0:1], self.column("L3_gnn_ln2_g"))
            self.load(cols[:, 1:2], self.column("L3_gnn_ln2_b"))
            self.load(cols[:, 2:4], io["L3_gnn_b1_t"])
            self.wait_setup()
            weights, own = acc[:, :, D:D + HEADS], acc[:, :, D + HEADS:]
            t = q.dve(lambda e: e.tensor_scalar(den[:, :, :], weights, 0.0, None, ALU.is_equal))
            t = q.dve(lambda e: e.tensor_tensor(own, own, den[:, :, :], ALU.add), after=[t])
            t = q.dve(lambda e: e.tensor_tensor(den[:, :, :], weights, own, ALU.add), after=[t])
            t = q.dve(lambda e: e.tensor_scalar(den[:, :, :], den[:, :, :], DENOM_EPS, None, ALU.add), after=[t])
            t = q.dve(lambda e: e.reciprocal(den[:, :, :], den[:, :, :]), after=[t])

            def per_head(m):
                return m.rearrange("p b (h o) -> p b h o", o=1).to_broadcast([P, s.nb, HEADS, CH])
            sums = acc[:, :, 0:D].rearrange("p b (h c) -> p b h c", c=CH)
            own_rows = ut[:, :].rearrange("p (b h c) -> p b h c", h=HEADS, c=CH)
            u = q.dve(lambda e: e.tensor_tensor(own_rows, own_rows, per_head(own), ALU.mult), after=[t])
            u = q.dve(lambda e: e.tensor_tensor(sums, sums, own_rows, ALU.add), after=[u])
            u = q.dve(lambda e: e.tensor_tensor(sums, sums, per_head(den[:, :, :]), ALU.mult), after=[u])
            u = q.dve(lambda e: e.tensor_tensor(h[:, :, :], h[:, :, :], acc[:, :, 0:D], ALU.add), after=[u])
            turned = self.ln_affine_t(scope, ut, h, cols[:, 0:1], cols[:, 1:2], [u])
            u = q.dve(lambda e: e.tensor_tensor(x[:, :, :], x[:, :, :], h[:, :, :], ALU.add))
            wide = 400
            assert wide * 8 == s.nb * P
            mids = []
            for c in range(8):
                for j in range(2):
                    i = self.next_bank()
                    ps = self.bank[i][:, 0:wide]
                    tk = q.pe(lambda e, c=c, j=j, ps=ps: e.matmul(
                        ps, w1[:, j * D:(j + 1) * D], ut[:, c * wide:(c + 1) * wide], start=True, stop=True),
                        after=[turned[((c + 1) * wide - 1) // P], self.bank_free[i]])
                    m = self.bank_free[i] = q.act(lambda e, c=c, j=j, ps=ps: e.activation(
                        mid[:, j, c * wide:(c + 1) * wide], ps, ACT.Gelu, bias=cols[:, 2 + j:3 + j]), after=[tk])
                mids.append(m)
            for b in range(s.nb):
                i = self.next_bank()
                ps = self.bank[i][:, 0:D]
                for j in range(2):
                    tk = q.pe(lambda e, b=b, j=j, ps=ps: e.matmul(
                        ps, mid[:, j, b * P:(b + 1) * P], w2[:, j, :], start=j == 0, stop=j == 1),
                        after=[mids[min(7, ((b + 1) * P - 1) // wide)], self.bank_free[i]])
                done = self.bank_free[i] = q.dve(lambda e, b=b, ps=ps: e.tensor_tensor(
                    x[:, b, :], x[:, b, :], ps, ALU.add), after=[tk, u])
            self.store_nodes(x, done)

    def store_nodes(self, x, after):
        s, q = self.s, self.q
        lane = q.lane("output")
        full = (s.nb - 1) * P
        q.dma("sync", lane, lambda e: e.dma_start(
            self.out[0:full, :].rearrange("(b l) f -> l b f", l=P), x[:, 0:s.nb - 1, :]), after=[after])
        end = q.dma("sync", lane, lambda e: e.dma_start(self.out[full:s.n, :], x[0:s.last, s.nb - 1, :]))
        q.wait("sync", [end])

    def build(self):
        s, q, ctx, io = self.s, self.q, self.ctx, self.io
        self.constants()
        self.tables()
        x = self.sb(ctx, "x", [P, s.nb, D])
        with ExitStack() as scope:
            counts = self.sb(scope, "counts", [P, s.nb, s.nc], F16)
            self.count_matrix(counts)
            self.layer0(x)
            rdeg = self.sb(scope, "rdeg", [P, s.nb])
            self.layer1(x, rdeg)
            self.layer2(x, rdeg)
            q.barrier()
        self.layer3(x)
        q.barrier()
        q.emit()


def gnn_program(nc, n_nodes, n_edges, io, out):
    with ExitStack() as ctx:
        Kernel(nc, ctx, Shapes(n_nodes, n_edges), io, out).build()




def layouts(inputs):
    import numpy as np

    s = Shapes(inputs["x"].shape[0], inputs["dst"].shape[0])
    a = {k: np.ascontiguousarray(v) for k, v in inputs.items()}
    src, dst, edge = a.pop("src"), a.pop("dst"), a.pop("edge_attr_32")
    total = (s.quads + 1) * 4 * P
    room = total - dst.shape[0]
    dst = np.concatenate([dst, np.full(room, s.pad_dst, dst.dtype)])
    src = np.concatenate([src, np.zeros(room, src.dtype)])
    a["dst_rows"], a["src_rows"] = dst.reshape(-1, P), src.reshape(-1, P)
    a["dst_quads"], a["src_quads"] = dst.reshape(-1, 4 * P), src.reshape(-1, 4 * P)
    a["dst_last"] = np.ascontiguousarray(a["dst_rows"][:s.tiles, -1])
    a["dst_quad_last"] = np.ascontiguousarray(a["dst_quads"][:s.quads, -1])
    edge = np.concatenate([edge, np.zeros((room, DE), edge.dtype)]).reshape(s.quads + 1, 4, P, DE)
    a["edge_t"] = np.ascontiguousarray(edge.transpose(0, 1, 3, 2)).reshape(s.quads + 1, 4 * DE, P)
    for name in ("L0_gnn_W_ih", "L0_gnn_W_hh", "L2_gnn_W1", "L2_gnn_W2", "L2_gnn_W_self"):
        a[name + "_t"] = np.ascontiguousarray(a.pop(name).T)
    for name in ("L0_gnn_b_ih", "L0_gnn_b_hh"):
        a[name + "_t"] = np.ascontiguousarray(a.pop(name).reshape(3, D).T)
    a["L3_gnn_b1_t"] = np.ascontiguousarray(a.pop("L3_gnn_b1").reshape(2, D).T)
    a["att_row"] = a.pop("L3_gnn_att").reshape(D)
    far = np.arange(s.nb)[:, None] * 2.0 * s.w + np.arange(s.w)
    a["c_ident"] = np.eye(P, dtype=np.float32)
    a["c_iota"] = np.arange(P, dtype=np.float32)
    a["c_far"] = far.reshape(-1).astype(np.float32)
    a["c_tile_no"] = np.arange(s.tiles, dtype=np.float32)
    a["c_step"] = np.ascontiguousarray(np.arange(16 * P, dtype=np.float32).reshape(16, P).T)
    return a


def kernel(**inputs):
    import concourse.bacc as bacc
    from concourse.bass_utils import run_bass_kernel_spmd

    arrays = layouts(inputs)
    n_nodes, n_edges = inputs["x"].shape[0], inputs["dst"].shape[0]
    nc = bacc.Bacc("TRN2", target_bir_lowering=False, num_devices=1)
    io = {name: nc.dram_tensor(name, a.shape, mybir.dt.from_np(a.dtype), kind="ExternalInput").ap()
          for name, a in arrays.items()}
    out = nc.dram_tensor("out", (n_nodes, D), F32, kind="ExternalOutput").ap()
    gnn_program(nc, n_nodes, n_edges, io, out)
    r = run_bass_kernel_spmd(nc, [arrays], core_ids=[0])
    return r.results[0]["out"]
```
